# Optimizing a Trainium2 kernel written in Bass

```python
import numpy as np
import jax
import jax.numpy as jnp

def _softmax(x, axis=-1):
    return jax.nn.softmax(x, axis=axis)

def _gelu(x):
    return jax.nn.gelu(x, approximate=True)

def _silu(x):
    return jax.nn.silu(x)

def _sigmoid(x):
    return jax.nn.sigmoid(x)

def _layernorm(x, axis=-1, eps=1e-05):
    m = jnp.mean(x, axis=axis, keepdims=True)
    v = jnp.var(x, axis=axis, keepdims=True)
    return (x - m) / jnp.sqrt(v + eps)

def _scatter_add(tgt, idx, src, axis=0):
    return tgt.at[idx].add(src)

def _segment_sum(src, seg, n):
    return jax.ops.segment_sum(src, seg, n)
kernel_name = 'mk_seq_postln_d2_jaxref_r8_ca3793'

def setup_inputs(seed: int=0):
    np.random.seed(seed)
    _w = jnp.asarray

    def _L0_attn_setup():
        import jax, jax.numpy as jnp
        import numpy as np
        B, N, DIM = (4, 512, 128)
        HEADS, DH = (16, 64)
        W, S, R = (128, 16, 1)
        SCALE = DH ** (-0.5)
        EPS = 1e-05

        def _layernorm(x, g, b):
            m = jnp.mean(x, axis=-1, keepdims=True)
            v = jnp.var(x, axis=-1, keepdims=True)
            return (x - m) * jax.lax.rsqrt(v + EPS) * g + b

        def _rotate_half(x):
            x1, x2 = jnp.split(x, 2, axis=-1)
            return jnp.concatenate([-x2, x1], axis=-1)

        def _apply_rotary(t, emb):
            return t * jnp.cos(emb) + _rotate_half(t) * jnp.sin(emb)

        def _look_around(x, pad_value):
            pad = [(0, 0)] * x.ndim
            pad[1] = (1, 0)
            p = jnp.pad(x, pad, constant_values=pad_value)
            return jnp.concatenate([p[:, :-1], p[:, 1:]], axis=2)
        key = jax.random.key(seed)
        ks = jax.random.split(key, 6)
        std = 0.02
        return {'x': jax.random.normal(ks[0], (B, N, DIM), jnp.float32), 'Wq': jax.random.normal(ks[1], (DIM, HEADS * DH), jnp.float32) * std, 'Wkv': jax.random.normal(ks[2], (DIM, HEADS * DH), jnp.float32) * std, 'Wproj': jax.random.normal(ks[3], (DH, R), jnp.float32) * std, 'Wout': jax.random.normal(ks[4], (HEADS * DH, DIM), jnp.float32) * std, 'bout': jnp.zeros((DIM,), jnp.float32), 'ln_local_g': jnp.ones((DH,), jnp.float32), 'ln_local_b': jnp.zeros((DH,), jnp.float32), 'ln_global_g': jnp.ones((DH,), jnp.float32), 'ln_global_b': jnp.zeros((DH,), jnp.float32)}
    _L0_attn_in = _L0_attn_setup()

    def _L0_ffn_setup():
        import jax, jax.numpy as jnp
        import numpy as np
        EPS = 1e-05

        @jax.custom_vjp
        def ste_quantize(w):
            scale = jnp.maximum(jnp.mean(jnp.abs(w)), EPS)
            return jnp.clip(jnp.round(w / scale), -1.0, 1.0)

        def _ste_fwd(w):
            return (ste_quantize(w), None)

        def _ste_bwd(_, g):
            return (g,)
        ste_quantize.defvjp(_ste_fwd, _ste_bwd)
        key = jax.random.key(seed)
        k1, k2 = jax.random.split(key)
        x = jax.random.normal(k1, (8, 1024, 128), dtype=jnp.float32)
        weight = jax.random.normal(k2, (128, 128), dtype=jnp.float32) * 0.02
        return {'x': x, 'weight': weight}
    _L0_ffn_in = _L0_ffn_setup()

    def _L1_attn_setup():
        import jax, jax.numpy as jnp
        import numpy as np
        B, N, D, H = (4, 256, 128, 16)
        Dh = D // H
        ROPE_THETA = 10000.0

        def _rope(x):
            n, d = (x.shape[-2], x.shape[-1])
            inv_freq = 1.0 / ROPE_THETA ** (jnp.arange(0, d, 2, dtype=jnp.float32) / d)
            freqs = jnp.arange(n, dtype=jnp.float32)[:, None] * inv_freq[None, :]
            freqs = jnp.repeat(freqs, 2, axis=-1)
            cos, sin = (jnp.cos(freqs), jnp.sin(freqs))
            x1 = x[..., ::2]
            x2 = x[..., 1::2]
            rot = jnp.stack([-x2, x1], axis=-1).reshape(x.shape)
            return x * cos + rot * sin
        key = jax.random.key(seed)
        ks = jax.random.split(key, 9)
        s = 0.02
        return {'x': jax.random.normal(ks[0], (B, N, D), dtype=jnp.float32), 'Wq': jax.random.normal(ks[1], (D, D), dtype=jnp.float32) * s, 'bq': jax.random.normal(ks[2], (D,), dtype=jnp.float32) * s, 'Wk': jax.random.normal(ks[3], (D, D), dtype=jnp.float32) * s, 'bk': jax.random.normal(ks[4], (D,), dtype=jnp.float32) * s, 'Wv': jax.random.normal(ks[5], (D, D), dtype=jnp.float32) * s, 'bv': jax.random.normal(ks[6], (D,), dtype=jnp.float32) * s, 'Wo': jax.random.normal(ks[7], (D, D), dtype=jnp.float32) * s, 'bo': jax.random.normal(ks[8], (D,), dtype=jnp.float32) * s}
    _L1_attn_in = _L1_attn_setup()

    def _L1_ffn_setup():
        import jax, jax.numpy as jnp
        import numpy as np
        B, T, D, F, E = (2, 128, 128, 512, 8)
        EPS = 1e-06
        key = jax.random.key(seed)
        k = jax.random.split(key, 5)
        scale = 0.02
        return {'x': jax.random.normal(k[0], (B, T, D), dtype=jnp.float32), 'rms_w': jnp.ones((D,), dtype=jnp.float32), 'gate_w': jax.random.normal(k[1], (E, D), dtype=jnp.float32) * scale, 'W1': jax.random.normal(k[2], (E, D, F), dtype=jnp.float32) * scale, 'b1': jnp.zeros((E, F), dtype=jnp.float32), 'W2': jax.random.normal(k[3], (E, F, D), dtype=jnp.float32) * scale, 'b2': jnp.zeros((E, D), dtype=jnp.float32)}
    _L1_ffn_in = _L1_ffn_setup()
    _d = {'L0_attn_x': _L0_attn_in['x'], 'L0_attn_Wq': _L0_attn_in['Wq'], 'L0_attn_Wkv': _L0_attn_in['Wkv'], 'L0_attn_Wproj': _L0_attn_in['Wproj'], 'L0_attn_Wout': _L0_attn_in['Wout'], 'L0_attn_bout': _L0_attn_in['bout'], 'L0_attn_ln_local_g': _L0_attn_in['ln_local_g'], 'L0_attn_ln_local_b': _L0_attn_in['ln_local_b'], 'L0_attn_ln_global_g': _L0_attn_in['ln_global_g'], 'L0_attn_ln_global_b': _L0_attn_in['ln_global_b'], 'L0_ffn_weight': _L0_ffn_in['weight'], 'L1_attn_Wq': _L1_attn_in['Wq'], 'L1_attn_bq': _L1_attn_in['bq'], 'L1_attn_Wk': _L1_attn_in['Wk'], 'L1_attn_bk': _L1_attn_in['bk'], 'L1_attn_Wv': _L1_attn_in['Wv'], 'L1_attn_bv': _L1_attn_in['bv'], 'L1_attn_Wo': _L1_attn_in['Wo'], 'L1_attn_bo': _L1_attn_in['bo'], 'L1_ffn_rms_w': _L1_ffn_in['rms_w'], 'L1_ffn_gate_w': _L1_ffn_in['gate_w'], 'L1_ffn_W1': _L1_ffn_in['W1'], 'L1_ffn_b1': _L1_ffn_in['b1'], 'L1_ffn_W2': _L1_ffn_in['W2'], 'L1_ffn_b2': _L1_ffn_in['b2']}
    _x0 = _d['L0_attn_x']
    _d['L0_attn_x'] = jax.random.normal(jax.random.fold_in(jax.random.key(seed), 1), (4, 1024, 128), dtype=_x0.dtype)
    del _x0
    return _d

def reference(L0_attn_x, L0_attn_Wq, L0_attn_Wkv, L0_attn_Wproj, L0_attn_Wout, L0_attn_bout, L0_attn_ln_local_g, L0_attn_ln_local_b, L0_attn_ln_global_g, L0_attn_ln_global_b, L0_ffn_weight, L1_attn_Wq, L1_attn_bq, L1_attn_Wk, L1_attn_bk, L1_attn_Wv, L1_attn_bv, L1_attn_Wo, L1_attn_bo, L1_ffn_rms_w, L1_ffn_gate_w, L1_ffn_W1, L1_ffn_b1, L1_ffn_W2, L1_ffn_b2):

    def _L0_attn_ref(x, Wq, Wkv, Wproj, Wout, bout, ln_local_g, ln_local_b, ln_global_g, ln_global_b):
        import jax, jax.numpy as jnp
        import numpy as np
        B, N, DIM = (4, 512, 128)
        HEADS, DH = (16, 64)
        W, S, R = (128, 16, 1)
        SCALE = DH ** (-0.5)
        EPS = 1e-05

        def _layernorm(x, g, b):
            m = jnp.mean(x, axis=-1, keepdims=True)
            v = jnp.var(x, axis=-1, keepdims=True)
            return (x - m) * jax.lax.rsqrt(v + EPS) * g + b

        def _rotate_half(x):
            x1, x2 = jnp.split(x, 2, axis=-1)
            return jnp.concatenate([-x2, x1], axis=-1)

        def _apply_rotary(t, emb):
            return t * jnp.cos(emb) + _rotate_half(t) * jnp.sin(emb)

        def _look_around(x, pad_value):
            pad = [(0, 0)] * x.ndim
            pad[1] = (1, 0)
            p = jnp.pad(x, pad, constant_values=pad_value)
            return jnp.concatenate([p[:, :-1], p[:, 1:]], axis=2)
        b, n, _ = x.shape
        bh = b * HEADS
        neg = -jnp.finfo(x.dtype).max
        q = (x @ Wq).reshape(b, n, HEADS, DH).transpose(0, 2, 1, 3).reshape(bh, n, DH)
        kv = (x @ Wkv).reshape(b, n, HEADS, DH).transpose(0, 2, 1, 3).reshape(bh, n, DH)
        seq = jnp.arange(n)
        inv_freq = 1.0 / 10000.0 ** (jnp.arange(0, DH, 2, dtype=jnp.float32) / DH)
        freqs = seq[:, None].astype(jnp.float32) * inv_freq[None, :]
        emb = jnp.concatenate([freqs, freqs], axis=-1)[None]
        q = _apply_rotary(q, emb) * SCALE
        kv = _apply_rotary(kv, emb)
        windows = n // W
        lq = q.reshape(bh, windows, W, DH)
        lkv = kv.reshape(bh, windows, W, DH)
        lkv = _look_around(lkv, -1.0)
        lkv = _layernorm(lkv, ln_local_g, ln_local_b)
        lsim = jnp.einsum('bwid,bwjd->bwij', lq, lkv)
        nseg = n // S
        gkv = kv.reshape(bh, nseg, S, DH)
        pkv = jax.nn.softmax(gkv @ Wproj, axis=-2)
        gkv = jnp.einsum('bnsd,bnsr->bnrd', gkv, pkv).reshape(bh, nseg * R, DH)
        gkv = _layernorm(gkv, ln_global_g, ln_global_b)
        gsim = jnp.einsum('bnd,brd->bnr', q, gkv)
        seq_w = seq.reshape(1, windows, W)
        pad_mask = _look_around(seq_w, -1) == -1
        lsim = jnp.where(pad_mask[:, :, None, :], neg, lsim)
        causal_mask = jnp.triu(jnp.ones((W, 2 * W), bool), k=W + 1)
        lsim = jnp.where(causal_mask[None, None], neg, lsim)
        g_range_max = (jnp.arange(nseg) + 1) * S - 1
        g_mask = jnp.repeat(seq[:, None] > g_range_max[None, :], R, axis=1)
        gsim = jnp.where(~g_mask[None], neg, gsim)
        v = jnp.concatenate([jnp.broadcast_to(gkv[:, None], (bh, windows, nseg * R, DH)), lkv], axis=2)
        sim = jnp.concatenate([gsim.reshape(bh, windows, W, nseg * R), lsim], axis=-1)
        attn = jax.nn.softmax(sim, axis=-1)
        out = jnp.einsum('bwij,bwjd->bwid', attn, v)
        out = out.reshape(b, HEADS, n, DH).transpose(0, 2, 1, 3).reshape(b, n, HEADS * DH)
        return out @ Wout + bout

    def _L0_ffn_ref(x, weight):
        import jax, jax.numpy as jnp
        import numpy as np
        EPS = 1e-05

        @jax.custom_vjp
        def ste_quantize(w):
            scale = jnp.maximum(jnp.mean(jnp.abs(w)), EPS)
            return jnp.clip(jnp.round(w / scale), -1.0, 1.0)

        def _ste_fwd(w):
            return (ste_quantize(w), None)

        def _ste_bwd(_, g):
            return (g,)
        ste_quantize.defvjp(_ste_fwd, _ste_bwd)
        w_ternary = ste_quantize(weight)
        scale = jnp.maximum(jnp.mean(jnp.abs(weight)), EPS)
        return jnp.einsum('bsi,oi->bso', x, w_ternary * scale)

    def _L1_attn_ref(x, Wq, bq, Wk, bk, Wv, bv, Wo, bo):
        import jax, jax.numpy as jnp
        import numpy as np
        B, N, D, H = (4, 256, 128, 16)
        Dh = D // H
        ROPE_THETA = 10000.0

        def _rope(x):
            n, d = (x.shape[-2], x.shape[-1])
            inv_freq = 1.0 / ROPE_THETA ** (jnp.arange(0, d, 2, dtype=jnp.float32) / d)
            freqs = jnp.arange(n, dtype=jnp.float32)[:, None] * inv_freq[None, :]
            freqs = jnp.repeat(freqs, 2, axis=-1)
            cos, sin = (jnp.cos(freqs), jnp.sin(freqs))
            x1 = x[..., ::2]
            x2 = x[..., 1::2]
            rot = jnp.stack([-x2, x1], axis=-1).reshape(x.shape)
            return x * cos + rot * sin
        b, n, d = x.shape
        split = lambda t: t.reshape(b, n, H, Dh).transpose(0, 2, 1, 3)
        q = split(x @ Wq + bq)
        k = split(x @ Wk + bk)
        v = split(x @ Wv + bv)
        q = _rope(q)
        k = _rope(k)
        scores = jnp.einsum('bhnd,bhmd->bhnm', q, k) / jnp.sqrt(jnp.float32(d))
        weights = jax.nn.softmax(scores, axis=-1)
        inter = jnp.einsum('bhnm,bhmd->bhnd', weights, v)
        inter = inter.transpose(0, 2, 1, 3).reshape(b, n, d)
        return inter @ Wo + bo

    def _L1_ffn_ref(x, rms_w, gate_w, W1, b1, W2, b2):
        import jax, jax.numpy as jnp
        import numpy as np
        B, T, D, F, E = (2, 128, 128, 512, 8)
        EPS = 1e-06
        ms = jnp.mean(x * x, axis=-1, keepdims=True)
        xn = x * jax.lax.rsqrt(ms + EPS) * rms_w
        logits = jnp.einsum('btd,ed->bte', xn, gate_w)
        scores = jax.nn.softmax(logits, axis=-1)
        top1_idx = jnp.argmax(scores, axis=-1)
        top1_score = jnp.max(scores, axis=-1)
        out = jnp.zeros_like(xn)
        for e in range(E):
            h = jax.nn.silu(jnp.einsum('btd,df->btf', xn, W1[e]) + b1[e])
            ye = jnp.einsum('btf,fd->btd', h, W2[e]) + b2[e]
            out = jnp.where((top1_idx == e)[..., None], ye, out)
        return out * top1_score[..., None]
    x = L0_attn_x
    x = _layernorm(x + _L0_attn_ref(x, L0_attn_Wq, L0_attn_Wkv, L0_attn_Wproj, L0_attn_Wout, L0_attn_bout, L0_attn_ln_local_g, L0_attn_ln_local_b, L0_attn_ln_global_g, L0_attn_ln_global_b), axis=-1)
    x = _layernorm(x + _L0_ffn_ref(x, L0_ffn_weight), axis=-1)
    x = _layernorm(x + _L1_attn_ref(x, L1_attn_Wq, L1_attn_bq, L1_attn_Wk, L1_attn_bk, L1_attn_Wv, L1_attn_bv, L1_attn_Wo, L1_attn_bo), axis=-1)
    x = _layernorm(x + _L1_ffn_ref(x, L1_ffn_rms_w, L1_ffn_gate_w, L1_ffn_W1, L1_ffn_b1, L1_ffn_W2, L1_ffn_b2), axis=-1)
    return x

_drawn_inputs = setup_inputs


def setup_inputs(seed=0):
    import zlib

    import numpy as np

    out = dict(_drawn_inputs(seed))
    spreads = {'L0_attn_bout': (0.0, 0.1),
     'L0_attn_ln_local_g': (1.0, 0.6),
     'L0_attn_ln_local_b': (0.0, 0.1),
     'L0_attn_ln_global_g': (1.0, 0.6),
     'L0_attn_ln_global_b': (0.0, 0.795),
     'L1_ffn_rms_w': (1.0, 0.6),
     'L1_ffn_b1': (0.0, 0.8),
     'L1_ffn_b2': (0.0, 0.445)}
    factors = {'L0_attn_Wproj': 8.0,
     'L1_attn_Wq': 8.0,
     'L1_attn_bq': 8.0,
     'L1_attn_Wk': 8.0,
     'L1_attn_bk': 8.0,
     'L1_attn_Wv': 8.0,
     'L1_attn_bv': 8.0,
     'L1_attn_Wo': 6.889,
     'L1_attn_bo': 2.69,
     'L1_ffn_gate_w': 2.919,
     'L1_ffn_W1': 6.015,
     'L1_ffn_W2': 5.528}
    for name, (base, spread) in spreads.items():
        noise = np.random.default_rng([zlib.crc32(name.encode()), seed]).standard_normal(out[name].shape)
        drawn = base * np.exp(spread * noise) if base else spread * noise
        out[name] = jnp.asarray(drawn.astype(out[name].dtype))
    for name, factor in factors.items():
        out[name] = (out[name] * factor).astype(out[name].dtype)
    return out
```

```python
from contextlib import ExitStack

import numpy as np

import concourse.bass as bass
from concourse import mybir

F32 = mybir.dt.float32
BF16 = mybir.dt.bfloat16
ALU = mybir.AluOpType
ACT = mybir.ActivationFunctionType
AX = mybir.AxisListType

P = 128
B, N, D = 4, 1024, 128
TILES = B * N // P
WIN = N // P
EPS = 1e-5

H0, DH = 16, 64
PAIRS = H0 // 2
SEG = 16
SPW = P // SEG
NSEG = N // SEG
KEYS = 2 * P + NSEG
GLOB = (2 * P, 0)
LOCAL = (0, NSEG)


class Tally:

    def __init__(self, eng, sem, start=0):
        self.eng, self.sem, self.start, self.n = eng, sem, start, 0

    def done(self, ins):
        ins.then_inc(self.sem, 1)
        self.n += 1
        return self.n

    def wait(self, n=None):
        self.eng.wait_ge(self.sem, self.start + (self.n if n is None else n))


def layer0_attention(nc, ctx, io, res):

    def sb(name, shape, dt=F32):
        return ctx.enter_context(nc.sbuf_tensor(name, shape, dt))

    def sem(name):
        return ctx.enter_context(nc.semaphore(name))

    x_sb = sb("x_sb", [P, TILES, D])
    xT = sb("xT", [P, 2, P])
    wqs = sb("wqs", [P, H0, P])
    wkv = sb("wkv", [P, H0 * DH])
    wout = sb("wout", [P, PAIRS, D])
    wproj = sb("wproj", [P, DH])
    lg, lb = sb("lg", [P, DH]), sb("lb", [P, DH])
    gg, gb = sb("gg", [P, DH]), sb("gb", [P, DH])
    csT = sb("csT", [P, N])
    cosn = sb("cosn", [P, WIN, DH])
    sinn = sb("sinn", [P, WIN, DH])
    masks = sb("masks", [P, WIN, 2, KEYS], BF16)
    identb = sb("identb", [P, P], BF16)
    ident = sb("ident", [P, P])
    segsel = sb("segsel", [P, SPW])
    headsel = sb("headsel", [P, 4])
    qT = sb("qT", [P, 2, H0, P])
    KT = sb("KT", [P, H0, KEYS])
    V = sb("V", [P, 2, H0 * DH])
    gV = sb("gV", [P, PAIRS, P])
    rc, rs = sb("rc", [P, H0, DH]), sb("rs_", [P, H0, DH])
    kvr = sb("kvr", [P, H0, DH])
    wl = sb("wl", [P, H0, DH])
    cen = sb("cen", [P, H0, DH])
    vn = sb("vn", [P, H0, DH])
    vst = sb("vst", [P, H0, DH])
    st = sb("st", [P, H0, 6])
    sm = sb("sm", [P, 16, H0])
    logit = sb("logit", [P, H0])
    e0, e1, pk = (sb(n, [H0, P]) for n in ("e0", "e1", "pk"))
    smax, ssum, srec = (sb(n, [H0, SPW]) for n in ("smax", "ssum", "srec"))
    wg = sb("wg", [P, H0, SPW])
    gm = sb("gm", [P, 4, DH])
    g0, g1, g2 = sb("g0", [P, DH]), sb("g1", [P, DH]), sb("g2", [P, DH])
    gk = sb("gk", [P, 2, DH])
    gst, gmv, gsm = sb("gst", [P, 6]), sb("gmv", [P, 2]), sb("gsm", [P, 8])
    spare = sb("spare", [P, 9])
    pr = sb("pr", [P, 2, 2 * KEYS])
    nmax = sb("nmax", [P, 2, 2])
    psums = sb("psums", [P, 2, 2])
    prec = sb("prec", [P, 2, 2])
    prT = sb("prT", [P, 2, 5 * P])
    oT = sb("oT", [P, PAIRS, P])

    ps_s = [ctx.enter_context(nc.psum_tensor(f"ps_s{k}", [P, 2, 512], F32)) for k in range(2)]
    ps_x = ctx.enter_context(nc.psum_tensor("ps_x", [P, 512], F32))
    ps_g = ctx.enter_context(nc.psum_tensor("ps_g", [P, 512], F32))
    ps_o = ctx.enter_context(nc.psum_tensor("ps_o", [P, 512], F32))
    ps_r = ctx.enter_context(nc.psum_tensor("ps_r", [P, 512], F32))
    gk_dram = nc.dram_tensor("gk_dram", [H0, NSEG, DH], F32, kind="Internal").ap()

    consts = sem("consts")
    zeroed = sem("zeroed")
    x_landed = [sem(f"x_landed{k}") for k in range(2)]
    scores_ready = sem("scores_ready")
    max_done = sem("max_done")
    exp_done = sem("exp_done")
    recip_done = sem("recip_done")
    norm_done = sem("norm_done")
    turned = sem("turned")
    x_copied = sem("x_copied")
    g_copied = sem("g_copied")
    pv_done = sem("pv_done")
    o_copied = sem("o_copied")
    work_ready = sem("work_ready")
    work_free = sem("work_free")
    rot_products = sem("rot_products")
    kvr_done = sem("kvr_done")
    wl_done = sem("wl_done")
    cen_done = sem("cen_done")
    vn_done = sem("vn_done")
    vst_done = sem("vst_done")
    v_copied = sem("v_copied")
    var_done = sem("var_done")
    ln_done = sem("ln_done")
    y0_done = sem("y0_done")
    stats_done = sem("stats_done")
    logit_done = sem("logit_done")
    e0_done = sem("e0_done")
    e1_done = sem("e1_done")
    pk_done = sem("pk_done")
    wg_done = sem("wg_done")
    gm_done = sem("gm_done")
    gvar_done = sem("gvar_done")
    gy0_done = sem("gy0_done")
    gk_done = sem("gk_done")
    gk_zeroed = sem("gk_zeroed")
    gk_stored = sem("gk_stored")
    gv_landed = sem("gv_landed")
    q_done = sem("q_done")
    kt_copied = sem("kt_copied")
    res_done = sem("res_done")
    dve_step = sem("dve_step")
    DVE_STEPS = 19

    loads = [(x_sb[:, :, :], io["x"].rearrange("(t p) d -> p t d", p=P)),
             (wqs[:, :, :], io["wqs"]), (wkv[:, :], io["wkv"]),
             (wout[:, :, :], io["wout"].rearrange("(k p) d -> p k d", p=P)),
             (wproj[:, :], io["wproj"].rearrange("d a -> a d").to_broadcast([P, DH])),
             (lg[:, :], io["lg"].to_broadcast([P, DH])), (lb[:, :], io["lb"].to_broadcast([P, DH])),
             (gg[:, :], io["gg"].to_broadcast([P, DH])), (gb[:, :], io["gb"].to_broadcast([P, DH])),
             (csT[:, :], io["csT"]), (cosn[:, :, :], io["cosn"]), (sinn[:, :, :], io["sinn"]),
             (masks[:, :, :, :], io["masks"]), (identb[:, :], io["identb"]), (ident[:, :], io["ident"]),
             (segsel[:, :], io["segsel"]), (headsel[:, :], io["headsel"])]
    ALL_CONSTS = 16 * len(loads)

    def is_first(n):
        return isinstance(n, int) and n == 0

    def row(small, k):
        return small[:, k, :]

    block = ctx.enter_context(nc.Block())

    @block.sync
    def _(sp):
        def load_x(n, par):
            sp.dma_start(xT[:, par, :], io["xT"][bass.ds(n, 1), :, :].rearrange("a p t -> (a p) t")
                         ).then_inc(x_landed[par], 16)

        def store_segments(n, w):
            sp.wait_ge(gk_done, n + 1)
            sp.dma_start(gk_dram[:, bass.ds(w * SPW, SPW), :].rearrange("h s d -> h s d"),
                         gk[:, 0, :]).then_inc(gk_stored, 16)

        def load_segments(n, pairs=None):
            sp.wait_ge(gk_stored, 16 * (n + 1))
            if pairs is not None:
                sp.wait_ge(pv_done, pairs)
            for par in range(2):
                sp.dma_start(gV[par * NSEG:(par + 1) * NSEG, :, par * DH:(par + 1) * DH],
                             gk_dram.rearrange("(k a) s d -> a s k d", a=2)[par]).then_inc(gv_landed, 16)

        load_x(0, 0)
        for dst, src in loads:
            sp.dma_start(dst, src).then_inc(consts, 16)
        load_x(1, 1)
        sp.wait_ge(zeroed, 4)
        sp.dma_start(gk_dram.rearrange("h s d -> (h s) d").rearrange("(a p) d -> p a d", p=P),
                     gV[:, :, 0:DH]).then_inc(gk_zeroed, 16)
        sp.wait_ge(gk_zeroed, 16)
        store_segments(0, 0)
        load_segments(0)
        def two_tiles(i):
            for par in range(2):
                t = i * 2 + par
                n = t + 1
                sp.wait_ge(q_done, 4 * (t + 1))
                sp.wait_ge(consts, ALL_CONSTS)
                load_x((t + 2) % TILES, par)
                store_segments(n, n % WIN)
                load_segments(n, t * PAIRS + PAIRS)

        two_tiles(0)
        with sp.Fori(1, TILES // 2) as i:
            two_tiles(i)
        for par in range(2):
            sp.wait_ge(x_landed[par], 16 * (TILES // 2 + 1))
        sp.wait_ge(gv_landed, 32 * (TILES + 1))

    @block.tensor
    def _(pe):
        def kv(n, np_, half, turns=0):
            if half == 0:
                pe.wait_ge(x_landed[np_], 16 * (turns + 1))
                if not is_first(n):
                    pe.wait_ge(res_done, n - 1)
            else:
                pe.wait_ge(rot_products, 2 * n + 1)
            pe.matmul(ps_r[:, :], xT[:, np_, :], wkv[:, half * 512:half * 512 + 512],
                      start=True, stop=True).then_inc(work_ready, 1)

        def q(n, np_, quad):
            if quad == 0:
                pe.wait_ge(rot_products, 2 * n + 2)
            else:
                pe.wait_ge(q_done, 4 * n + quad)
            for k in range(4):
                mm = pe.matmul(ps_r[:, k * P:(k + 1) * P], wqs[:, 4 * quad + k, :], xT[:, np_, :],
                               start=True, stop=True)
            mm.then_inc(work_ready, 1)

        def logit_turn(n):
            pe.wait_ge(q_done, 4 * n + 4)
            pe.wait_ge(logit_done, n + 1)
            pe.transpose(ps_r[0:H0, 0:P], logit[:, :], ident[:, :]).then_inc(work_ready, 1)

        def pk_turn(n):
            pe.wait_ge(pk_done, n + 1)
            pe.matmul(ps_r[:, 0:H0], pk[:, :], ident[0:H0, 0:H0], start=True, stop=True).then_inc(work_ready, 1)

        def seg_sums(n):
            pe.wait_ge(wg_done, n + 1)
            for j in range(4):
                mm = pe.matmul(ps_r[32 * j:32 * j + 32, 0:4 * DH],
                               wg[:, 4 * j:4 * j + 4, :].rearrange("p h s -> p (h s)"),
                               kvr[:, 4 * j:4 * j + 4, :].rearrange("p h d -> p (h d)"), start=True, stop=True)
            mm.then_inc(work_ready, 1)

        def keys_turn(n, half):
            if half == 0:
                pe.wait_ge(vst_done, n + 1)
                pe.wait_ge(gm_done, n + 1)
            else:
                pe.wait_ge(kt_copied, 8 * n + 4)
            for k in range(4):
                h = 8 * half + 2 * k
                mm = pe.transpose(ps_r[:, k * P:(k + 1) * P], vst[:, h:h + 2, :].rearrange("p h d -> p (h d)"),
                                  ident[:, :])
            mm.then_inc(work_ready, 1)

        def seg_turn(n):
            pe.wait_ge(kt_copied, 8 * n + 8)
            pe.wait_ge(gk_done, n + 1)
            pe.transpose(ps_r[:, 0:P], gk[:, :, :].rearrange("p a d -> p (a d)"), ident[:, :]).then_inc(work_ready, 1)

        def out_proj(t):
            pe.wait_ge(g_copied, (PAIRS + 1) * (t + 1) + 1)
            pe.wait_ge(o_copied, 2 * (t + 1))
            for k in range(PAIRS):
                mm = pe.matmul(ps_r[:, 0:D], oT[:, k, :], wout[:, k, :], start=(k == 0), stop=(k == PAIRS - 1))
            mm.then_inc(work_ready, 1)

        def scores(t, par, w, p):
            if p == 0:
                pe.wait_ge(kt_copied, 8 * (t + 1))
                pe.wait_ge(q_done, 4 * (t + 1))
                pe.wait_ge(g_copied, (PAIRS + 1) * t + 1)
            if p >= 2:
                pe.wait_ge(exp_done, PAIRS * t + p - 1)
            else:
                pe.wait_ge(exp_done, PAIRS * t)
            bank = ps_s[p % 2]
            for a in range(2):
                h = 2 * p + a
                pe.matmul(bank[:, a, 0:KEYS], qT[:, par, h, :], KT[:, h, :], start=True, stop=False)
                mm = pe.matmul(bank[:, a, 0:KEYS], identb[:, :], masks[:, bass.ds(w, 1), a, :].rearrange("p a k -> p (a k)"),
                               start=False, stop=True)
            mm.then_inc(scores_ready, 1)

        def turn(t, p):
            pe.wait_ge(norm_done, PAIRS * t + p + 1)
            if p > 0:
                pe.wait_ge(x_copied, PAIRS * t + p)
                pe.wait_ge(g_copied, (PAIRS + 1) * t + p + 1)
            else:
                pe.wait_ge(x_copied, PAIRS * t)
            r = pr[:, p % 2, :]
            for k, at in enumerate((0, P, 3 * P, 4 * P)):
                pe.transpose(ps_x[:, k * P:(k + 1) * P], r[:, at:at + P], ident[:, :])
            pe.transpose(ps_g[:, 0:P], r[:, 2 * P:3 * P], ident[:, :]).then_inc(turned, 1)

        def values(t, par, p):
            pe.wait_ge(x_copied, PAIRS * t + p + 1)
            pe.wait_ge(g_copied, (PAIRS + 1) * t + p + 2)
            if p == 0:
                pe.wait_ge(gv_landed, 32 * (t + 1))
                pe.wait_ge(v_copied, t + 1)
                pe.wait_ge(o_copied, 2 * t)
            if p == 4:
                pe.wait_ge(o_copied, 2 * t + 1)
            at = (p % 4) * P
            pT = prT[:, p % 2, :]
            pe.matmul(ps_o[:, at:at + P], gV[:, p, :], pT[:, 4 * P:5 * P], start=True, stop=False,
                      skip_group_check=True)
            for s in range(2):
                for a in range(2):
                    h = 2 * p + a
                    mm = pe.matmul(ps_o[DH * a:DH * a + DH, at:at + P], V[:, s, h * DH:(h + 1) * DH],
                                   pT[:, (2 * a + s) * P:(2 * a + s + 1) * P], start=False, stop=(s == 1),
                                   skip_group_check=True)
            mm.then_inc(pv_done, 1)

        pe.wait_ge(consts, ALL_CONSTS)
        kv(0, 0, 0)
        kv(0, 0, 1)
        for quad in range(4):
            q(0, 0, quad)
        logit_turn(0)
        pk_turn(0)
        seg_sums(0)
        keys_turn(0, 0)
        keys_turn(0, 1)
        seg_turn(0)
        pe.wait_ge(zeroed, 4)
        def two_tiles(i):
            for par in range(2):
                t = i * 2 + par
                n, np_ = t + 1, 1 - par
                w = t % WIN
                first = {0: lambda: kv(n, np_, 0, i + par), 1: lambda: q(n, np_, 0), 2: lambda: q(n, np_, 2),
                         4: lambda: logit_turn(n)}
                second = {0: lambda: kv(n, np_, 1), 1: lambda: q(n, np_, 1), 2: lambda: q(n, np_, 3),
                          5: lambda: pk_turn(n), 6: lambda: seg_sums(n)}
                for p in range(PAIRS + 2):
                    if p < PAIRS:
                        scores(t, par, w, p)
                    if p in first:
                        first[p]()
                    if p >= 2:
                        values(t, par, p - 2)
                    if p in second:
                        second[p]()
                    if p == PAIRS:
                        keys_turn(n, 0)
                    if 1 <= p <= PAIRS:
                        turn(t, p - 1)
                keys_turn(n, 1)
                seg_turn(n)
                out_proj(t)

        two_tiles(0)
        with pe.Fori(1, TILES // 2) as i:
            two_tiles(i)

    @block.scalar
    def _(act):
        def exps(t, p):
            act.wait_ge(scores_ready, PAIRS * t + p + 1)
            act.wait_ge(max_done, PAIRS * t + p + 1)
            if p >= 2:
                act.wait_ge(turned, PAIRS * t + p - 1)
            else:
                act.wait_ge(turned, PAIRS * t)
            for a in range(2):
                e = act.activation(pr[:, p % 2, a * KEYS:(a + 1) * KEYS], ps_s[p % 2][:, a, 0:KEYS], ACT.Exp,
                                   bias=nmax[:, p % 2, a:a + 1], scale=1.0, accum_out=psums[:, p % 2, a:a + 1])
            e.then_inc(exp_done, 1)

        def copy_x(t, p):
            act.wait_ge(turned, PAIRS * t + p + 1)
            if p >= 2:
                act.wait_ge(pv_done, PAIRS * t + p - 1)
            else:
                act.wait_ge(pv_done, PAIRS * t)
            act.activation(prT[:, p % 2, 0:4 * P], ps_x[:, :], ACT.Copy).then_inc(x_copied, 1)

        def copy_o(t, half):
            act.wait_ge(pv_done, PAIRS * t + 4 * half + 4)
            if half == 0:
                act.wait_ge(res_done, t)
            act.activation(oT[:, 4 * half:4 * half + 4, :].rearrange("p k t -> p (k t)"), ps_o[:, :],
                           ACT.Copy).then_inc(o_copied, 1)

        def rstd(n):
            act.wait_ge(var_done, n + 1)
            act.activation(row(sm, 6), row(sm, 5), ACT.Ln).then_inc(ln_done, 1)
            act.wait_ge(ln_done, 2 * n + 1)
            act.activation(row(sm, 7), row(sm, 6), ACT.Exp, scale=-0.5).then_inc(y0_done, 1)

        def seg_exp(n):
            act.wait_ge(e0_done, n + 1)
            act.activation(e1[:, :], e0[:, :], ACT.Exp).then_inc(e1_done, 1)

        def grstd(n):
            act.wait_ge(gvar_done, n + 1)
            act.activation(gsm[:, 1:2], gsm[:, 0:1], ACT.Ln).then_inc(ln_done, 1)
            act.wait_ge(ln_done, 2 * n + 2)
            act.activation(gsm[:, 2:3], gsm[:, 1:2], ACT.Exp, scale=-0.5).then_inc(gy0_done, 1)

        def copy_keys(n, slot, half, at):
            act.wait_ge(work_ready, at)
            for a in range(2):
                for to in range(2):
                    c0 = LOCAL[a] + slot * P
                    c = act.activation(
                        KT[DH * to:DH * to + DH, 8 * half + a:8 * half + 8:2, c0:c0 + P],
                        ps_r[DH * a:DH * a + DH, :].rearrange("p (k t) -> p k t", k=4), ACT.Copy)
                    c.then_inc(kt_copied, 1)

        act.wait_ge(zeroed, 4)
        rstd(0)
        seg_exp(0)
        grstd(0)
        for half in range(2):
            copy_keys(0, 0, half, 10 + half)
        def two_tiles(i):
            for par in range(2):
                t = i * 2 + par
                n = t + 1
                for p in range(PAIRS + 1):
                    if p == 4:
                        rstd(n)
                    if p == 5:
                        seg_exp(n)
                    if p < PAIRS:
                        exps(t, p)
                    if p == 7:
                        grstd(n)
                    if p == 6:
                        copy_o(t, 0)
                    if 1 <= p <= PAIRS:
                        copy_x(t, p - 1)
                for half in range(2):
                    copy_keys(n, 1 - par, half, 13 * t + 12 + 10 + half)
                    if half == 0:
                        copy_o(t, 1)

        two_tiles(0)
        with act.Fori(1, TILES // 2) as i:
            two_tiles(i)

    @block.gpsimd
    def _(pool):
        pool.memset(KT[:, :, :], 0.0).then_inc(zeroed, 1)
        pool.memset(V[:, :, :], 0.0).then_inc(zeroed, 1)
        pool.memset(gV[:, :, :], 0.0).then_inc(zeroed, 1)
        pool.memset(st[:, :, :], 0.0).then_inc(zeroed, 1)
        pool.wait_ge(zeroed, 4)
        pool.memset(spare[:, :], 0.0).then_inc(zeroed, 1)

        def carry_wait(k):
            pool.tensor_tensor(spare[:, k:k + 1], spare[:, 8:9], spare[:, 8:9], ALU.mult)

        def add_halves(n, half):
            pool.wait_ge(rot_products, 2 * n + half + 1)
            hs = slice(8 * half, 8 * half + 8)
            if half == 0:
                pool.wait_ge(gm_done, n)
            pool.tensor_tensor(kvr[:, hs, :], rc[:, hs, :], rs[:, hs, :], ALU.add).then_inc(kvr_done, 1)

        def weigh(n):
            pool.wait_ge(kvr_done, 2 * n + 2)
            pool.wait_ge(logit_done, n)
            pool.tensor_tensor(wl[:, :, :], kvr[:, :, :], wproj[:, :].unsqueeze(1).to_broadcast([P, H0, DH]),
                               ALU.mult).then_inc(wl_done, 1)

        def centre(n):
            pool.wait_ge(stats_done, n + 1)
            pool.tensor_tensor(cen[:, :, :], kvr[:, :, :], row(sm, 2).unsqueeze(2).to_broadcast([P, H0, DH]),
                               ALU.subtract).then_inc(cen_done, 1)

        def normalise(n):
            pool.wait_ge(cen_done, n + 1)
            pool.tensor_tensor(vn[:, :, :], cen[:, :, :], row(sm, 11).unsqueeze(2).to_broadcast([P, H0, DH]),
                               ALU.mult).then_inc(vn_done, 1)

        def norm(t, p):
            pool.wait_ge(recip_done, PAIRS * t + p + 1)
            carry_wait(p % 2)
            for a in range(2):
                r = pr[:, p % 2, a * KEYS:(a + 1) * KEYS]
                s = pool.tensor_scalar(r, r, prec[:, p % 2, a:a + 1], 1.0, ALU.mult, ALU.mult)
            s.then_inc(norm_done, 1)

        def keep_values(n, slot):
            pool.wait_ge(vst_done, n + 1)
            carry_wait(2)
            pool.tensor_scalar(V[:, slot, :], vst[:, :, :].rearrange("p h d -> p (h d)"), 1.0, 1.0,
                               ALU.mult, ALU.mult).then_inc(v_copied, 1)

        pool.wait_ge(consts, ALL_CONSTS)
        add_halves(0, 0)
        add_halves(0, 1)
        weigh(0)
        centre(0)
        normalise(0)
        pool.wait_ge(zeroed, 5)
        keep_values(0, 0)
        def two_tiles(i):
            for par in range(2):
                t = i * 2 + par
                n = t + 1
                for p in range(PAIRS):
                    if p == 1:
                        add_halves(n, 0)
                        norm(t, 0)
                        add_halves(n, 1)
                    elif p == 2:
                        norm(t, 1)
                        weigh(n)
                    elif p == 4:
                        norm(t, 3)
                        centre(n)
                    elif p == 5:
                        norm(t, 4)
                        normalise(n)
                    elif p > 0:
                        norm(t, p - 1)
                norm(t, PAIRS - 1)
                pool.wait_ge(pv_done, PAIRS * (t + 1))
                keep_values(n, 1 - par)

        two_tiles(0)
        with pool.Fori(1, TILES // 2) as i:
            two_tiles(i)

    @block.vector
    def _(dve):
        def rotate(n, w, half, at):
            dve.wait_ge(work_ready, at)
            dve.wait_ge(kvr_done, 2 * n)
            hs = slice(8 * half, 8 * half + 8)
            r = ps_r[:, :].rearrange("p (h d) -> p h d", h=8)
            c = cosn[:, bass.ds(w, 1), :].to_broadcast([P, 8, DH])
            h = DH // 2
            s0 = sinn[:, bass.ds(w, 1), 0:h].to_broadcast([P, 8, h])
            s1 = sinn[:, bass.ds(w, 1), h:DH].to_broadcast([P, 8, h])
            dve.tensor_tensor(rc[:, hs, :], r, c, ALU.mult)
            dve.tensor_tensor(rs[:, hs, 0:h], r[:, :, h:DH], s0, ALU.mult)
            dve.tensor_tensor(rs[:, hs, h:DH], r[:, :, 0:h], s1, ALU.mult).then_inc(rot_products, 1)

        def q_mult(n, np_, w, quad, at):
            dve.wait_ge(work_ready, at)
            dve.tensor_tensor(qT[:, np_, 4 * quad:4 * quad + 4, :], ps_r[:, :].rearrange("p (h t) -> p h t", h=4),
                              csT[:, bass.ds(w * P, P)].unsqueeze(1).to_broadcast([P, 4, P]),
                              ALU.mult).then_inc(q_done, 1)

        def stats(n, half):
            dve.wait_ge(kvr_done, 2 * n + half + 1)
            for h in range(8 * half, 8 * half + 8):
                last = dve.bn_stats(st[:, h, :], kvr[:, h, :])
            return last

        def variance(n, own, mark):
            own.wait(mark)
            dve.tensor_tensor(row(sm, 0), st[:, :, 1], st[:, :, 4], ALU.add)
            dve.tensor_tensor(row(sm, 1), st[:, :, 1], st[:, :, 4], ALU.subtract)
            m = own.done(dve.tensor_tensor(row(sm, 3), st[:, :, 2], st[:, :, 5], ALU.add))
            own.wait(m)
            dve.tensor_scalar(row(sm, 2), row(sm, 0), 0.5, None, ALU.mult)
            dve.tensor_scalar(row(sm, 8), row(sm, 3), 1.0 / DH, EPS, ALU.mult, ALU.add)
            m = own.done(dve.scalar_tensor_tensor(row(sm, 4), row(sm, 1), 0.25, row(sm, 1), ALU.mult, ALU.mult))
            own.wait(m)
            dve.tensor_tensor(row(sm, 5), row(sm, 4), row(sm, 8), ALU.add).then_inc(var_done, 1)

        def newton(own, v, y, a, b, c, out):
            m = own.done(dve.tensor_tensor(a, y, y, ALU.mult))
            own.wait(m)
            m = own.done(dve.tensor_tensor(b, a, v, ALU.mult))
            own.wait(m)
            m = own.done(dve.tensor_scalar(c, b, -0.5, 1.5, ALU.mult, ALU.add))
            own.wait(m)
            return dve.tensor_tensor(out, c, y, ALU.mult)

        def refine(n, own):
            dve.wait_ge(y0_done, n + 1)
            newton(own, row(sm, 5), row(sm, 7), row(sm, 9), row(sm, 10), row(sm, 12), row(sm, 11)
                   ).then_inc(stats_done, 1)

        def logits(n):
            dve.wait_ge(wl_done, n + 1)
            dve.tensor_reduce(logit[:, :], wl[:, :, :], AX.X, ALU.add).then_inc(logit_done, 1)

        def seg_shift(n, own, at):
            dve.wait_ge(work_ready, at)
            r = ps_r[0:H0, 0:P].rearrange("h (g s) -> h g s", s=SEG)
            m = own.done(dve.tensor_reduce(smax[:, :], r, AX.X, ALU.max))
            own.wait(m)
            dve.tensor_tensor(e0[:, :].rearrange("h (g s) -> h g s", s=SEG), r,
                              smax[:, :].unsqueeze(2).to_broadcast([H0, SPW, SEG]), ALU.subtract).then_inc(e0_done, 1)

        def seg_probs(n, own):
            dve.wait_ge(e1_done, n + 1)
            e = e1[:, :].rearrange("h (g s) -> h g s", s=SEG)
            m = own.done(dve.tensor_reduce(ssum[:, :], e, AX.X, ALU.add))
            own.wait(m)
            m = own.done(dve.reciprocal(srec[:, :], ssum[:, :]))
            own.wait(m)
            dve.tensor_tensor(pk[:, :].rearrange("h (g s) -> h g s", s=SEG), e,
                              srec[:, :].unsqueeze(2).to_broadcast([H0, SPW, SEG]), ALU.mult).then_inc(pk_done, 1)

        def seg_weights(n, at):
            dve.wait_ge(work_ready, at)
            dve.tensor_tensor(wg[:, :, :], ps_r[:, 0:H0].unsqueeze(2).to_broadcast([P, H0, SPW]),
                              segsel[:, :].unsqueeze(1).to_broadcast([P, H0, SPW]), ALU.mult).then_inc(wg_done, 1)

        def seg_variance(n, own, at):
            dve.wait_ge(work_ready, at)
            dve.tensor_tensor(gm[:, :, :], ps_r[:, 0:4 * DH].rearrange("p (h d) -> p h d", h=4),
                              headsel[:, :].unsqueeze(2).to_broadcast([P, 4, DH]), ALU.mult).then_inc(gm_done, 1)
            dve.wait_ge(gm_done, n + 1)
            m = own.done(dve.tensor_reduce(g0[:, :], gm[:, :, :].rearrange("p h d -> p d h"), AX.X, ALU.add))
            own.wait(m)
            m = own.done(dve.bn_stats(gst[:, :], g0[:, :]))
            own.wait(m)
            dve.memset(gsm[:, 7:8], 0.0)
            m = own.done(dve.bn_aggr(gmv[:, :], gst[:, :]))
            own.wait(m)
            dve.tensor_scalar(gsm[:, 0:1], gmv[:, 1:2], EPS, None, ALU.add).then_inc(gvar_done, 1)

        def seg_keys(n, own):
            dve.wait_ge(gy0_done, n + 1)
            m = own.done(newton(own, gsm[:, 0:1], gsm[:, 2:3], gsm[:, 3:4], gsm[:, 4:5], gsm[:, 5:6], gsm[:, 6:7]))
            own.wait(m)
            m = own.done(dve.tensor_scalar(g1[:, :], g0[:, :], gmv[:, 0:1], gsm[:, 6:7], ALU.subtract, ALU.mult))
            own.wait(m)
            m = own.done(dve.tensor_tensor(g2[:, :], g1[:, :], gg[:, :], ALU.mult))
            own.wait(m)
            dve.wait_ge(gk_stored, 16 * n)
            dve.tensor_tensor(gk[:, :, :], g2[:, :].unsqueeze(1).to_broadcast([P, 2, DH]),
                              gb[:, :].unsqueeze(1).to_broadcast([P, 2, DH]), ALU.add).then_inc(gk_done, 1)

        def affine(n, own):
            dve.wait_ge(vn_done, n + 1)
            m = own.done(dve.tensor_tensor(cen[:, :, :], vn[:, :, :], lg[:, :].unsqueeze(1).to_broadcast([P, H0, DH]),
                                           ALU.mult))
            own.wait(m)
            dve.wait_ge(v_copied, n)
            dve.tensor_tensor(vst[:, :, :], cen[:, :, :], lb[:, :].unsqueeze(1).to_broadcast([P, H0, DH]),
                              ALU.add).then_inc(vst_done, 1)

        def copy_segments(n, w, at):
            dve.wait_ge(work_ready, at)
            r = ps_r[:, 0:P].rearrange("p (k a s) -> p k a s", a=2, s=SPW)
            for a in range(2):
                c = dve.tensor_copy(KT[:, a:H0:2, bass.ds(w * SPW + GLOB[a], SPW)], r[:, :, a, :])
            c.then_inc(g_copied, 1)

        def maxima(t, p):
            dve.wait_ge(scores_ready, PAIRS * t + p + 1)
            dve.tensor_reduce(nmax[:, p % 2, :], ps_s[p % 2][:, :, 0:KEYS], AX.X, ALU.max,
                              negate=True).then_inc(max_done, 1)

        def recips(t, p):
            dve.wait_ge(exp_done, PAIRS * t + p + 1)
            dve.reciprocal(prec[:, p % 2, :], psums[:, p % 2, :]).then_inc(recip_done, 1)

        def copy_g(t, p):
            dve.wait_ge(turned, PAIRS * t + p + 1)
            if p >= 2:
                dve.wait_ge(pv_done, PAIRS * t + p - 1)
            else:
                dve.wait_ge(pv_done, PAIRS * t)
            dve.tensor_copy(prT[:, p % 2, 4 * P:5 * P], ps_g[:, 0:P]).then_inc(g_copied, 1)

        def residual(t, at):
            dve.wait_ge(work_ready, at)
            dve.tensor_tensor(res[:, bass.ds(t, 1), :].rearrange("p a d -> p (a d)"), ps_r[:, 0:D],
                              x_sb[:, bass.ds(t, 1), :].rearrange("p a d -> p (a d)"), ALU.add).then_inc(res_done, 1)

        dve.wait_ge(consts, ALL_CONSTS)
        dve.wait_ge(zeroed, 4)
        own = Tally(dve, dve_step, 0)
        rotate(0, 0, 0, 1)
        rotate(0, 0, 1, 2)
        for quad in range(4):
            q_mult(0, 0, 0, quad, 3 + quad)
        stats(0, 0)
        variance(0, own, own.done(stats(0, 1)))
        refine(0, own)
        logits(0)
        seg_shift(0, own, 7)
        seg_probs(0, own)
        seg_weights(0, 8)
        seg_variance(0, own, 9)
        seg_keys(0, own)
        affine(0, own)
        copy_segments(0, 0, 12)
        assert own.n == DVE_STEPS, own.n
        def two_tiles(i):
            for par in range(2):
                t = i * 2 + par
                n, np_ = t + 1, 1 - par
                w = n % WIN
                ready = 13 * t + 12
                own = Tally(dve, dve_step, n * DVE_STEPS)
                for p in range(PAIRS):
                    maxima(t, p)
                    if p == 0:
                        rotate(n, w, 0, ready + 1)
                    elif p == 1:
                        q_mult(n, np_, w, 0, ready + 3)
                    elif p == 2:
                        q_mult(n, np_, w, 2, ready + 5)
                    elif p == 3:
                        variance(n, own, mark)
                    elif p == 4:
                        refine(n, own)
                    elif p == 5:
                        seg_probs(n, own)
                    elif p == 7:
                        seg_variance(n, own, ready + 9)
                    recips(t, p)
                    if p == 0:
                        rotate(n, w, 1, ready + 2)
                    elif p == 1:
                        q_mult(n, np_, w, 1, ready + 4)
                    elif p == 2:
                        q_mult(n, np_, w, 3, ready + 6)
                        stats(n, 0)
                    elif p == 3:
                        logits(n)
                    elif p == 4:
                        seg_shift(n, own, ready + 7)
                    if p > 0:
                        copy_g(t, p - 1)
                    if p == 5:
                        seg_weights(n, ready + 8)
                    elif p == 2:
                        mark = own.done(stats(n, 1))
                seg_keys(n, own)
                affine(n, own)
                copy_g(t, PAIRS - 1)
                copy_segments(n, w, ready + 12)
                residual(t, ready + 13)
                assert own.n == DVE_STEPS

        two_tiles(0)
        with dve.Fori(1, TILES // 2) as i:
            two_tiles(i)

I32 = mybir.dt.int32
GROUPS = TILES // 4
GT = 4
GC = GT * P
H1, D1 = 16, 8
PARTS = 3
E, F = 8, 512


def rsqrt(own, v, y, t):
    dve = own.eng
    own.wait(own.done(dve.tensor_scalar(t.bitcast(I32), v.bitcast(I32), 1, None, ALU.logical_shift_right)))
    own.wait(own.done(dve.tensor_scalar(y.bitcast(I32), t.bitcast(I32), -1.0, 1597463007.0, ALU.mult, ALU.add)))
    for k in range(3):
        own.wait(own.done(dve.tensor_tensor(t, y, y, ALU.mult)))
        own.wait(own.done(dve.scalar_tensor_tensor(t, t, -0.5, v, ALU.mult, ALU.mult)))
        last = dve.scalar_tensor_tensor(y, t, 1.5, y, ALU.add, ALU.mult)
        if k < 2:
            own.wait(own.done(last))
    return last


def layernorm(own, src, dst, st, mv, ve, y, t, n=GT):
    dve = own.eng
    for k in range(n):
        last = dve.bn_stats(st[:, k, :], src[:, k, :])
    own.wait(own.done(last))
    dve.memset(t[:, 0:1], 0.0)
    for k in range(n):
        last = dve.bn_aggr(mv[:, k, :], st[:, k, :])
    own.wait(own.done(last))
    own.wait(own.done(dve.tensor_scalar(ve, mv[:, :, 1], EPS, None, ALU.add)))
    own.wait(own.done(rsqrt(own, ve, y, t)))
    for k in range(n):
        last = dve.tensor_scalar(dst(k), src[:, k, :], mv[:, k, 0:1], y[:, k:k + 1], ALU.subtract, ALU.mult)
    return last


def between_attentions(nc, ctx, io, res, x2, v1, parts_dram):

    def sb(name, shape, dt=F32):
        return ctx.enter_context(nc.sbuf_tensor(name, shape, dt))

    def sem(name):
        return ctx.enter_context(nc.semaphore(name))

    bout = sb("bout", [P, D])
    bv = sb("bv", [P, D])
    bqk = sb("bqk", [P, 4])
    wqk = sb("wqk", [P, 4, D])
    wv = sb("wv", [P, D])
    cos1, sin1 = sb("cos1", [P, 2, N]), sb("sin1", [P, 2, N])
    ident = sb("ident_b", [P, P])
    ones = sb("ones_b", [P, P])
    w = sb("w", [P, D])
    tern = sb("tern", [P, D])
    ternT = sb("ternT", [P, D])
    ws = sb("ws", [P, 8])
    xb = sb("xb", [P, GT, D])
    x1 = sb("x1", [P, GT, D])
    x1T = sb("x1T", [P, GC])
    xf = sb("xf", [P, GT, D])
    x2T = sb("x2T", [P, GC])
    st = sb("stb", [P, GT, 6])
    mv = sb("mvb", [P, GT, 2])
    sv = sb("svb", [P, 3, GT])
    rot = sb("rot", [P, 2, 2, GC])
    full = sb("full", [P, 2, GC])
    rest = sb("rest", [P, 2, 2, GC])
    part = sb("part", [P, 2, PARTS, GC], BF16)
    ps = [ctx.enter_context(nc.psum_tensor(f"psb{k}", [P, 512], F32)) for k in range(8)]

    consts = sem("consts_b")
    w_step = sem("w_step")
    row_sums = sem("row_sums")
    w_sum = sem("w_sum")
    tern_done = sem("tern_done")
    tern_turned = sem("tern_turned")
    ternT_done = sem("ternT_done")
    ones_done = sem("ones_done")
    x1_done = sem("x1_done")
    x1_turned = sem("x1_turned")
    x1T_done = sem("x1T_done")
    ffn_done = sem("ffn_done")
    x2_done = sem("x2_done")
    x2_turned = sem("x2_turned")
    x2T_done = sem("x2T_done")
    qk_done = sem("qk_done")
    v_done = sem("v_done")
    v_kept = sem("v_kept")
    rot_done = sem("rot_done")
    full_done = sem("full_done")
    hi_done = sem("hi_done")
    r1_done = sem("r1_done")
    mid_done = sem("mid_done")
    r2_done = sem("r2_done")
    lo_done = sem("lo_done")
    stored = [sem(f"stored{k}") for k in range(2)]
    dve_step = sem("dve_step_b")
    STEPS = 30

    loads = [(bout[:, :], io["bout"].to_broadcast([P, D])), (bv[:, :], io["bv"].to_broadcast([P, D])),
             (bqk[:, :], io["bqk"]), (wqk[:, :, :], io["wqk"]), (wv[:, :], io["wv"]),
             (cos1[:, :, :], io["cos1"]), (sin1[:, :, :], io["sin1"]), (ident[:, :], io["ident"]),
             (w[:, :], io["w"])]
    ALL = 16 * len(loads)
    block = ctx.enter_context(nc.Block())

    @block.sync
    def _(sp):
        for dst, src in loads:
            sp.dma_start(dst, src).then_inc(consts, 16)
        def group(g):
            for k in range(2):
                sp.wait_ge(lo_done, 2 * g + k + 1)
                sp.dma_start(parts_dram[k].rearrange("j c t -> c j t")[:, :, bass.ds(g * GC, GC)],
                             part[:, k, :, :]).then_inc(stored[k], 16)

        group(0)
        with sp.Fori(1, GROUPS) as g:
            group(g)
        for k in range(2):
            sp.wait_ge(stored[k], 16 * GROUPS)

    @block.gpsimd
    def _(pool):
        pool.memset(ones[:, :], 1.0).then_inc(ones_done, 1)
        pool.memset(v1[:, :, :, :], 0.0).then_inc(ones_done, 1)
        def group(g):
            for k in range(2):
                pool.wait_ge(rot_done, 4 * g + 2 * k + 2)
                pool.wait_ge(r1_done, 2 * g + k)
                pool.tensor_tensor(full[:, k, :], rot[:, k, 0, :], rot[:, k, 1, :], ALU.add).then_inc(full_done, 1)

        group(0)
        with pool.Fori(1, GROUPS) as g:
            group(g)

    @block.scalar
    def _(act):
        def group(g):
            act.wait_ge(x1_turned, g + 1)
            act.activation(x1T[:, :], ps[0][:, :], ACT.Copy).then_inc(x1T_done, 1)
            act.wait_ge(x2_turned, g + 1)
            act.activation(x2T[:, :], ps[2][:, :], ACT.Copy).then_inc(x2T_done, 1)
            for src, ready, done, j in ((full, full_done, hi_done, 0), (rest, r1_done, mid_done, 1),
                                        (rest, r2_done, lo_done, 2)):
                for k in range(2):
                    act.wait_ge(ready, 2 * g + k + 1)
                    if j == 0:
                        act.wait_ge(stored[k], 16 * g)
                    s = full[:, k, :] if j == 0 else rest[:, k, j - 1, :]
                    act.activation(part[:, k, j, :], s, ACT.Copy).then_inc(done, 1)

        group(0)
        with act.Fori(1, GROUPS) as g:
            group(g)

    @block.tensor
    def _(pe):
        pe.wait_ge(ones_done, 2)
        pe.wait_ge(consts, ALL)
        pe.wait_ge(row_sums, 1)
        pe.matmul(ps[0][:, 0:1], ones[:, :], ws[:, 0:1], start=True, stop=True).then_inc(w_sum, 1)
        pe.wait_ge(tern_done, 1)
        pe.transpose(ps[1][:, 0:D], tern[:, :], ident[:, :]).then_inc(tern_turned, 1)
        pe.wait_ge(ternT_done, 1)
        def group(g):
            pe.wait_ge(x1_done, g + 1)
            for k in range(GT):
                mm = pe.transpose(ps[0][:, k * P:(k + 1) * P], x1[:, k, :], ident[:, :])
            mm.then_inc(x1_turned, 1)
            pe.wait_ge(x1T_done, g + 1)
            for k in range(GT):
                mm = pe.matmul(ps[1][:, k * P:(k + 1) * P], x1T[:, k * P:(k + 1) * P], ternT[:, :], start=True, stop=True)
            mm.then_inc(ffn_done, 1)
            pe.wait_ge(x2_done, g + 1)
            for k in range(GT):
                mm = pe.transpose(ps[2][:, k * P:(k + 1) * P], xb[:, k, :], ident[:, :])
            mm.then_inc(x2_turned, 1)
            pe.wait_ge(x2T_done, g + 1)
            pe.wait_ge(rot_done, 4 * g)
            for k in range(4):
                pe.matmul(ps[4 + k][:, :], wqk[:, k, :], x2T[:, :], start=True, stop=True).then_inc(qk_done, 1)
            pe.wait_ge(v_kept, g)
            for k in range(GT):
                mm = pe.matmul(ps[3][:, k * P:(k + 1) * P], x2T[:, k * P:(k + 1) * P], wv[:, :], start=True, stop=True)
            mm.then_inc(v_done, 1)

        group(0)
        with pe.Fori(1, GROUPS) as g:
            group(g)

    @block.vector
    def _(dve):
        dve.wait_ge(consts, ALL)
        dve.wait_ge(ones_done, 2)
        own = Tally(dve, w_step)
        dve.tensor_reduce(ws[:, 0:1], w[:, :], AX.X, ALU.add, apply_absolute_value=True).then_inc(row_sums, 1)
        dve.wait_ge(w_sum, 1)
        own.wait(own.done(dve.tensor_scalar(ws[:, 1:2], ps[0][:, 0:1], 1.0 / (D * D), EPS, ALU.mult, ALU.max)))
        own.wait(own.done(dve.reciprocal(ws[:, 2:3], ws[:, 1:2])))
        own.wait(own.done(dve.tensor_scalar(tern[:, :], w[:, :], ws[:, 2:3], None, ALU.mult)))
        own.wait(own.done(dve.tensor_scalar(tern[:, :], tern[:, :], 12582912.0, None, ALU.add)))
        own.wait(own.done(dve.tensor_scalar(tern[:, :], tern[:, :], -12582912.0, 1.0, ALU.add, ALU.min)))
        dve.tensor_scalar(tern[:, :], tern[:, :], -1.0, ws[:, 1:2], ALU.max, ALU.mult).then_inc(tern_done, 1)
        dve.wait_ge(tern_turned, 1)
        dve.tensor_copy(ternT[:, :], ps[1][:, 0:D]).then_inc(ternT_done, 1)
        def group(g):
            own = Tally(dve, dve_step, g * STEPS)
            tiles = bass.ds(g * GT, GT)
            dve.wait_ge(x2_turned, g)
            own.wait(own.done(dve.tensor_tensor(xb[:, :, :], res[:, tiles, :],
                                                bout[:, :].unsqueeze(1).to_broadcast([P, GT, D]), ALU.add)))
            layernorm(own, xb, lambda k: x1[:, k, :], st, mv, sv[:, 0, :], sv[:, 1, :], sv[:, 2, :]).then_inc(x1_done, 1)
            dve.wait_ge(ffn_done, g + 1)
            dve.wait_ge(x1_done, g + 1)
            own.wait(own.done(dve.tensor_tensor(xf[:, :, :], ps[1][:, :].rearrange("p (k d) -> p k d", k=GT),
                                                x1[:, :, :], ALU.add)))
            layernorm(own, xf, lambda k: xb[:, k, :], st, mv, sv[:, 0, :], sv[:, 1, :], sv[:, 2, :]).then_inc(x2_done, 1)
            dve.wait_ge(x2_done, g + 1)
            dve.tensor_copy(x2[:, tiles, :], xb[:, :, :])
            half = bass.ds(g % 2 * GC, GC)
            for k in range(2):
                for c, table in enumerate((cos1, sin1)):
                    dve.wait_ge(qk_done, 4 * g + 2 * k + c + 1)
                    dve.wait_ge(full_done, 2 * g)
                    dve.scalar_tensor_tensor(rot[:, k, c, :], ps[4 + 2 * k + c][:, :], bqk[:, 2 * k + c:2 * k + c + 1],
                                             table[:, k, half], ALU.add, ALU.mult).then_inc(rot_done, 1)
            dve.wait_ge(v_done, g + 1)
            dve.tensor_tensor(v1[:, tiles, :, 0:D1].rearrange("p k h d -> p k h d"),
                              ps[3][:, :].rearrange("p (k h d) -> p k h d", k=GT, h=H1),
                              bv[:, :].rearrange("p (h d) -> p h d", h=H1).unsqueeze(1).to_broadcast([P, GT, H1, D1]),
                              ALU.add).then_inc(v_kept, 1)
            for k in range(2):
                dve.wait_ge(hi_done, 2 * g + k + 1)
                dve.wait_ge(lo_done, 2 * g)
                dve.tensor_tensor(rest[:, k, 0, :], full[:, k, :], part[:, k, 0, :], ALU.subtract).then_inc(r1_done, 1)
            for k in range(2):
                dve.wait_ge(mid_done, 2 * g + k + 1)
                dve.wait_ge(r1_done, 2 * g + k + 1)
                dve.tensor_tensor(rest[:, k, 1, :], rest[:, k, 0, :], part[:, k, 1, :], ALU.subtract).then_inc(r2_done, 1)
            assert own.n == STEPS, own.n

        group(0)
        with dve.Fori(1, GROUPS) as g:
            group(g)
        own = Tally(dve, w_step, 5)
        dve.wait_ge(ones_done, 2)
        dve.memset(v1[:, :, :, D1:D1 + 1], 1.0).then_inc(ones_done, 1)


def layer1_attention(nc, ctx, io, v1, parts_dram, inter):

    def sb(name, shape, dt=F32):
        return ctx.enter_context(nc.sbuf_tensor(name, shape, dt))

    def sem(name):
        return ctx.enter_context(nc.semaphore(name))

    G = 4
    SPB = H1 // G
    KB = N // P
    HALF = N // 2
    STEPS = 2 * KB
    FULL = 96
    CHUNKS = [5] * 12 + [4, 0, 0, 0]
    TURN_M = {4: 0, 7: 1, 10: 2, 13: 3}
    TURN_O = 11
    LOADS = 2 * PARTS * PARTS
    assert sum(CHUNKS) == G * KB * 2

    ident = sb("ident_c", [P, P])
    identb = sb("identb_c", [P, P], BF16)
    qa = sb("qa", [P, SPB, G, N], BF16)
    ka = sb("ka", [P, SPB, G, N], BF16)
    vg = sb("vg", [P, 2, KB, G, 32])
    pT = sb("pT", [P, 2, G, HALF])
    cmax = sb("cmax", [P, 2, KB, 2])
    nm = sb("nm", [P, 2, KB])
    nr = sb("nr", [P, 2, KB])
    mp = sb("mp", [P, 2, PARTS, KB], BF16)
    mT = sb("mT", [PARTS * KB, G, P], BF16)
    oT = sb("oT1", [P, HALF])
    orec = sb("orec", [P, G, G])

    ps_t = [ctx.enter_context(nc.psum_tensor(f"ps_t{k}", [P, 2, HALF], F32)) for k in range(2)]
    ps_q = [ctx.enter_context(nc.psum_tensor(f"ps_q{k}", [P, 512], F32)) for k in range(2)]
    ps_o = ctx.enter_context(nc.psum_tensor("ps_o1", [P, 512], F32))
    ps_w = ctx.enter_context(nc.psum_tensor("ps_w1", [P, 512], F32))
    turned_m = ps_w[0:PARTS * KB, :].bitcast(BF16)[:, 0:P]

    consts = sem("consts_c")
    filled = sem("filled")
    loaded = [sem(f"loaded{k}") for k in range(SPB)]
    vg_done = sem("vg_done")
    chunk_ready = sem("chunk_ready")
    chunk_read = sem("chunk_read")
    m_split = sem("m_split")
    m_turned = sem("m_turned")
    m_copied = sem("m_copied")
    m_placed = [sem(f"m_placed{k}") for k in range(SPB)]
    t_ready = sem("t_ready")
    t_exp = sem("t_exp")
    pv_done = sem("pv_done1")
    o_copied = sem("o_copied1")
    o_turned = sem("o_turned")
    o_kept = sem("o_kept")
    dve_step = sem("dve_step_c")
    OWN_SPLITS, OWN_TURN = 5 * G, 5 * G + 2

    def after(i, hg, k):
        return (i + (hg + k) // SPB), (hg + k) % SPB

    block = ctx.enter_context(nc.Block())

    @block.sync
    def _(sp):
        sp.dma_start(ident[:, :], io["ident"]).then_inc(consts, 16)
        sp.dma_start(identb[:, :], io["identb"]).then_inc(consts, 16)

        def load(b, hg):
            chans = slice(hg * G * D1, (hg + 1) * G * D1)
            for i in range(PARTS):
                for j in range(PARTS):
                    r = slice((i * PARTS + j) * D1, (i * PARTS + j + 1) * D1)
                    for dst, src in ((qa, parts_dram[0, i]), (ka, parts_dram[1, j])):
                        sp.dma_start(dst[r, hg, :, :], src[chans, bass.ds(b * N, N)].rearrange("(a d) t -> d a t", a=G)
                                     ).then_inc(loaded[hg], 16)

        def place(s, hg):
            for a in range(G):
                sp.wait_ge(m_copied, G * s + a + 1)
                sp.dma_start(qa[FULL:FULL + PARTS, hg, a, :], mT[:, a, :]).then_inc(m_placed[hg], 16)

        def turn(i, hg, last_batch):
            s = i * SPB + hg
            b, at = after(i, hg, 3)
            if not (last_batch and hg >= 1):
                sp.wait_ge(t_exp, 32 * s)
                load(b, at)
            if not (last_batch and hg == SPB - 1):
                place(s + 1, (hg + 1) % SPB)

        sp.wait_ge(filled, 4)
        for hg in range(3):
            load(0, hg)
        place(0, 0)
        def batch(i):
            for hg in range(SPB):
                turn(i, hg, False)

        batch(0)
        with sp.Fori(1, B - 1) as i:
            batch(i)
        for hg in range(SPB):
            turn(B - 1, hg, True)

    @block.gpsimd
    def _(pool):
        pool.memset(qa[:, :, :, :], 0.0).then_inc(filled, 1)
        pool.memset(ka[:, :, :, :], 0.0).then_inc(filled, 1)
        pool.wait_ge(filled, 2)
        pool.memset(ka[FULL:FULL + PARTS, :, :, :], 1.0).then_inc(filled, 1)
        pool.wait_ge(filled, 3)
        pool.memset(vg[:, :, :, :, :], 0.0).then_inc(filled, 1)
        pool.wait_ge(filled, 4)

        def values(b, hg):
            for k in range(KB):
                c = pool.tensor_copy(vg[:, hg % 2, k, :, 0:D1 + 1],
                                     v1[:, bass.ds(b * KB + k, 1), hg * G:(hg + 1) * G, :]
                                     .rearrange("p a h d -> p (a h) d"))
            c.then_inc(vg_done, 1)

        def turn(i, hg):
            pool.wait_ge(pv_done, STEPS * (i * SPB + hg))
            values(*after(i, hg, 1))

        values(0, 0)
        def batch(i):
            for hg in range(SPB):
                turn(i, hg)

        batch(0)
        with pool.Fori(1, B - 1) as i:
            batch(i)
        for hg in range(SPB - 1):
            turn(B - 1, hg)

    @block.scalar
    def _(act):
        def exps(s, step, k):
            act.wait_ge(t_ready, 32 * s + 2 * step + k + 1)
            if step >= 2:
                act.wait_ge(pv_done, STEPS * s + step - 1)
            else:
                act.wait_ge(pv_done, STEPS * s)
            act.activation(pT[:, step % 2, 2 * k:2 * k + 2, :], ps_t[k][:, :, :], ACT.Exp).then_inc(t_exp, 1)

        def copy_o(s, h):
            act.wait_ge(pv_done, STEPS * s + KB * h + KB)
            act.wait_ge(o_turned, 2 * s + h)
            act.activation(oT[:, :], ps_o[:, :], ACT.Copy).then_inc(o_copied, 1)

        def one_set(s):
            for step in range(STEPS):
                for k in range(2):
                    exps(s, step, k)
                if step == KB:
                    copy_o(s, 0)
            copy_o(s, 1)

        one_set(0)
        with act.Fori(1, B * SPB) as s:
            one_set(s)

    @block.tensor
    def _(pe):
        def chunk(s, hg, c):
            a, k, h = c // 16, c // 2 % KB, c % 2
            pe.wait_ge(chunk_read, 64 * s + max(c - 1, 0))
            pe.matmul(ps_q[c % 2][:, :], qa[0:FULL, hg, a, k * P:(k + 1) * P], ka[0:FULL, hg, a, h * 512:(h + 1) * 512],
                      start=True, stop=True).then_inc(chunk_ready, 1)

        def turn_m(s, a):
            pe.wait_ge(m_split, G * s + a + 1)
            pe.transpose(turned_m, mp[:, a % 2, :, :].rearrange("p j k -> p (j k)"), identb[:, :]).then_inc(m_turned, 1)

        def scores(s, hg, step):
            kb, h = step % KB, step // KB
            for k in range(2):
                pe.wait_ge(t_exp, 32 * s + (2 * step + k - 1 if step else 0))
                for a in range(2):
                    mm = pe.matmul(ps_t[k][:, a, :], ka[:, hg, 2 * k + a, kb * P:(kb + 1) * P],
                                   qa[:, hg, 2 * k + a, h * HALF:(h + 1) * HALF], start=True, stop=True)
                mm.then_inc(t_ready, 1)

        def values(s, hg, step):
            kb = step % KB
            pe.wait_ge(t_exp, 32 * s + 2 * step + 2)
            if kb == 0:
                pe.wait_ge(o_copied, 2 * s + step // KB)
            for a in range(G):
                mm = pe.matmul(ps_o[32 * a:32 * a + 32, :], vg[:, hg % 2, kb, a, :], pT[:, step % 2, a, :],
                               start=(kb == 0), stop=(kb == KB - 1), skip_group_check=True)
            mm.then_inc(pv_done, 1)

        def turn_o(s, h):
            pe.wait_ge(o_copied, 2 * s + h + 1)
            for k in range(4):
                mm = pe.transpose(ps_w[:, k * P:(k + 1) * P], oT[:, k * P:(k + 1) * P], ident[:, :])
            mm.then_inc(o_turned, 1)

        def turn(i, hg, last):
            s = i * SPB + hg
            b, at = after(i, hg, 1)
            pe.wait_ge(m_placed[hg], 16 * G * (i + 1))
            pe.wait_ge(vg_done, s + 1)
            if not last:
                pe.wait_ge(loaded[at], 16 * LOADS * (b + 1))
            c = 0
            for step in range(STEPS):
                scores(s, hg, step)
                if not last:
                    for _ in range(CHUNKS[step]):
                        chunk(s + 1, at, c)
                        c += 1
                    if step in TURN_M:
                        a = TURN_M[step]
                        if a == 0:
                            pe.wait_ge(o_kept, 2 * s)
                        elif a == 3:
                            pe.wait_ge(o_kept, 2 * s + 1)
                        else:
                            pe.wait_ge(m_copied, G * (s + 1) + a)
                        turn_m(s + 1, a)
                if step >= 1:
                    values(s, hg, step - 1)
                if step == TURN_O:
                    pe.wait_ge(o_kept, 2 * s)
                    if not last:
                        pe.wait_ge(m_copied, G * (s + 1) + 3)
                    turn_o(s, 0)
            values(s, hg, STEPS - 1)
            pe.wait_ge(o_kept, 2 * s + 1)
            if not last:
                pe.wait_ge(m_copied, G * (s + 1) + G)
            turn_o(s, 1)

        pe.wait_ge(consts, 32)
        pe.wait_ge(filled, 4)
        pe.wait_ge(loaded[0], 16 * LOADS)
        for a in range(G):
            for c in range(16 * a, 16 * a + 16):
                chunk(0, 0, c)
            if a:
                pe.wait_ge(m_copied, a)
            turn_m(0, a)
        def batch(i):
            for hg in range(SPB):
                turn(i, hg, False)

        batch(0)
        with pe.Fori(1, B - 1) as i:
            batch(i)
        for hg in range(SPB):
            turn(B - 1, hg, hg == SPB - 1)

    @block.vector
    def _(dve):
        def maximum(s, c):
            a, k, h = c // 16, c // 2 % KB, c % 2
            dve.wait_ge(chunk_ready, 64 * s + c + 1)
            dve.tensor_reduce(cmax[:, a % 2, k, h:h + 1], ps_q[c % 2][:, :], AX.X, ALU.max,
                              negate=True).then_inc(chunk_read, 1)

        def split(s, a, own):
            dve.wait_ge(chunk_read, 64 * s + 16 * a + 16)
            dve.wait_ge(m_turned, G * s + max(a - 1, 0))
            own.wait(own.done(dve.tensor_tensor(nm[:, a % 2, :], cmax[:, a % 2, :, 0], cmax[:, a % 2, :, 1], ALU.min)))
            own.wait(own.done(dve.tensor_copy(mp[:, a % 2, 0, :], nm[:, a % 2, :])))
            own.wait(own.done(dve.tensor_tensor(nr[:, a % 2, :], nm[:, a % 2, :], mp[:, a % 2, 0, :], ALU.subtract)))
            own.wait(own.done(dve.tensor_copy(mp[:, a % 2, 1, :], nr[:, a % 2, :])))
            own.wait(own.done(dve.tensor_tensor(nm[:, a % 2, :], nr[:, a % 2, :], mp[:, a % 2, 1, :], ALU.subtract)))
            dve.tensor_copy(mp[:, a % 2, 2, :], nm[:, a % 2, :]).then_inc(m_split, 1)

        def copy_m(s, a):
            dve.wait_ge(m_turned, G * s + a + 1)
            dve.tensor_copy(mT[:, a, :], turned_m).then_inc(m_copied, 1)

        def keep_o(i, hg, h, own):
            s = i * SPB + hg
            dve.wait_ge(o_turned, 2 * s + h + 1)
            r = ps_w[:, :].rearrange("p (k a c) -> p k a c", k=4, a=G)
            own.wait(own.done(dve.reciprocal(orec[:, :, :], r[:, :, :, D1])))
            dst = inter[:, bass.ds(i * KB + h * 4, 4), hg * (G * D1):(hg + 1) * (G * D1)].rearrange("p k (a d) -> p k a d", a=G)
            dve.tensor_tensor(dst, r[:, :, :, 0:D1], orec[:, :, :].unsqueeze(3).to_broadcast([P, 4, G, D1]),
                              ALU.mult).then_inc(o_kept, 1)

        def turn(i, hg, last):
            s = i * SPB + hg
            own = Tally(dve, dve_step, OWN_SPLITS + OWN_TURN * s)
            c = 0
            if not last:
                dve.wait_ge(m_placed[hg], 16 * G * (i + 1))
            for step in range(STEPS):
                if not last:
                    for _ in range(CHUNKS[step]):
                        maximum(s + 1, c)
                        if c % 16 == 15:
                            split(s + 1, c // 16, own)
                        c += 1
                    if step in TURN_M:
                        copy_m(s + 1, TURN_M[step])
                if step == TURN_O:
                    keep_o(i, hg, 0, own)
            keep_o(i, hg, 1, own)
            assert last or own.n == OWN_TURN

        own = Tally(dve, dve_step)
        for a in range(G):
            for c in range(16 * a, 16 * a + 16):
                maximum(0, c)
            split(0, a, own)
            copy_m(0, a)
        assert own.n == OWN_SPLITS
        def batch(i):
            for hg in range(SPB):
                turn(i, hg, False)

        batch(0)
        with dve.Fori(1, B - 1) as i:
            batch(i)
        for hg in range(SPB):
            turn(B - 1, hg, hg == SPB - 1)


def output_and_experts(nc, ctx, io, x2, inter, out):

    def sb(name, shape, dt=F32):
        return ctx.enter_context(nc.sbuf_tensor(name, shape, dt))

    def sem(name):
        return ctx.enter_context(nc.semaphore(name))

    FC = F // P
    RMS_EPS = 1e-6
    ident = sb("ident_d", [P, P])
    wo = sb("wo", [P, D])
    bo = sb("bo", [P, D])
    rms = sb("rms", [P, D])
    gate = sb("gate", [P, E])
    w1 = sb("w1", [P, E, F])
    w2 = sb("w2", [P, E, FC, D])
    b1 = sb("b1", [P, E, FC])
    b2 = sb("b2", [E, D])
    rank = sb("rank", [P, E])
    xi = sb("xi", [P, GT, D])
    iT = sb("iT", [P, GC])
    xs = sb("xs", [P, GT, D])
    x3 = sb("x3", [P, GT, D])
    sq = sb("sq", [P, GT, D])
    xn = sb("xn", [P, GT, D])
    xnT = sb("xnT", [P, 2, GC])
    st = sb("std", [P, 2, GT, 6])
    mv = sb("mvd", [P, 2, GT, 2])
    sv = sb("svd", [P, 2, 5, GT])
    lg = sb("lgd", [P, 5, GT, E])
    tops = sb("tops", [P, 5, GT])
    wts = sb("wts", [P, 2, GT, E])
    wT = sb("wTd", [E, GC])
    hT = sb("hT", [P, 2, FC, GC])
    acc = sb("acc", [P, 2, GT, D])
    ys = sb("ys", [P, GT, D])
    ps_h = [ctx.enter_context(nc.psum_tensor(f"ps_h{k}", [P, 512], F32)) for k in range(2)]
    ps_y = [ctx.enter_context(nc.psum_tensor(f"ps_y{k}", [P, 512], F32)) for k in range(2)]
    ps_w = [ctx.enter_context(nc.psum_tensor(f"ps_w2{k}", [P, 512], F32)) for k in range(4)]

    consts = sem("consts_d")
    xi_done = sem("xi_done")
    i_turned = sem("i_turned")
    iT_done = sem("iT_done")
    proj_done = sem("proj_done")
    xn_done = sem("xn_done")
    xn_turned = sem("xn_turned")
    xnT_done = sem("xnT_done")
    logits_done = sem("logits_done")
    l_shifted = sem("l_shifted")
    l_exp = sem("l_exp")
    weights_done = sem("weights_done")
    w_turned = sem("w_turned")
    wT_done = sem("wT_done")
    bias_done = sem("bias_done")
    acc_begun = sem("acc_begun")
    h_ready = sem("h_ready")
    h_done = sem("h_done")
    y_ready = sem("y_ready")
    y_taken = sem("y_taken")
    out_done = sem("out_done")
    stored = sem("stored_d")
    front_step = sem("front_step")
    back_step = sem("back_step")
    FRONT_STEPS, BACK_STEPS = 37, 14

    loads = [(ident[:, :], io["ident"]), (wo[:, :], io["wo"]), (bo[:, :], io["bo"].to_broadcast([P, D])),
             (rms[:, :], io["rms"].to_broadcast([P, D])), (gate[:, :], io["gate"]), (w1[:, :, :], io["w1"]),
             (w2[:, :, :, :], io["w2"]), (b1[:, :, :], io["b1"]), (b2[:, :], io["b2"]), (rank[:, :], io["rank"])]
    ALL = 16 * len(loads)
    block = ctx.enter_context(nc.Block())

    @block.sync
    def _(sp):
        for dst, src in loads:
            sp.dma_start(dst, src).then_inc(consts, 16)
        def group(g):
            sp.wait_ge(out_done, g + 1)
            sp.dma_start(out.rearrange("(t p) d -> p t d", p=P)[:, bass.ds(g * GT, GT), :], ys[:, :, :]).then_inc(stored, 16)

        group(0)
        with sp.Fori(1, GROUPS) as g:
            group(g)
        sp.wait_ge(stored, 16 * GROUPS)

    @block.gpsimd
    def _(pool):
        def group(n):
            pool.wait_ge(i_turned, n)
            pool.tensor_copy(xi[:, :, :], inter[:, bass.ds(n * GT, GT), :]).then_inc(xi_done, 1)

        group(0)
        with pool.Fori(1, GROUPS) as n:
            group(n)

    @block.scalar
    def _(act):
        def copy_i(n):
            act.wait_ge(i_turned, n + 1)
            act.wait_ge(proj_done, n)
            act.activation(iT[:, :], ps_w[0][:, :], ACT.Copy).then_inc(iT_done, 1)

        def copy_xn(n, par):
            act.wait_ge(xn_turned, n + 1)
            act.activation(xnT[:, par, :], ps_w[2][:, :], ACT.Copy).then_inc(xnT_done, 1)

        def exps(n):
            act.wait_ge(l_shifted, n + 1)
            act.activation(lg[:, 1, :, :], lg[:, 0, :, :], ACT.Exp).then_inc(l_exp, 1)

        def copy_w(n):
            act.wait_ge(w_turned, n + 1)
            act.wait_ge(bias_done, n)
            act.activation(wT[:, :], ps_w[0][0:E, :], ACT.Copy).then_inc(wT_done, 1)

        def silu(g, e, c):
            n = e * FC + c
            act.wait_ge(h_ready, g * (E * FC) + n + 1)
            if e >= 2:
                act.wait_ge(y_ready, g * E + e - 1)
            else:
                act.wait_ge(y_ready, g * E)
            act.activation(hT[:, e % 2, c, :], ps_h[n % 2][:, :], ACT.Silu, bias=b1[:, e, c:c + 1],
                           scale=1.0).then_inc(h_done, 1)

        def turn(g, par, last):
            n = g + 1
            for e in range(E):
                for c in range(FC):
                    silu(g, e, c)
                if not last:
                    if e == 1:
                        copy_i(n)
                    elif e == 4:
                        copy_xn(n, 1 - par)
                    elif e == 5:
                        exps(n)
                    elif e == 7:
                        copy_w(n)

        act.wait_ge(consts, ALL)
        copy_i(0)
        copy_xn(0, 0)
        exps(0)
        copy_w(0)
        def two_groups(i):
            for par in range(2):
                turn(i * 2 + par, par, False)

        two_groups(0)
        with act.Fori(1, GROUPS // 2 - 1) as i:
            two_groups(i)
        turn(GROUPS - 2, 0, False)
        turn(GROUPS - 1, 1, True)

    @block.tensor
    def _(pe):
        def turn_i(n):
            pe.wait_ge(xi_done, n + 1)
            pe.wait_ge(wT_done, n)
            for k in range(GT):
                mm = pe.transpose(ps_w[0][:, k * P:(k + 1) * P], xi[:, k, :], ident[:, :])
            mm.then_inc(i_turned, 1)

        def project(n):
            pe.wait_ge(iT_done, n + 1)
            pe.wait_ge(acc_begun, n)
            for k in range(GT):
                mm = pe.matmul(ps_w[1][:, k * P:(k + 1) * P], iT[:, k * P:(k + 1) * P], wo[:, :], start=True, stop=True)
            mm.then_inc(proj_done, 1)

        def turn_xn(n):
            pe.wait_ge(xn_done, n + 1)
            for k in range(GT):
                mm = pe.transpose(ps_w[2][:, k * P:(k + 1) * P], xn[:, k, :], ident[:, :])
            mm.then_inc(xn_turned, 1)

        def logits(n, par):
            pe.wait_ge(xnT_done, n + 1)
            for k in range(GT):
                mm = pe.matmul(ps_w[3][:, k * E:(k + 1) * E], xnT[:, par, k * P:(k + 1) * P], gate[:, :],
                               start=True, stop=True)
            mm.then_inc(logits_done, 1)

        def turn_w(n, par):
            pe.wait_ge(weights_done, n + 1)
            for k in range(GT):
                mm = pe.transpose(ps_w[0][0:E, k * P:(k + 1) * P], wts[:, par, k, :], ident[:, :])
            mm.then_inc(w_turned, 1)

        def biases(n):
            pe.wait_ge(wT_done, n + 1)
            for k in range(GT):
                mm = pe.matmul(ps_w[1][:, k * P:(k + 1) * P], wT[:, k * P:(k + 1) * P], b2[:, :], start=True, stop=True)
            mm.then_inc(bias_done, 1)

        def inner(g, par, e):
            for c in range(FC):
                n = e * FC + c
                if n >= 2:
                    pe.wait_ge(h_done, g * (E * FC) + n - 1)
                else:
                    pe.wait_ge(h_done, g * (E * FC))
                pe.matmul(ps_h[n % 2][:, :], w1[:, e, c * P:(c + 1) * P], xnT[:, par, :],
                          start=True, stop=True).then_inc(h_ready, 1)

        def outer(g, e):
            pe.wait_ge(h_done, g * (E * FC) + (e + 1) * FC)
            pe.wait_ge(y_taken, g * E + max(e - 1, 0))
            for k in range(GT):
                for c in range(FC):
                    mm = pe.matmul(ps_y[e % 2][:, k * P:(k + 1) * P], hT[:, e % 2, c, k * P:(k + 1) * P], w2[:, e, c, :],
                                   start=(c == 0), stop=(c == FC - 1))
            mm.then_inc(y_ready, 1)

        def turn(g, par, last):
            n = g + 1
            for e in range(E):
                inner(g, par, e)
                if not last:
                    if e == 1:
                        turn_i(n)
                    elif e == 2:
                        project(n)
                    elif e == 4:
                        turn_xn(n)
                    elif e == 5:
                        logits(n, 1 - par)
                    elif e == 7:
                        turn_w(n, 1 - par)
                if e >= 1:
                    outer(g, e - 1)
            if not last:
                biases(n)
            outer(g, E - 1)

        pe.wait_ge(consts, ALL)
        turn_i(0)
        project(0)
        turn_xn(0)
        logits(0, 0)
        turn_w(0, 0)
        biases(0)
        def two_groups(i):
            for par in range(2):
                turn(i * 2 + par, par, False)

        two_groups(0)
        with pe.Fori(1, GROUPS // 2 - 1) as i:
            two_groups(i)
        turn(GROUPS - 2, 0, False)
        turn(GROUPS - 1, 1, True)

    @block.vector
    def _(dve):
        def third_norm(n, own):
            dve.wait_ge(proj_done, n + 1)
            dve.wait_ge(xn_turned, n)
            own.wait(own.done(dve.tensor_tensor(xs[:, :, :], ps_w[1][:, :].rearrange("p (k d) -> p k d", k=GT),
                                                bo[:, :].unsqueeze(1).to_broadcast([P, GT, D]), ALU.add)))
            own.wait(own.done(dve.tensor_tensor(xs[:, :, :], xs[:, :, :], x2[:, bass.ds(n * GT, GT), :], ALU.add)))
            own.wait(own.done(layernorm(own, xs, lambda k: x3[:, k, :], st[:, 0], mv[:, 0], sv[:, 0, 0, :], sv[:, 0, 1, :],
                                        sv[:, 0, 2, :])))
            own.wait(own.done(dve.tensor_tensor(sq[:, :, :], x3[:, :, :], x3[:, :, :], ALU.mult)))
            own.wait(own.done(dve.tensor_reduce(sv[:, 0, 3, :], sq[:, :, :], AX.X, ALU.add)))
            own.wait(own.done(dve.tensor_scalar(sv[:, 0, 0, :], sv[:, 0, 3, :], 1.0 / D, RMS_EPS, ALU.mult, ALU.add)))
            own.wait(own.done(rsqrt(own, sv[:, 0, 0, :], sv[:, 0, 1, :], sv[:, 0, 2, :])))
            for k in range(GT):
                last = dve.scalar_tensor_tensor(xn[:, k, :], x3[:, k, :], sv[:, 0, 1, k:k + 1], rms[:, :],
                                                ALU.mult, ALU.mult)
            last.then_inc(xn_done, 1)

        def shift(n, own):
            dve.wait_ge(logits_done, n + 1)
            r = ps_w[3][:, 0:GT * E].rearrange("p (k e) -> p k e", k=GT)
            own.wait(own.done(dve.tensor_reduce(tops[:, 0, :], r, AX.X, ALU.max)))
            dve.tensor_tensor(lg[:, 0, :, :], r, tops[:, 0, :].unsqueeze(2).to_broadcast([P, GT, E]),
                              ALU.subtract).then_inc(l_shifted, 1)

        def choose(n, par, own):
            def wide(row):
                return tops[:, row, :].unsqueeze(2).to_broadcast([P, GT, E])
            dve.wait_ge(l_exp, n + 1)
            dve.tensor_reduce(tops[:, 1, :], lg[:, 1, :, :], AX.X, ALU.add)
            own.wait(own.done(dve.tensor_reduce(tops[:, 2, :], lg[:, 1, :, :], AX.X, ALU.max)))
            dve.reciprocal(tops[:, 3, :], tops[:, 1, :])
            own.wait(own.done(dve.tensor_tensor(lg[:, 2, :, :], lg[:, 1, :, :], wide(2), ALU.is_ge)))
            dve.tensor_tensor(tops[:, 4, :], tops[:, 2, :], tops[:, 3, :], ALU.mult)
            own.wait(own.done(dve.tensor_tensor(lg[:, 3, :, :], lg[:, 2, :, :],
                                                rank[:, :].unsqueeze(1).to_broadcast([P, GT, E]), ALU.mult)))
            own.wait(own.done(dve.tensor_reduce(tops[:, 0, :], lg[:, 3, :, :], AX.X, ALU.max)))
            own.wait(own.done(dve.tensor_tensor(lg[:, 4, :, :], lg[:, 3, :, :], wide(0), ALU.is_ge)))
            dve.tensor_tensor(wts[:, par, :, :], lg[:, 4, :, :], wide(4), ALU.mult).then_inc(weights_done, 1)

        def begin(n, par):
            dve.wait_ge(bias_done, n + 1)
            dve.tensor_tensor(acc[:, par, :, :], ps_w[1][:, :].rearrange("p (k d) -> p k d", k=GT), x3[:, :, :],
                              ALU.add).then_inc(acc_begun, 1)

        def take(g, par, e, own):
            dve.wait_ge(y_ready, g * E + e + 1)
            if e == 0:
                dve.wait_ge(acc_begun, g + 1)
            else:
                dve.wait_ge(y_taken, g * E + e)
            for k in range(GT):
                last = dve.scalar_tensor_tensor(acc[:, par, k, :], ps_y[e % 2][:, k * P:(k + 1) * P],
                                                wts[:, par, k, e:e + 1], acc[:, par, k, :], ALU.mult, ALU.add)
            last.then_inc(y_taken, 1)

        def last_norm(g, par, own):
            dve.wait_ge(y_taken, g * E + E)
            dve.wait_ge(stored, 16 * g)
            layernorm(own, acc[:, par], lambda k: ys[:, k, :], st[:, 1], mv[:, 1], sv[:, 1, 0, :], sv[:, 1, 1, :],
                      sv[:, 1, 2, :]).then_inc(out_done, 1)

        def turn(g, par, last):
            n = g + 1
            own = Tally(dve, front_step, n * FRONT_STEPS)
            back = Tally(dve, back_step, g * BACK_STEPS)
            for e in range(E):
                if not last:
                    if e == 2:
                        third_norm(n, own)
                    elif e == 5:
                        shift(n, own)
                    elif e == 6:
                        choose(n, 1 - par, own)
                if e >= 1:
                    take(g, par, e - 1, back)
            if not last:
                begin(n, 1 - par)
                assert own.n == FRONT_STEPS, own.n
            take(g, par, E - 1, back)
            last_norm(g, par, back)
            assert back.n == BACK_STEPS, back.n

        dve.wait_ge(consts, ALL)
        own = Tally(dve, front_step)
        third_norm(0, own)
        shift(0, own)
        choose(0, 0, own)
        begin(0, 0)
        def two_groups(i):
            for par in range(2):
                turn(i * 2 + par, par, False)

        two_groups(0)
        with dve.Fori(1, GROUPS // 2 - 1) as i:
            two_groups(i)
        turn(GROUPS - 2, 0, False)
        turn(GROUPS - 1, 1, True)


def build(nc, io, out):
    with ExitStack() as ctx:
        inter = ctx.enter_context(nc.sbuf_tensor("inter", [P, TILES, D], F32))
        parts_dram = nc.dram_tensor("parts_dram", [2, PARTS, P, B * N], BF16, kind="Internal").ap()
        with ExitStack() as phase:
            layer0_attention(nc, phase, io, inter)
        x2 = ctx.enter_context(nc.sbuf_tensor("x2", [P, TILES, D], F32))
        v1 = ctx.enter_context(nc.sbuf_tensor("v1", [P, TILES, H1, D1 + 1], F32))
        with ExitStack() as phase:
            between_attentions(nc, phase, io, inter, x2, v1, parts_dram)
        with ExitStack() as phase:
            layer1_attention(nc, phase, io, v1, parts_dram, inter)
        with ExitStack() as phase:
            output_and_experts(nc, phase, io, x2, inter, out)


def _tables():
    f = np.float32

    def angles(width):
        inv = (f(1) / f(10000) ** (np.arange(0, width, 2, dtype=f) / f(width))).astype(f)
        return (np.arange(N, dtype=f)[:, None] * inv[None]).astype(f)

    t = {}
    a = np.concatenate([angles(DH)] * 2, 1)
    cos, sin = np.cos(a), np.sin(a) * np.repeat(f([-1, 1]), DH // 2)
    t["csT"] = np.concatenate([cos.T, sin.T], 0) * f(DH ** -0.5)
    t["cosn"] = cos.reshape(WIN, P, DH).transpose(1, 0, 2)
    t["sinn"] = sin.reshape(WIN, P, DH).transpose(1, 0, 2)
    masks = np.zeros((P, WIN, 2, KEYS), f)
    q = np.arange(P)[:, None]
    for w in range(WIN):
        own = np.where(np.arange(P)[None] > q, -1e30, 0)
        before = np.full((P, P), -1e30 if w == 0 else 0)
        slots = [own, before] if w % 2 == 0 else [before, own]
        segs = np.where(w * P + q > SEG * np.arange(NSEG)[None] + SEG - 1, 0, -1e30)
        masks[:, w, 0] = np.concatenate(slots + [segs], 1)
        masks[:, w, 1] = np.concatenate([segs] + slots, 1)
    t["masks"] = masks.astype(mybir.dt.np(BF16))
    t["ident"] = np.eye(P, dtype=f)
    t["identb"] = np.eye(P).astype(mybir.dt.np(BF16))
    t["segsel"] = (np.arange(P)[:, None] // SEG == np.arange(SPW)[None]).astype(f)
    t["headsel"] = ((np.arange(P)[:, None] // SPW) % 4 == np.arange(4)[None]).astype(f)
    a = np.repeat(angles(D1), 2, -1)
    cos = np.tile(np.cos(a).T, (H1, 1))
    sin = np.tile((np.sin(a) * np.tile(f([-1, 1]), D1 // 2)).T, (H1, 1))
    scale = f(1) / np.sqrt(f(D))
    t["cos1"] = np.stack([cos * scale, cos], 1)
    t["sin1"] = np.stack([sin * scale, sin], 1)
    t["rank"] = np.tile((E - np.arange(E)).astype(f), (P, 1))
    return t


def kernel(**inputs):
    import concourse.bacc as _bacc
    from concourse.bass_utils import run_bass_kernel_spmd as _run

    v = {k: np.asarray(a) for k, a in inputs.items()}

    def swapped(a):
        return a.reshape(*a.shape[:-1], D // 2, 2)[..., ::-1].reshape(a.shape)

    arrays = _tables()
    x = v["L0_attn_x"].reshape(TILES, P, D)
    wq0 = v["L0_attn_Wq"].reshape(D, H0, DH)
    h = DH // 2
    wq, bq, wk, bk = (v["L1_attn_" + n] for n in ("Wq", "bq", "Wk", "bk"))
    arrays.update(
        x=x.reshape(TILES * P, D), xT=x.transpose(0, 2, 1),
        wqs=np.concatenate([wq0, wq0[:, :, h:], wq0[:, :, :h]], 2),
        wkv=v["L0_attn_Wkv"], wout=v["L0_attn_Wout"], wproj=v["L0_attn_Wproj"],
        lg=v["L0_attn_ln_local_g"][None], lb=v["L0_attn_ln_local_b"][None],
        gg=v["L0_attn_ln_global_g"][None], gb=v["L0_attn_ln_global_b"][None],
        bout=v["L0_attn_bout"][None], w=v["L0_ffn_weight"],
        wqk=np.stack([wq, swapped(wq), wk, swapped(wk)], 1), bqk=np.stack([bq, swapped(bq), bk, swapped(bk)], 1),
        wv=v["L1_attn_Wv"], bv=v["L1_attn_bv"][None], wo=v["L1_attn_Wo"], bo=v["L1_attn_bo"][None],
        rms=v["L1_ffn_rms_w"][None], gate=v["L1_ffn_gate_w"].T,
        w1=v["L1_ffn_W1"].transpose(1, 0, 2), b1=v["L1_ffn_b1"].reshape(E, F // P, P).transpose(2, 0, 1),
        w2=v["L1_ffn_W2"].reshape(E, F // P, P, D).transpose(2, 0, 1, 3), b2=v["L1_ffn_b2"])
    arrays = {f"in_{k}": np.ascontiguousarray(a) for k, a in arrays.items()}

    nc = _bacc.Bacc("TRN2", target_bir_lowering=False, num_devices=1)
    io = {k[3:]: nc.dram_tensor(k, a.shape, mybir.dt.from_np(a.dtype), kind="ExternalInput").ap()
          for k, a in arrays.items()}
    out = nc.dram_tensor("out", (TILES * P, D), F32, kind="ExternalOutput").ap()
    build(nc, io, out)
    r = _run(nc, [arrays], core_ids=[0])
    return r.results[0]["out"].reshape(B, N, D)
```

```python
from contextlib import ExitStack

import numpy as np

import concourse.bass as bass
from concourse import mybir

F32 = mybir.dt.float32
BF16 = mybir.dt.bfloat16
I32 = mybir.dt.int32
ALU = mybir.AluOpType
ACT = mybir.ActivationFunctionType
AX = mybir.AxisListType

P = 128
B, N, D = 4, 1024, 128
TILES = B * N // P
WIN = N // P
EPS = 1e-5

H0, DH = 16, 64
PAIRS = H0 // 2
SEG = 16
SPW = P // SEG
NSEG = N // SEG
KEYS = 2 * P + NSEG
GLOB = (2 * P, 0)
LOCAL = (0, NSEG)
RING = 3


class Tally:

    def __init__(self, eng, sem, start=0):
        self.eng, self.sem, self.start, self.n = eng, sem, start, 0

    def done(self, ins):
        ins.then_inc(self.sem, 1)
        self.n += 1
        return self.n

    def wait(self, n=None):
        self.eng.wait_ge(self.sem, self.start + (self.n if n is None else n))


def is_first(n):
    return isinstance(n, int) and n == 0


def rsqrt(own, v, y, t):
    dve = own.eng
    own.wait(own.done(dve.tensor_scalar(t.bitcast(I32), v.bitcast(I32), 1, None, ALU.logical_shift_right)))
    own.wait(own.done(dve.tensor_scalar(y.bitcast(I32), t.bitcast(I32), -1.0, 1597463007.0, ALU.mult, ALU.add)))
    for k in range(3):
        own.wait(own.done(dve.tensor_tensor(t, y, y, ALU.mult)))
        own.wait(own.done(dve.scalar_tensor_tensor(t, t, -0.5, v, ALU.mult, ALU.mult)))
        last = dve.scalar_tensor_tensor(y, t, 1.5, y, ALU.add, ALU.mult)
        if k < 2:
            own.wait(own.done(last))
    return last


def layer0_attention(nc, ctx, io, res):

    def sb(name, shape, dt=F32):
        return ctx.enter_context(nc.sbuf_tensor(name, shape, dt))

    def sem(name):
        return ctx.enter_context(nc.semaphore(name))

    x_sb = sb("x_sb", [P, TILES, D])
    xT = sb("xT", [P, 2, P])
    wqs = sb("wqs", [P, H0, P])
    wkv = sb("wkv", [P, H0 * DH])
    wout = sb("wout", [P, PAIRS, D])
    wproj = sb("wproj", [P, DH])
    lg, lb = sb("lg", [P, DH]), sb("lb", [P, DH])
    gg, gb = sb("gg", [P, DH]), sb("gb", [P, DH])
    csT = sb("csT", [P, N])
    cosn = sb("cosn", [P, WIN, DH])
    sinn = sb("sinn", [P, WIN, DH])
    masks = sb("masks", [P, WIN, 2, KEYS], BF16)
    identb = sb("identb", [P, P], BF16)
    ident = sb("ident", [P, P])
    segsel = sb("segsel", [P, SPW])
    headsel = sb("headsel", [P, 4])
    qT = sb("qT", [P, 2, H0, P])
    KT = sb("KT", [P, H0, RING * P])
    KG = sb("KG", [P, H0, NSEG])
    V = sb("V", [P, 2, H0 * DH])
    gV = sb("gV", [P, 2, PAIRS, P])
    rc, rs = sb("rc", [P, H0, DH]), sb("rs_", [P, H0, DH])
    kvr = sb("kvr", [P, H0, DH])
    wl = sb("wl", [P, H0, DH])
    cen = sb("cen", [P, H0, DH])
    vn = sb("vn", [P, H0, DH])
    vst = sb("vst", [P, H0, DH])
    st = sb("st", [P, H0, 6])
    sm = sb("sm", [P, 16, H0])
    logit = sb("logit", [P, H0])
    e0, e1, pk = (sb(n, [H0, P]) for n in ("e0", "e1", "pk"))
    smax, ssum, srec = (sb(n, [H0, SPW]) for n in ("smax", "ssum", "srec"))
    wg = sb("wg", [P, H0, SPW])
    gm = sb("gm", [P, 4, DH])
    g0, g1, g2 = sb("g0", [P, DH]), sb("g1", [P, DH]), sb("g2", [P, DH])
    gk = sb("gk", [P, 2, DH])
    gst, gmv, gsm = sb("gst", [P, 6]), sb("gmv", [P, 2]), sb("gsm", [P, 8])
    spare = sb("spare", [P, 9])
    pr = sb("pr", [P, 2, 2 * KEYS])
    nmax = sb("nmax", [P, 2, 2])
    psums = sb("psums", [P, 2, 2])
    prec = sb("prec", [P, 2, 2])
    prT = sb("prT", [P, 2, 5 * P])
    oT = sb("oT", [P, PAIRS, P])

    ps_s = [ctx.enter_context(nc.psum_tensor(f"ps_s{k}", [P, 2, 512], F32)) for k in range(2)]
    ps_xg = ctx.enter_context(nc.psum_tensor("ps_xg", [P, 1024], F32))
    ps_k = ps_xg[:, 5 * P:7 * P]
    ps_o = ctx.enter_context(nc.psum_tensor("ps_o", [P, 512], F32))
    ps_r = ctx.enter_context(nc.psum_tensor("ps_r", [P, 512], F32))
    gk_dram = nc.dram_tensor("gk_dram", [H0, NSEG, DH], F32, kind="Internal").ap()

    consts = sem("consts")
    zeroed = sem("zeroed")
    x_landed = [sem(f"x_landed{k}") for k in range(2)]
    scores_ready = sem("scores_ready")
    max_done = sem("max_done")
    exp_done = sem("exp_done")
    recip_done = sem("recip_done")
    norm_done = sem("norm_done")
    turned = sem("turned")
    p_copied = sem("p_copied")
    pv_done = sem("pv_done")
    o_copied = sem("o_copied")
    proj_ready = sem("proj_ready")
    res_done = sem("res_done")
    kv_ready = sem("kv_ready")
    rot_products = sem("rot_products")
    kvr_done = sem("kvr_done")
    q_ready = sem("q_ready")
    q_done = sem("q_done")
    wl_done = sem("wl_done")
    cen_done = sem("cen_done")
    vn_done = sem("vn_done")
    vst_done = sem("vst_done")
    v_copied = sem("v_copied")
    keys_ready = sem("keys_ready")
    kt_copied = sem("kt_copied")
    logit_done = sem("logit_done")
    logit_turned = sem("logit_turned")
    e0_done = sem("e0_done")
    e1_done = sem("e1_done")
    pk_done = sem("pk_done")
    pk_turned = sem("pk_turned")
    wg_done = sem("wg_done")
    sums_ready = sem("sums_ready")
    gm_done = sem("gm_done")
    gk_done = sem("gk_done")
    gk_turned = sem("gk_turned")
    kg_copied = sem("kg_copied")
    gk_zeroed = sem("gk_zeroed")
    gk_stored = sem("gk_stored")
    gv_landed = [sem(f"gv_landed{k}") for k in range(2)]
    dve_step = sem("dve_step")
    DVE_STEPS = 35

    loads = [(x_sb[:, :, :], io["x"].rearrange("(t p) d -> p t d", p=P)),
             (wqs[:, :, :], io["wqs"]), (wkv[:, :], io["wkv"]),
             (wout[:, :, :], io["wout"].rearrange("(k p) d -> p k d", p=P)),
             (wproj[:, :], io["wproj"].rearrange("d a -> a d").to_broadcast([P, DH])),
             (lg[:, :], io["lg"].to_broadcast([P, DH])), (lb[:, :], io["lb"].to_broadcast([P, DH])),
             (gg[:, :], io["gg"].to_broadcast([P, DH])), (gb[:, :], io["gb"].to_broadcast([P, DH])),
             (csT[:, :], io["csT"]), (cosn[:, :, :], io["cosn"]), (sinn[:, :, :], io["sinn"]),
             (masks[:, :, :, :], io["masks"]), (identb[:, :], io["identb"]), (ident[:, :], io["ident"]),
             (segsel[:, :], io["segsel"]), (headsel[:, :], io["headsel"])]
    ALL_CONSTS = 16 * len(loads)

    def row(small, k):
        return small[:, k, :]

    def before(t, p, k):
        return (t, p - k) if p >= k else (t - 1, p - k + PAIRS)

    block = ctx.enter_context(nc.Block())

    @block.sync
    def _(sp):
        def load_x(n, par):
            sp.dma_start(xT[:, par, :], io["xT"][bass.ds(n, 1), :, :].rearrange("a p t -> (a p) t")
                         ).then_inc(x_landed[par], 16)

        def store_segments(n, w):
            sp.wait_ge(gk_done, n + 1)
            sp.dma_start(gk_dram[:, bass.ds(w * SPW, SPW), :].rearrange("h s d -> h s d"),
                         gk[:, 0, :]).then_inc(gk_stored, 16)

        def load_segments(n, np_):
            sp.wait_ge(gk_stored, 16 * (n + 1))
            for a in range(2):
                sp.dma_start(gV[a * NSEG:(a + 1) * NSEG, np_, :, a * DH:(a + 1) * DH],
                             gk_dram.rearrange("(k a) s d -> a s k d", a=2)[a]).then_inc(gv_landed[np_], 16)

        load_x(0, 0)
        for dst, src in loads:
            sp.dma_start(dst, src).then_inc(consts, 16)
        load_x(1, 1)
        sp.wait_ge(zeroed, 5)
        sp.dma_start(gk_dram.rearrange("h s d -> (h s) d").rearrange("(a p) d -> p a d", p=P),
                     gV[:, 0, :, 0:DH]).then_inc(gk_zeroed, 16)
        sp.wait_ge(gk_zeroed, 16)
        store_segments(0, 0)
        load_segments(0, 0)

        def two_tiles(i):
            for par in range(2):
                t = i * 2 + par
                n = t + 1
                sp.wait_ge(q_done, 4 * (t + 1))
                sp.wait_ge(consts, ALL_CONSTS)
                load_x((t + 2) % TILES, par)
                store_segments(n, n % WIN)
                load_segments(n, 1 - par)

        two_tiles(0)
        with sp.Fori(1, TILES // 2) as i:
            two_tiles(i)
        for par in range(2):
            sp.wait_ge(x_landed[par], 16 * (TILES // 2 + 1))
        sp.wait_ge(gv_landed[0], 32 * (TILES // 2 + 1))
        sp.wait_ge(gv_landed[1], 32 * (TILES // 2))

    @block.tensor
    def _(pe):
        def kv(n, np_, half, turns=0):
            if half == 0:
                pe.wait_ge(x_landed[np_], 16 * (turns + 1))
                if not is_first(n):
                    pe.wait_ge(kg_copied, n)
            else:
                pe.wait_ge(rot_products, 2 * n + 1)
            pe.matmul(ps_r[:, :], xT[:, np_, :], wkv[:, half * 512:half * 512 + 512],
                      start=True, stop=True).then_inc(kv_ready, 1)

        def q(n, np_, quad):
            if quad == 0:
                pe.wait_ge(rot_products, 2 * n + 2)
            else:
                pe.wait_ge(q_done, 4 * n + quad)
            for k in range(4):
                mm = pe.matmul(ps_r[:, k * P:(k + 1) * P], wqs[:, 4 * quad + k, :], xT[:, np_, :],
                               start=True, stop=True)
            mm.then_inc(q_ready, 1)

        def logit_turn(n):
            pe.wait_ge(logit_done, n + 1)
            if not is_first(n) and not (isinstance(n, int) and n == 1):
                pe.wait_ge(res_done, n - 1)
            else:
                pe.wait_ge(q_done, 4 * n + 4)
            pe.transpose(ps_r[0:H0, 0:P], logit[:, :], ident[:, :]).then_inc(logit_turned, 1)

        def pk_turn(n):
            pe.wait_ge(pk_done, n + 1)
            pe.matmul(ps_r[:, 0:H0], pk[:, :], ident[0:H0, 0:H0], start=True, stop=True).then_inc(pk_turned, 1)

        def seg_sums(n):
            pe.wait_ge(wg_done, n + 1)
            for j in range(4):
                mm = pe.matmul(ps_r[32 * j:32 * j + 32, 0:4 * DH],
                               wg[:, 4 * j:4 * j + 4, :].rearrange("p h s -> p (h s)"),
                               kvr[:, 4 * j:4 * j + 4, :].rearrange("p h d -> p (h d)"), start=True, stop=True)
            mm.then_inc(sums_ready, 1)

        def keys_turn(n, j):
            if j % 2 == 0:
                pe.wait_ge(vst_done, 2 * n + j // 2 + 1)
            if j or not is_first(n):
                pe.wait_ge(kt_copied, 16 * n + 4 * j)
            for k in range(2):
                h = 4 * j + 2 * k
                mm = pe.transpose(ps_k[:, k * P:(k + 1) * P], vst[:, h:h + 2, :].rearrange("p h d -> p (h d)"),
                                  ident[:, :])
            mm.then_inc(keys_ready, 1)

        def seg_turn(n):
            pe.wait_ge(gk_done, n + 1)
            pe.transpose(ps_r[:, 0:P], gk[:, :, :].rearrange("p a d -> p (a d)"), ident[:, :]).then_inc(gk_turned, 1)

        def out_proj(t):
            if not (isinstance(t, int) and t == TILES - 1):
                pe.wait_ge(q_done, 4 * t + 12)
            pe.wait_ge(o_copied, 4 * t + 4)
            for k in range(PAIRS):
                mm = pe.matmul(ps_r[:, 0:D], oT[:, k, :], wout[:, k, :], start=(k == 0), stop=(k == PAIRS - 1))
            mm.then_inc(proj_ready, 1)

        def scores(t, par, p, slots, w):
            if p % 2 == 0:
                pe.wait_ge(kt_copied, 16 * t + 4 + 2 * p)
            pe.wait_ge(q_done, 4 * (t + 1))
            if p >= 2 or not is_first(t):
                pe.wait_ge(exp_done, PAIRS * t + p - 1)
            bank = ps_s[p % 2]
            for a in range(2):
                h = 2 * p + a
                pe.matmul(bank[:, a, 0:KEYS], identb[:, :], masks[:, bass.ds(w, 1), a, :].rearrange("p a k -> p (a k)"),
                          start=True, stop=False)
                for k, slot in enumerate(slots):
                    at = LOCAL[a] + k * P
                    pe.matmul(bank[:, a, at:at + P], qT[:, par, h, :], KT[:, h, bass.ds(slot * P, P)],
                              start=False, stop=False)

        def seg_scores(t, par, p):
            bank = ps_s[p % 2]
            if p == 0:
                pe.wait_ge(kg_copied, t + 1)
            for a in range(2):
                h = 2 * p + a
                mm = pe.matmul(bank[:, a, GLOB[a]:GLOB[a] + NSEG], qT[:, par, h, :], KG[:, h, :], start=False, stop=True)
            mm.then_inc(scores_ready, 1)

        def turn(t, p, keys=None):
            if p or not is_first(t):
                pe.wait_ge(p_copied, PAIRS * t + p)
            if p in (0, 1, 6, 7):
                pe.wait_ge(kt_copied, 16 * t + {0: 12, 1: 16, 6: 20, 7: 24}[p])
            if keys is not None:
                keys_turn(*keys)
            pe.wait_ge(norm_done, PAIRS * t + p + 1)
            r = pr[:, p % 2, :]
            for k, at in enumerate((0, P, 3 * P, 4 * P, 2 * P)):
                mm = pe.transpose(ps_xg[:, k * P:(k + 1) * P], r[:, at:at + P], ident[:, :])
            mm.then_inc(turned, 1)

        def values(t, par, p, turns):
            pe.wait_ge(p_copied, PAIRS * t + p + 1)
            if p == 0:
                pe.wait_ge(gv_landed[par], 32 * (turns + 1))
            if p % 4 == 0:
                pe.wait_ge(v_copied, 2 * t + p // 4 + 1)
            if p % 2 == 0 and (p or not is_first(t)):
                pe.wait_ge(o_copied, 4 * t + p // 2)
            at = (p % 4) * P
            pT = prT[:, p % 2, :]
            pe.matmul(ps_o[:, at:at + P], gV[:, par, p, :], pT[:, 4 * P:5 * P], start=True, stop=False,
                      skip_group_check=True)
            for s in range(2):
                for a in range(2):
                    h = 2 * p + a
                    mm = pe.matmul(ps_o[DH * a:DH * a + DH, at:at + P], V[:, (par + 1 + s) % 2, h * DH:(h + 1) * DH],
                                   pT[:, (2 * a + s) * P:(2 * a + s + 1) * P], start=False, stop=(s == 1),
                                   skip_group_check=True)
            mm.then_inc(pv_done, 1)

        pe.wait_ge(consts, ALL_CONSTS)
        kv(0, 0, 0)
        kv(0, 0, 1)
        for quad in range(4):
            q(0, 0, quad)
        logit_turn(0)
        pk_turn(0)
        seg_sums(0)
        keys_turn(0, 0)
        keys_turn(0, 1)
        seg_turn(0)
        pe.wait_ge(zeroed, 6)

        def two_tiles(i):
            for par in range(2):
                t = i * 2 + par
                n, np_ = t + 1, 1 - par
                slots = (t + RING - 1) % RING, t % RING
                for p in range(PAIRS):
                    scores(t, par, p, slots, t % WIN)
                    if p:
                        seg_scores(t, par, p)
                    if p == 1:
                        kv(n, np_, 1)
                    elif p == 2:
                        q(n, np_, 1)
                    elif p == 3:
                        q(n, np_, 3)
                    elif p == 6:
                        pk_turn(n)
                    if p >= 2:
                        values(t, par, p - 2, i)
                    elif not is_first(t):
                        values(t - 1, np_, p - 2 + PAIRS, None)
                    if p == 0 and not is_first(t):
                        seg_turn(t)
                    if p == 0 and is_first(t):
                        keys_turn(t, 2)
                    elif p == 0:
                        turn(t - 1, PAIRS - 1, (t, 2))
                    else:
                        turn(t, p - 1, {1: (t, 3), 6: (n, 0), 7: (n, 1)}.get(p))
                    if p == 0:
                        seg_scores(t, par, p)
                    if p == 0:
                        kv(n, np_, 0, i + par)
                    elif p == 1:
                        q(n, np_, 0)
                    elif p == 2:
                        q(n, np_, 2)
                    elif p == 3 and not is_first(t):
                        out_proj(t - 1)
                    elif p == 4:
                        logit_turn(n)
                    elif p == 6:
                        seg_sums(n)

        two_tiles(0)
        with pe.Fori(1, TILES // 2) as i:
            two_tiles(i)
        seg_turn(TILES)
        last = TILES - 1
        values(last, 1, PAIRS - 2, None)
        turn(last, PAIRS - 1)
        values(last, 1, PAIRS - 1, None)
        pe.wait_ge(kg_copied, TILES + 1)
        out_proj(last)

    @block.scalar
    def _(act):
        def exps(t, p):
            act.wait_ge(max_done, PAIRS * t + p + 1)
            if p >= 2 or not is_first(t):
                act.wait_ge(turned, PAIRS * t + p - 1)
            for a in range(2):
                e = act.activation(pr[:, p % 2, a * KEYS:(a + 1) * KEYS], ps_s[p % 2][:, a, 0:KEYS], ACT.Exp,
                                   bias=nmax[:, p % 2, a:a + 1], scale=1.0, accum_out=psums[:, p % 2, a:a + 1])
            e.then_inc(exp_done, 1)

        def copy_p(t, p):
            act.wait_ge(turned, PAIRS * t + p + 1)
            if p >= 2 or not is_first(t):
                act.wait_ge(pv_done, PAIRS * t + p - 1)
            act.activation(prT[:, p % 2, :], ps_xg[:, 0:5 * P], ACT.Copy).then_inc(p_copied, 1)

        def copy_o(t, j):
            act.wait_ge(pv_done, PAIRS * t + 2 * j + 2)
            if j == 0 and not is_first(t):
                act.wait_ge(res_done, t)
            at = (2 * j % 4) * P
            act.activation(oT[:, 2 * j:2 * j + 2, :].rearrange("p k t -> p (k t)"), ps_o[:, at:at + 2 * P],
                           ACT.Copy).then_inc(o_copied, 1)

        def seg_exp(n):
            act.wait_ge(e0_done, n + 1)
            act.activation(e1[:, :], e0[:, :], ACT.Exp).then_inc(e1_done, 1)

        def copy_keys(n, slot, j):
            act.wait_ge(keys_ready, 4 * n + j + 1)
            for a in range(2):
                for to in range(2):
                    act.activation(KT[DH * to:DH * to + DH, 4 * j + a:4 * j + 4:2, bass.ds(slot * P, P)],
                                   ps_k[DH * a:DH * a + DH, :].rearrange("p (k t) -> p k t", k=2), ACT.Copy
                                   ).then_inc(kt_copied, 1)

        act.wait_ge(zeroed, 6)
        seg_exp(0)
        copy_keys(0, 0, 0)
        copy_keys(0, 0, 1)

        def two_tiles(i):
            for par in range(2):
                t = i * 2 + par
                n = t + 1
                for p in range(PAIRS):
                    if p == 5:
                        seg_exp(n)
                    exps(t, p)
                    if p >= 1:
                        copy_p(t, p - 1)
                    elif not is_first(t):
                        copy_p(t - 1, PAIRS - 1)
                    if p == 1 and not is_first(t):
                        copy_o(t - 1, 3)
                    elif p in (3, 5, 7):
                        copy_o(t, p // 2 - 1)
                    if p < 2:
                        copy_keys(t, t % RING, 2 + p)
                    elif p >= 6:
                        copy_keys(n, n % RING, p - 6)

        two_tiles(0)
        with act.Fori(1, TILES // 2) as i:
            two_tiles(i)
        copy_p(TILES - 1, PAIRS - 1)
        copy_o(TILES - 1, 3)

    @block.gpsimd
    def _(pool):
        for n, fill in enumerate((KT[:, :, :], KG[:, :, :], V[:, :, :], gV[:, :, :, :], st[:, :, :])):
            pool.memset(fill, 0.0).then_inc(zeroed, 1)
        pool.wait_ge(zeroed, 5)
        pool.memset(spare[:, :], 0.0).then_inc(zeroed, 1)

        def carry_wait(k):
            pool.tensor_tensor(spare[:, k:k + 1], spare[:, 8:9], spare[:, 8:9], ALU.mult)

        def heads(half):
            return slice(8 * half, 8 * half + 8)

        def add_halves(n, half):
            pool.wait_ge(rot_products, 2 * n + half + 1)
            if half == 0 and not is_first(n):
                pool.wait_ge(gm_done, n)
            hs = heads(half)
            pool.tensor_tensor(kvr[:, hs, :], rc[:, hs, :], rs[:, hs, :], ALU.add).then_inc(kvr_done, 1)

        def weigh(n):
            pool.wait_ge(kvr_done, 2 * n + 2)
            if not is_first(n):
                pool.wait_ge(logit_done, n)
            pool.tensor_tensor(wl[:, :, :], kvr[:, :, :], wproj[:, :].unsqueeze(1).to_broadcast([P, H0, DH]),
                               ALU.mult).then_inc(wl_done, 1)

        def gain(n, half):
            pool.wait_ge(cen_done, 2 * n + half + 1)
            if not is_first(n):
                pool.wait_ge(vst_done, 2 * n)
            hs = heads(half)
            pool.tensor_tensor(vn[:, hs, :], cen[:, hs, :], lg[:, :].unsqueeze(1).to_broadcast([P, 8, DH]),
                               ALU.mult).then_inc(vn_done, 1)

        def norm(t, p):
            pool.wait_ge(recip_done, PAIRS * t + p + 1)
            carry_wait(p % 2)
            for a in range(2):
                r = pr[:, p % 2, a * KEYS:(a + 1) * KEYS]
                s = pool.tensor_scalar(r, r, prec[:, p % 2, a:a + 1], 1.0, ALU.mult, ALU.mult)
            s.then_inc(norm_done, 1)

        def keep_values(n, slot, half):
            pool.wait_ge(vst_done, 2 * n + half + 1)
            if not is_first(n):
                pool.wait_ge(pv_done, PAIRS * (n - 1) + 4 * half + 4)
            carry_wait(2)
            pool.tensor_scalar(V[:, slot, half * 512:half * 512 + 512],
                               vst[:, heads(half), :].rearrange("p h d -> p (h d)"), 1.0, 1.0,
                               ALU.mult, ALU.mult).then_inc(v_copied, 1)

        pool.wait_ge(consts, ALL_CONSTS)
        add_halves(0, 0)
        add_halves(0, 1)
        weigh(0)
        gain(0, 0)
        gain(0, 1)
        pool.wait_ge(zeroed, 6)
        keep_values(0, 0, 0)

        def two_tiles(i):
            for par in range(2):
                t = i * 2 + par
                n = t + 1
                for p in range(PAIRS):
                    if p == 1:
                        add_halves(n, 0)
                    elif p == 3:
                        keep_values(t, par, 1)
                    elif p == 5:
                        gain(n, 0)
                    norm(t, p)
                    if p == 1:
                        add_halves(n, 1)
                    elif p == 2:
                        weigh(n)
                    elif p == 5:
                        gain(n, 1)
                    elif p == 6:
                        keep_values(n, 1 - par, 0)

        two_tiles(0)
        with pool.Fori(1, TILES // 2) as i:
            two_tiles(i)

    @block.vector
    def _(dve):
        def heads(half):
            return slice(8 * half, 8 * half + 8)

        def rotate(n, w, half):
            dve.wait_ge(kv_ready, 2 * n + half + 1)
            if not is_first(n):
                dve.wait_ge(kvr_done, 2 * n)
            hs = heads(half)
            r = ps_r[:, :].rearrange("p (h d) -> p h d", h=8)
            c = cosn[:, bass.ds(w, 1), :].to_broadcast([P, 8, DH])
            h = DH // 2
            s0 = sinn[:, bass.ds(w, 1), 0:h].to_broadcast([P, 8, h])
            s1 = sinn[:, bass.ds(w, 1), h:DH].to_broadcast([P, 8, h])
            dve.tensor_tensor(rc[:, hs, :], r, c, ALU.mult)
            dve.tensor_tensor(rs[:, hs, 0:h], r[:, :, h:DH], s0, ALU.mult)
            dve.tensor_tensor(rs[:, hs, h:DH], r[:, :, 0:h], s1, ALU.mult).then_inc(rot_products, 1)

        def q_mult(n, np_, w, quad):
            dve.wait_ge(q_ready, 4 * n + quad + 1)
            dve.tensor_tensor(qT[:, np_, 4 * quad:4 * quad + 4, :], ps_r[:, :].rearrange("p (h t) -> p h t", h=4),
                              csT[:, bass.ds(w * P, P)].unsqueeze(1).to_broadcast([P, 4, P]),
                              ALU.mult).then_inc(q_done, 1)

        def stats(n, half):
            dve.wait_ge(kvr_done, 2 * n + half + 1)
            for h in range(8 * half, 8 * half + 8):
                last = dve.bn_stats(st[:, h, :], kvr[:, h, :])
            return last

        def variance(n, own, mark):
            own.wait(mark)
            dve.tensor_tensor(row(sm, 0), st[:, :, 1], st[:, :, 4], ALU.add)
            dve.tensor_tensor(row(sm, 1), st[:, :, 1], st[:, :, 4], ALU.subtract)
            m = own.done(dve.tensor_tensor(row(sm, 3), st[:, :, 2], st[:, :, 5], ALU.add))
            own.wait(m)
            dve.tensor_scalar(row(sm, 2), row(sm, 0), 0.5, None, ALU.mult)
            dve.tensor_scalar(row(sm, 8), row(sm, 3), 1.0 / DH, EPS, ALU.mult, ALU.add)
            m = own.done(dve.scalar_tensor_tensor(row(sm, 4), row(sm, 1), 0.25, row(sm, 1), ALU.mult, ALU.mult))
            own.wait(m)
            own.wait(own.done(dve.tensor_tensor(row(sm, 5), row(sm, 4), row(sm, 8), ALU.add)))
            return own.done(rsqrt(own, row(sm, 5), row(sm, 7), row(sm, 6)))

        def normalise(n, half, own, mark):
            own.wait(mark)
            if not is_first(n):
                dve.wait_ge(vn_done, 2 * n)
            for h in range(8 * half, 8 * half + 8):
                c = dve.tensor_scalar(cen[:, h, :], kvr[:, h, :], sm[:, 2, h:h + 1], sm[:, 7, h:h + 1],
                                      ALU.subtract, ALU.mult)
            c.then_inc(cen_done, 1)

        def add_bias(n, half):
            dve.wait_ge(vn_done, 2 * n + half + 1)
            if not is_first(n):
                dve.wait_ge(v_copied, 2 * n)
                dve.wait_ge(keys_ready, 4 * n)
            hs = heads(half)
            dve.tensor_tensor(vst[:, hs, :], vn[:, hs, :], lb[:, :].unsqueeze(1).to_broadcast([P, 8, DH]),
                              ALU.add).then_inc(vst_done, 1)

        def logits(n):
            dve.wait_ge(wl_done, n + 1)
            dve.tensor_reduce(logit[:, :], wl[:, :, :], AX.X, ALU.add).then_inc(logit_done, 1)

        def seg_shift(n, own):
            dve.wait_ge(logit_turned, n + 1)
            r = ps_r[0:H0, 0:P].rearrange("h (g s) -> h g s", s=SEG)
            own.wait(own.done(dve.tensor_reduce(smax[:, :], r, AX.X, ALU.max)))
            dve.tensor_tensor(e0[:, :].rearrange("h (g s) -> h g s", s=SEG), r,
                              smax[:, :].unsqueeze(2).to_broadcast([H0, SPW, SEG]), ALU.subtract).then_inc(e0_done, 1)

        def seg_probs(n, own):
            dve.wait_ge(e1_done, n + 1)
            e = e1[:, :].rearrange("h (g s) -> h g s", s=SEG)
            own.wait(own.done(dve.tensor_reduce(ssum[:, :], e, AX.X, ALU.add)))
            own.wait(own.done(dve.reciprocal(srec[:, :], ssum[:, :])))
            dve.tensor_tensor(pk[:, :].rearrange("h (g s) -> h g s", s=SEG), e,
                              srec[:, :].unsqueeze(2).to_broadcast([H0, SPW, SEG]), ALU.mult).then_inc(pk_done, 1)

        def seg_weights(n):
            dve.wait_ge(pk_turned, n + 1)
            dve.tensor_tensor(wg[:, :, :], ps_r[:, 0:H0].unsqueeze(2).to_broadcast([P, H0, SPW]),
                              segsel[:, :].unsqueeze(1).to_broadcast([P, H0, SPW]), ALU.mult).then_inc(wg_done, 1)

        def seg_variance(n, own):
            dve.wait_ge(sums_ready, n + 1)
            dve.tensor_tensor(gm[:, :, :], ps_r[:, 0:4 * DH].rearrange("p (h d) -> p h d", h=4),
                              headsel[:, :].unsqueeze(2).to_broadcast([P, 4, DH]), ALU.mult).then_inc(gm_done, 1)
            dve.wait_ge(gm_done, n + 1)
            own.wait(own.done(dve.tensor_reduce(g0[:, :], gm[:, :, :].rearrange("p h d -> p d h"), AX.X, ALU.add)))
            own.wait(own.done(dve.bn_stats(gst[:, :], g0[:, :])))
            dve.memset(gsm[:, 7:8], 0.0)
            own.wait(own.done(dve.bn_aggr(gmv[:, :], gst[:, :])))
            own.done(dve.tensor_scalar(gsm[:, 0:1], gmv[:, 1:2], EPS, None, ALU.add))

        def seg_scale(n, own):
            own.wait()
            return own.done(rsqrt(own, gsm[:, 0:1], gsm[:, 1:2], gsm[:, 2:3]))

        def seg_keys(n, own, mark):
            own.wait(mark)
            own.wait(own.done(dve.tensor_scalar(g1[:, :], g0[:, :], gmv[:, 0:1], gsm[:, 1:2], ALU.subtract, ALU.mult)))
            own.wait(own.done(dve.tensor_tensor(g2[:, :], g1[:, :], gg[:, :], ALU.mult)))
            if not is_first(n):
                dve.wait_ge(gk_stored, 16 * n)
                if not (isinstance(n, int) and n == 1):
                    dve.wait_ge(pv_done, PAIRS * (n - 1))
            dve.tensor_tensor(gk[:, :, :], g2[:, :].unsqueeze(1).to_broadcast([P, 2, DH]),
                              gb[:, :].unsqueeze(1).to_broadcast([P, 2, DH]), ALU.add).then_inc(gk_done, 1)

        def copy_segments(n, w):
            dve.wait_ge(gk_turned, n + 1)
            if not is_first(n):
                dve.wait_ge(scores_ready, PAIRS * n)
            r = ps_r[:, 0:P].rearrange("p (k a s) -> p k a s", a=2, s=SPW)
            for a in range(2):
                c = dve.tensor_copy(KG[:, a:H0:2, bass.ds(w * SPW, SPW)], r[:, :, a, :])
            c.then_inc(kg_copied, 1)

        def maxima(t, p):
            dve.wait_ge(scores_ready, PAIRS * t + p + 1)
            dve.tensor_reduce(nmax[:, p % 2, :], ps_s[p % 2][:, :, 0:KEYS], AX.X, ALU.max,
                              negate=True).then_inc(max_done, 1)

        def recips(t, p):
            dve.wait_ge(exp_done, PAIRS * t + p + 1)
            dve.reciprocal(prec[:, p % 2, :], psums[:, p % 2, :]).then_inc(recip_done, 1)

        def residual(t):
            dve.wait_ge(proj_ready, t + 1)
            dve.tensor_tensor(res[:, bass.ds(t, 1), :].rearrange("p a d -> p (a d)"), ps_r[:, 0:D],
                              x_sb[:, bass.ds(t, 1), :].rearrange("p a d -> p (a d)"), ALU.add).then_inc(res_done, 1)

        dve.wait_ge(consts, ALL_CONSTS)
        dve.wait_ge(zeroed, 6)
        own = Tally(dve, dve_step, 0)
        rotate(0, 0, 0)
        rotate(0, 0, 1)
        for quad in range(4):
            q_mult(0, 0, 0, quad)
        stats(0, 0)
        mark = variance(0, own, own.done(stats(0, 1)))
        logits(0)
        seg_shift(0, own)
        normalise(0, 0, own, mark)
        normalise(0, 1, own, mark)
        seg_probs(0, own)
        seg_weights(0)
        seg_variance(0, own)
        mark = seg_scale(0, own)
        seg_keys(0, own, mark)
        add_bias(0, 0)
        add_bias(0, 1)
        assert own.n == DVE_STEPS, own.n
        copy_segments(0, 0)

        def two_tiles(i):
            for par in range(2):
                t = i * 2 + par
                n, np_ = t + 1, 1 - par
                w = n % WIN
                own = Tally(dve, dve_step, n * DVE_STEPS)
                for p in range(PAIRS):
                    if p == 0 and not is_first(t):
                        copy_segments(t, t % WIN)
                    elif p == 4 and not is_first(t):
                        residual(t - 1)
                    elif p == 5:
                        seg_shift(n, own)
                    elif p == 7:
                        seg_variance(n, own)
                    maxima(t, p)
                    if p == 1:
                        rotate(n, w, 1)
                    elif p == 2:
                        q_mult(n, np_, w, 1)
                    elif p == 3:
                        q_mult(n, np_, w, 3)
                    elif p == 4:
                        logits(n)
                    elif p == 5:
                        seg_probs(n, own)
                    elif p == 6:
                        seg_weights(n)
                        add_bias(n, 0)
                    elif p == 7:
                        scale_mark = seg_scale(n, own)
                    recips(t, p)
                    if p == 0:
                        rotate(n, w, 0)
                    elif p == 1:
                        q_mult(n, np_, w, 0)
                        stats(n, 0)
                    elif p == 2:
                        q_mult(n, np_, w, 2)
                        mark = own.done(stats(n, 1))
                    elif p == 3:
                        mark = variance(n, own, mark)
                    elif p in (4, 5):
                        normalise(n, p - 4, own, mark)
                    elif p == 6:
                        add_bias(n, 1)
                    elif p == 7:
                        seg_keys(n, own, scale_mark)
                assert own.n == DVE_STEPS, own.n

        two_tiles(0)
        with dve.Fori(1, TILES // 2) as i:
            two_tiles(i)
        copy_segments(TILES, 0)
        residual(TILES - 1)

GROUPS = TILES // 4
GT = 4
GC = GT * P
H1, D1 = 16, 8
PARTS = 3
E, F = 8, 512


def layernorm(own, src, dst, st, mv, ve, y, t, n=GT):
    dve = own.eng
    for k in range(n):
        last = dve.bn_stats(st[:, k, :], src[:, k, :])
    own.wait(own.done(last))
    dve.memset(t[:, 0:1], 0.0)
    for k in range(n):
        last = dve.bn_aggr(mv[:, k, :], st[:, k, :])
    own.wait(own.done(last))
    own.wait(own.done(dve.tensor_scalar(ve, mv[:, :, 1], EPS, None, ALU.add)))
    own.wait(own.done(rsqrt(own, ve, y, t)))
    for k in range(n):
        last = dve.tensor_scalar(dst(k), src[:, k, :], mv[:, k, 0:1], y[:, k:k + 1], ALU.subtract, ALU.mult)
    return last


def between_attentions(nc, ctx, io, res, x2, v1, parts_dram):

    def sb(name, shape, dt=F32):
        return ctx.enter_context(nc.sbuf_tensor(name, shape, dt))

    def sem(name):
        return ctx.enter_context(nc.semaphore(name))

    bout = sb("bout", [P, D])
    bv = sb("bv", [P, D])
    bqk = sb("bqk", [P, 4])
    wqk = sb("wqk", [P, 4, D])
    wv = sb("wv", [P, D])
    cos1, sin1 = sb("cos1", [P, 2, N]), sb("sin1", [P, 2, N])
    ident = sb("ident_b", [P, P])
    ones = sb("ones_b", [P, P])
    w = sb("w", [P, D])
    tern = sb("tern", [P, D])
    ternT = sb("ternT", [P, D])
    ws = sb("ws", [P, 8])
    xa = sb("xa", [P, GT, D])
    xb = sb("xb", [P, GT, D])
    x1 = sb("x1", [P, GT, D])
    x1T = sb("x1T", [P, GC])
    xf = sb("xf", [P, GT, D])
    x2T = sb("x2T", [P, GC])
    st = sb("stb", [P, GT, 6])
    mv = sb("mvb", [P, GT, 2])
    sv = sb("svb", [P, 3, GT])
    rot = sb("rot", [P, 2, 2, GC])
    full = sb("full", [P, 2, GC])
    rest = sb("rest", [P, 2, 2, GC])
    part = sb("part", [P, 2, PARTS, GC], BF16)
    ps = [ctx.enter_context(nc.psum_tensor(f"psb{k}", [P, 512], F32)) for k in range(8)]

    consts = sem("consts_b")
    w_step = sem("w_step")
    row_sums = sem("row_sums")
    w_sum = sem("w_sum")
    tern_done = sem("tern_done")
    tern_turned = sem("tern_turned")
    ternT_done = sem("ternT_done")
    ones_done = sem("ones_done")
    x1_done = sem("x1_done")
    x1_turned = sem("x1_turned")
    x1T_done = sem("x1T_done")
    ffn_done = sem("ffn_done")
    x2_done = sem("x2_done")
    x2_turned = sem("x2_turned")
    x2T_done = sem("x2T_done")
    qk_done = sem("qk_done")
    v_done = sem("v_done")
    v_kept = sem("v_kept")
    rot_done = sem("rot_done")
    full_done = sem("full_done")
    hi_done = sem("hi_done")
    r1_done = sem("r1_done")
    mid_done = sem("mid_done")
    r2_done = sem("r2_done")
    lo_done = sem("lo_done")
    stored = [sem(f"stored{k}") for k in range(2)]
    dve_step = sem("dve_step_b")
    STEPS = 30

    loads = [(bout[:, :], io["bout"].to_broadcast([P, D])), (bv[:, :], io["bv"].to_broadcast([P, D])),
             (bqk[:, :], io["bqk"]), (wqk[:, :, :], io["wqk"]), (wv[:, :], io["wv"]),
             (cos1[:, :, :], io["cos1"]), (sin1[:, :, :], io["sin1"]), (ident[:, :], io["ident"]),
             (w[:, :], io["w"])]
    ALL = 16 * len(loads)
    block = ctx.enter_context(nc.Block())

    @block.sync
    def _(sp):
        for dst, src in loads:
            sp.dma_start(dst, src).then_inc(consts, 16)
        def group(g):
            for k in range(2):
                sp.wait_ge(lo_done, 2 * g + k + 1)
                sp.dma_start(parts_dram[k].rearrange("j c t -> c j t")[:, :, bass.ds(g * GC, GC)],
                             part[:, k, :, :]).then_inc(stored[k], 16)

        group(0)
        with sp.Fori(1, GROUPS) as g:
            group(g)
        for k in range(2):
            sp.wait_ge(stored[k], 16 * GROUPS)

    @block.gpsimd
    def _(pool):
        pool.memset(ones[:, :], 1.0).then_inc(ones_done, 1)
        pool.memset(v1[:, :, :, :], 0.0).then_inc(ones_done, 1)
        def group(g):
            for k in range(2):
                pool.wait_ge(rot_done, 4 * g + 2 * k + 2)
                pool.wait_ge(r1_done, 2 * g + k)
                pool.tensor_tensor(full[:, k, :], rot[:, k, 0, :], rot[:, k, 1, :], ALU.add).then_inc(full_done, 1)

        group(0)
        with pool.Fori(1, GROUPS) as g:
            group(g)

    @block.scalar
    def _(act):
        def front(n):
            act.wait_ge(x1_turned, n + 1)
            act.activation(x1T[:, :], ps[0][:, :], ACT.Copy).then_inc(x1T_done, 1)

        def group(g, last=False):
            act.wait_ge(x2_turned, g + 1)
            act.activation(x2T[:, :], ps[2][:, :], ACT.Copy).then_inc(x2T_done, 1)
            if not last:
                front(g + 1)
            for src, ready, done, j in ((full, full_done, hi_done, 0), (rest, r1_done, mid_done, 1),
                                        (rest, r2_done, lo_done, 2)):
                for k in range(2):
                    act.wait_ge(ready, 2 * g + k + 1)
                    if j == 0:
                        act.wait_ge(stored[k], 16 * g)
                    s = full[:, k, :] if j == 0 else rest[:, k, j - 1, :]
                    act.activation(part[:, k, j, :], s, ACT.Copy).then_inc(done, 1)

        front(0)
        group(0)
        with act.Fori(1, GROUPS - 1) as g:
            group(g)
        group(GROUPS - 1, True)

    @block.tensor
    def _(pe):
        pe.wait_ge(ones_done, 2)
        pe.wait_ge(consts, ALL)
        pe.wait_ge(row_sums, 1)
        pe.matmul(ps[0][:, 0:1], ones[:, :], ws[:, 0:1], start=True, stop=True).then_inc(w_sum, 1)
        pe.wait_ge(tern_done, 1)
        pe.transpose(ps[1][:, 0:D], tern[:, :], ident[:, :]).then_inc(tern_turned, 1)
        pe.wait_ge(ternT_done, 1)

        def front(n):
            pe.wait_ge(x1_done, n + 1)
            for k in range(GT):
                mm = pe.transpose(ps[0][:, k * P:(k + 1) * P], x1[:, k, :], ident[:, :])
            mm.then_inc(x1_turned, 1)
            pe.wait_ge(x1T_done, n + 1)
            for k in range(GT):
                mm = pe.matmul(ps[1][:, k * P:(k + 1) * P], x1T[:, k * P:(k + 1) * P], ternT[:, :], start=True, stop=True)
            mm.then_inc(ffn_done, 1)

        def group(g, last=False):
            pe.wait_ge(x2_done, g + 1)
            for k in range(GT):
                mm = pe.transpose(ps[2][:, k * P:(k + 1) * P], xb[:, k, :], ident[:, :])
            mm.then_inc(x2_turned, 1)
            pe.wait_ge(x2T_done, g + 1)
            pe.wait_ge(rot_done, 4 * g)
            for k in range(4):
                pe.matmul(ps[4 + k][:, :], wqk[:, k, :], x2T[:, :], start=True, stop=True).then_inc(qk_done, 1)
            pe.wait_ge(v_kept, g)
            for k in range(GT):
                mm = pe.matmul(ps[3][:, k * P:(k + 1) * P], x2T[:, k * P:(k + 1) * P], wv[:, :], start=True, stop=True)
            mm.then_inc(v_done, 1)
            if not last:
                front(g + 1)

        front(0)
        group(0)
        with pe.Fori(1, GROUPS - 1) as g:
            group(g)
        group(GROUPS - 1, True)

    @block.vector
    def _(dve):
        dve.wait_ge(consts, ALL)
        dve.wait_ge(ones_done, 2)
        own = Tally(dve, w_step)
        dve.tensor_reduce(ws[:, 0:1], w[:, :], AX.X, ALU.add, apply_absolute_value=True).then_inc(row_sums, 1)
        dve.wait_ge(w_sum, 1)
        own.wait(own.done(dve.tensor_scalar(ws[:, 1:2], ps[0][:, 0:1], 1.0 / (D * D), EPS, ALU.mult, ALU.max)))
        own.wait(own.done(dve.reciprocal(ws[:, 2:3], ws[:, 1:2])))
        own.wait(own.done(dve.tensor_scalar(tern[:, :], w[:, :], ws[:, 2:3], None, ALU.mult)))
        own.wait(own.done(dve.tensor_scalar(tern[:, :], tern[:, :], 12582912.0, None, ALU.add)))
        own.wait(own.done(dve.tensor_scalar(tern[:, :], tern[:, :], -12582912.0, 1.0, ALU.add, ALU.min)))
        dve.tensor_scalar(tern[:, :], tern[:, :], -1.0, ws[:, 1:2], ALU.max, ALU.mult).then_inc(tern_done, 1)
        dve.wait_ge(tern_turned, 1)
        dve.tensor_copy(ternT[:, :], ps[1][:, 0:D]).then_inc(ternT_done, 1)

        def first_norm(n, own):
            own.wait(own.done(dve.tensor_tensor(xa[:, :, :], res[:, bass.ds(n * GT, GT), :],
                                                bout[:, :].unsqueeze(1).to_broadcast([P, GT, D]), ALU.add)))
            layernorm(own, xa, lambda k: x1[:, k, :], st, mv, sv[:, 0, :], sv[:, 1, :], sv[:, 2, :]).then_inc(x1_done, 1)

        def second_norm(n, own):
            dve.wait_ge(ffn_done, n + 1)
            dve.wait_ge(x1_done, n + 1)
            own.wait(own.done(dve.tensor_tensor(xf[:, :, :], ps[1][:, :].rearrange("p (k d) -> p k d", k=GT),
                                                x1[:, :, :], ALU.add)))
            dve.wait_ge(x2_turned, n)
            layernorm(own, xf, lambda k: xb[:, k, :], st, mv, sv[:, 0, :], sv[:, 1, :], sv[:, 2, :]).then_inc(x2_done, 1)
            assert own.n == STEPS, own.n

        def keep(n):
            dve.wait_ge(x2_done, n + 1)
            dve.tensor_copy(x2[:, bass.ds(n * GT, GT), :], xb[:, :, :])

        def group(g, last=False):
            own = Tally(dve, dve_step, (g + 1) * STEPS)
            if not last:
                first_norm(g + 1, own)
            half = bass.ds(g % 2 * GC, GC)
            for k in range(2):
                for c, table in enumerate((cos1, sin1)):
                    dve.wait_ge(qk_done, 4 * g + 2 * k + c + 1)
                    dve.wait_ge(full_done, 2 * g)
                    dve.scalar_tensor_tensor(rot[:, k, c, :], ps[4 + 2 * k + c][:, :], bqk[:, 2 * k + c:2 * k + c + 1],
                                             table[:, k, half], ALU.add, ALU.mult).then_inc(rot_done, 1)
            dve.wait_ge(v_done, g + 1)
            dve.tensor_tensor(v1[:, bass.ds(g * GT, GT), :, 0:D1],
                              ps[3][:, :].rearrange("p (k h d) -> p k h d", k=GT, h=H1),
                              bv[:, :].rearrange("p (h d) -> p h d", h=H1).unsqueeze(1).to_broadcast([P, GT, H1, D1]),
                              ALU.add).then_inc(v_kept, 1)
            if not last:
                second_norm(g + 1, own)
            for k in range(2):
                dve.wait_ge(hi_done, 2 * g + k + 1)
                dve.wait_ge(lo_done, 2 * g)
                dve.tensor_tensor(rest[:, k, 0, :], full[:, k, :], part[:, k, 0, :], ALU.subtract).then_inc(r1_done, 1)
            if not last:
                keep(g + 1)
            for k in range(2):
                dve.wait_ge(mid_done, 2 * g + k + 1)
                dve.wait_ge(r1_done, 2 * g + k + 1)
                dve.tensor_tensor(rest[:, k, 1, :], rest[:, k, 0, :], part[:, k, 1, :], ALU.subtract).then_inc(r2_done, 1)

        own = Tally(dve, dve_step)
        first_norm(0, own)
        second_norm(0, own)
        keep(0)
        group(0)
        with dve.Fori(1, GROUPS - 1) as g:
            group(g)
        group(GROUPS - 1, True)
        dve.memset(v1[:, :, :, D1:D1 + 1], 1.0).then_inc(ones_done, 1)


def layer1_attention(nc, ctx, io, v1, parts_dram, inter):

    def sb(name, shape, dt=F32):
        return ctx.enter_context(nc.sbuf_tensor(name, shape, dt))

    def sem(name):
        return ctx.enter_context(nc.semaphore(name))

    G = 4
    SPB = H1 // G
    KB = N // P
    HALF = N // 2
    STEPS = 2 * KB
    FULL = 96
    CHUNKS = [5] * 8 + [4] * 6 + [0, 0]
    TURN_M = {5: 0, 8: 1, 12: 2, 14: 3}
    TURN_O0, TURN_O1 = 11, 2
    LOADS = 2 * PARTS * PARTS
    assert sum(CHUNKS) == G * KB * 2
    LAST = B * SPB - 1

    units, n = [], 0
    for step in range(STEPS):
        units += [("c", n + k) for k in range(CHUNKS[step])]
        n += CHUNKS[step]
        if step in TURN_M:
            units.append(("m", TURN_M[step]))
        if step in (TURN_O0, TURN_O1):
            units.append(("o", 0 if step == TURN_O0 else 1))
    before_all = [u for a in range(G) for u in [("c", 16 * a + k) for k in range(16)] + [("m", a)]]

    def units_of(s):
        if isinstance(s, int) and s < 0:
            return before_all, 0
        if is_first(s):
            return [u for u in units if u != ("o", 1)], len(before_all)
        went = len(before_all) - 1 + len(units) * s
        return ([("o", 1), ("o", 0), ("o", "last")] if isinstance(s, int) and s == LAST else units), went

    def count(s, unit):
        seq, went = units_of(s)
        return went + (seq.index(unit) + 1)

    def bank(s, unit):
        return units_of(s)[0].index(unit) % 3

    def freed(s, unit):
        seq, went = units_of(s)
        u = seq.index(unit)
        if u >= 3:
            return went + (u - 2)
        if isinstance(s, int) and s < 0:
            return None
        past = len(units_of(s - 1)[0] if isinstance(s, int) else units)
        return went - (past - 1 - max(v for v in range(past) if v % 3 == u))

    ident = sb("ident_c", [P, P])
    identb = sb("identb_c", [P, P], BF16)
    qa = sb("qa", [P, SPB, G, N], BF16)
    ka = sb("ka", [P, SPB, G, N], BF16)
    vg = sb("vg", [P, 2, KB, G, 32])
    pT = sb("pT", [P, 2, G, HALF])
    cmax = sb("cmax", [P, 2, KB, 2])
    nm = sb("nm", [P, 2, KB])
    nr = sb("nr", [P, 2, KB])
    mp = sb("mp", [P, 2, PARTS, KB], BF16)
    mT = sb("mT", [PARTS * KB, G, P], BF16)
    oT = sb("oT1", [P, HALF])
    orec = sb("orec", [P, G, G])

    ps_t = [ctx.enter_context(nc.psum_tensor(f"ps_t{k}", [P, 2, HALF], F32)) for k in range(2)]
    ps_q = [ctx.enter_context(nc.psum_tensor(f"ps_q{k}", [P, 512], F32)) for k in range(3)]
    ps_o = ctx.enter_context(nc.psum_tensor("ps_o1", [P, 512], F32))

    consts = sem("consts_c")
    filled_q = sem("filled_q")
    filled_k = sem("filled_k")
    loaded = [sem(f"loaded{k}") for k in range(SPB)]
    vg_done = sem("vg_done")
    unit_ready = sem("unit_ready")
    unit_read = sem("unit_read")
    m_split = sem("m_split")
    m_placed = [sem(f"m_placed{k}") for k in range(SPB)]
    t_ready = sem("t_ready")
    t_exp = sem("t_exp")
    pv_done = sem("pv_done1")
    o_copied = sem("o_copied1")
    o_inverted = sem("o_inverted")
    dve_step = sem("dve_step_c")
    OWN_TURN = 5 * G

    def turned_m(s, a):
        return ps_q[bank(s, ("m", a))][0:PARTS * KB, :].bitcast(BF16)[:, 0:P]

    def after(i, hg, k):
        return (i + (hg + k) // SPB), (hg + k) % SPB

    block = ctx.enter_context(nc.Block())

    @block.sync
    def _(sp):
        sp.dma_start(ident[:, :], io["ident"]).then_inc(consts, 16)
        sp.dma_start(identb[:, :], io["identb"]).then_inc(consts, 16)

        def load(b, hg):
            chans = slice(hg * G * D1, (hg + 1) * G * D1)
            for i in range(PARTS):
                for j in range(PARTS):
                    r = slice((i * PARTS + j) * D1, (i * PARTS + j + 1) * D1)
                    for dst, src in ((qa, parts_dram[0, i]), (ka, parts_dram[1, j])):
                        sp.dma_start(dst[r, hg, :, :], src[chans, bass.ds(b * N, N)].rearrange("(a d) t -> d a t", a=G)
                                     ).then_inc(loaded[hg], 16)

        def place(s, hg):
            for a in range(G):
                sp.wait_ge(unit_read, count(s, ("m", a)))
                sp.dma_start(qa[FULL:FULL + PARTS, hg, a, :], mT[:, a, :]).then_inc(m_placed[hg], 16)

        def turn(i, hg, last_batch):
            s = i * SPB + hg
            b, at = after(i, hg, 3)
            if not (last_batch and hg >= 1):
                sp.wait_ge(t_exp, 32 * s)
                load(b, at)
            if not (last_batch and hg == SPB - 1):
                place(s, (hg + 1) % SPB)

        for hg in range(SPB - 1):
            sp.wait_ge(filled_q, hg + 1)
            sp.wait_ge(filled_k, hg + 1)
            load(0, hg)
        sp.wait_ge(filled_q, SPB)
        sp.wait_ge(filled_k, SPB + 1)
        place(-1, 0)
        def batch(i):
            for hg in range(SPB):
                turn(i, hg, False)

        batch(0)
        with sp.Fori(1, B - 1) as i:
            batch(i)
        for hg in range(SPB):
            turn(B - 1, hg, True)

    @block.gpsimd
    def _(pool):
        for hg in range(SPB):
            pool.memset(ka[64:P, hg, :, :].rearrange("p a t -> p (a t)").bitcast(F32), 0.0).then_inc(filled_k, 1)
        pool.wait_ge(filled_k, SPB)
        pool.memset(ka[FULL:FULL + PARTS, :, :, :], 1.0).then_inc(filled_k, 1)
        pool.wait_ge(filled_k, SPB + 1)
        pool.memset(vg[:, :, :, :, :], 0.0).then_inc(vg_done, 1)
        pool.wait_ge(vg_done, 1)

        def values(b, hg):
            for k in range(KB):
                c = pool.tensor_copy(vg[:, hg % 2, k, :, 0:D1 + 1],
                                     v1[:, bass.ds(b * KB + k, 1), hg * G:(hg + 1) * G, :]
                                     .rearrange("p a h d -> p (a h) d"))
            c.then_inc(vg_done, 1)

        def turn(i, hg):
            pool.wait_ge(pv_done, STEPS * (i * SPB + hg))
            values(*after(i, hg, 1))

        values(0, 0)
        def batch(i):
            for hg in range(SPB):
                turn(i, hg)

        batch(0)
        with pool.Fori(1, B - 1) as i:
            batch(i)
        for hg in range(SPB - 1):
            turn(B - 1, hg)

    @block.scalar
    def _(act):
        def exps(s, step, k):
            act.wait_ge(t_ready, 32 * s + 2 * step + k + 1)
            if step >= 2 or not is_first(s):
                act.wait_ge(pv_done, STEPS * s + step - 1)
            act.activation(pT[:, step % 2, 2 * k:2 * k + 2, :], ps_t[k][:, :, :], ACT.Exp).then_inc(t_exp, 1)

        def copy_o(s, h):
            act.wait_ge(pv_done, STEPS * s + KB * h + KB)
            if h:
                act.wait_ge(unit_ready, count(s, ("o", 0)))
            elif not is_first(s):
                act.wait_ge(unit_ready, count(s, ("o", 1)))
            act.activation(oT[:, :], ps_o[:, :], ACT.Copy).then_inc(o_copied, 1)

        def one_set(s):
            for step in range(STEPS):
                for k in range(2):
                    exps(s, step, k)
                if step == 0 and not is_first(s):
                    copy_o(s - 1, 1)
                if step == KB:
                    copy_o(s, 0)

        one_set(0)
        with act.Fori(1, LAST) as s:
            one_set(s)
        one_set(LAST)
        copy_o(LAST, 1)

    @block.tensor
    def _(pe):
        def chunk(s, hg, c):
            a, k, h = c // 16, c // 2 % KB, c % 2
            free = freed(s, ("c", c))
            if free is not None:
                pe.wait_ge(unit_read, free)
            pe.matmul(ps_q[bank(s, ("c", c))][:, :], qa[0:FULL, hg, a, k * P:(k + 1) * P],
                      ka[0:FULL, hg, a, h * 512:(h + 1) * 512], start=True, stop=True).then_inc(unit_ready, 1)

        def turn_m(s, a):
            pe.wait_ge(unit_read, freed(s, ("m", a)))
            pe.wait_ge(m_split, G * s + G + a + 1)
            pe.transpose(turned_m(s, a), mp[:, a % 2, :, :].rearrange("p j k -> p (j k)"), identb[:, :]
                         ).then_inc(unit_ready, 1)

        def scores(s, hg, step, k):
            kb, h = step % KB, step // KB
            if step or not is_first(s):
                pe.wait_ge(t_exp, 32 * s + 2 * step + k - 1)
            for a in range(2):
                mm = pe.matmul(ps_t[k][:, a, :], ka[:, hg, 2 * k + a, kb * P:(kb + 1) * P],
                               qa[:, hg, 2 * k + a, h * HALF:(h + 1) * HALF], start=True, stop=True)
            mm.then_inc(t_ready, 1)

        def values(s, hg, step, heads):
            kb = step % KB
            if heads[0] == 0:
                pe.wait_ge(t_exp, 32 * s + 2 * step + 2)
                if kb == 0:
                    pe.wait_ge(o_copied, 2 * s + step // KB)
            for a in heads:
                mm = pe.matmul(ps_o[32 * a:32 * a + 32, :], vg[:, hg % 2, kb, a, :], pT[:, step % 2, a, :],
                               start=(kb == 0), stop=(kb == KB - 1), skip_group_check=True)
            if heads[-1] == G - 1:
                mm.then_inc(pv_done, 1)

        def turn_o(s, h, copied):
            pe.wait_ge(unit_read, freed(s, ("o", h)))
            pe.wait_ge(o_copied, copied)
            for k in range(4):
                mm = pe.transpose(ps_q[bank(s, ("o", h))][:, k * P:(k + 1) * P], oT[:, k * P:(k + 1) * P], ident[:, :])
            mm.then_inc(unit_ready, 1)

        def turn(i, hg, last):
            s = i * SPB + hg
            b, at = after(i, hg, 1)
            first = is_first(s)
            if not last:
                pe.wait_ge(loaded[at], 16 * LOADS * (b + 1))
            done = 0

            def some(n, step):
                nonlocal done
                if not last and done < sum(CHUNKS[:step + 1]):
                    for c in range(done, min(done + n, sum(CHUNKS[:step + 1]))):
                        chunk(s, at, c)
                        done = c + 1

            for step in range(STEPS):
                some(1, step)
                if step == 0:
                    pe.wait_ge(m_placed[hg], 16 * G * (i + 1))
                    pe.wait_ge(vg_done, s + 2)
                    if first:
                        pe.wait_ge(filled_k, SPB + 1)
                scores(s, hg, step, 0)
                some(1, step)
                scores(s, hg, step, 1)
                some(1, step)
                for heads in ((0, 1), (2, 3)):
                    if step:
                        values(s, hg, step - 1, heads)
                    elif not first:
                        values(s - 1, hg - 1, STEPS - 1, heads)
                    some(1, step)
                if not last and step in TURN_M:
                    turn_m(s, TURN_M[step])
                if step == TURN_O0:
                    turn_o(s, 0, 2 * s + 1)
                if step == TURN_O1 and not first:
                    turn_o(s, 1, 2 * s)

        pe.wait_ge(consts, 32)
        pe.wait_ge(loaded[0], 16 * LOADS)
        for a in range(G):
            for c in range(16 * a, 16 * a + 16):
                chunk(-1, 0, c)
            turn_m(-1, a)
        def batch(i):
            for hg in range(SPB):
                turn(i, hg, False)

        batch(0)
        with pe.Fori(1, B - 1) as i:
            batch(i)
        for hg in range(SPB):
            turn(B - 1, hg, hg == SPB - 1)
        values(B * SPB - 1, SPB - 1, STEPS - 1, range(G))
        turn_o(LAST, "last", 2 * B * SPB)

    @block.vector
    def _(dve):
        def maximum(s, c):
            a, k, h = c // 16, c // 2 % KB, c % 2
            dve.wait_ge(unit_ready, count(s, ("c", c)))
            dve.tensor_reduce(cmax[:, a % 2, k, h:h + 1], ps_q[bank(s, ("c", c))][:, :], AX.X, ALU.max,
                              negate=True).then_inc(unit_read, 1)

        def split(s, a, own):
            dve.wait_ge(unit_read, count(s, ("c", 16 * a + 15)))
            own.wait(own.done(dve.tensor_tensor(nm[:, a % 2, :], cmax[:, a % 2, :, 0], cmax[:, a % 2, :, 1], ALU.min)))
            own.wait(own.done(dve.tensor_copy(mp[:, a % 2, 0, :], nm[:, a % 2, :])))
            own.wait(own.done(dve.tensor_tensor(nr[:, a % 2, :], nm[:, a % 2, :], mp[:, a % 2, 0, :], ALU.subtract)))
            own.wait(own.done(dve.tensor_copy(mp[:, a % 2, 1, :], nr[:, a % 2, :])))
            own.wait(own.done(dve.tensor_tensor(nm[:, a % 2, :], nr[:, a % 2, :], mp[:, a % 2, 1, :], ALU.subtract)))
            dve.tensor_copy(mp[:, a % 2, 2, :], nm[:, a % 2, :]).then_inc(m_split, 1)

        def copy_m(s, a, placed=None, times=None):
            dve.wait_ge(unit_ready, count(s, ("m", a)))
            if a == 0 and placed is not None:
                dve.wait_ge(placed, times)
            dve.tensor_copy(mT[:, a, :], turned_m(s, a)).then_inc(unit_read, 1)

        def keep_o(s, unit, b, hg, h):
            n = 2 * (b * SPB + hg) + h
            dve.wait_ge(unit_ready, count(s, unit))
            r = ps_q[bank(s, unit)][:, :].rearrange("p (k a c) -> p k a c", k=4, a=G)
            dve.wait_ge(unit_read, count(s, unit) - 1)
            dve.reciprocal(orec[:, :, :], r[:, :, :, D1]).then_inc(o_inverted, 1)
            dve.wait_ge(o_inverted, n + 1)
            dst = inter[:, bass.ds(b * KB + h * 4, 4), hg * (G * D1):(hg + 1) * (G * D1)].rearrange("p k (a d) -> p k a d", a=G)
            dve.tensor_tensor(dst, r[:, :, :, 0:D1], orec[:, :, :].unsqueeze(3).to_broadcast([P, 4, G, D1]),
                              ALU.mult).then_inc(unit_read, 1)

        def turn(i, hg, last):
            s = i * SPB + hg
            own = Tally(dve, dve_step, OWN_TURN * (s + 1))
            c = 0
            for step in range(STEPS):
                if not last:
                    for _ in range(CHUNKS[step]):
                        maximum(s, c)
                        if c % 16 == 15:
                            split(s, c // 16, own)
                        c += 1
                    if step in TURN_M:
                        copy_m(s, TURN_M[step], m_placed[hg], 16 * G * (i + 1))
                if step == TURN_O0:
                    keep_o(s, ("o", 0), i, hg, 0)
                if step == TURN_O1 and not is_first(s):
                    keep_o(s, ("o", 1), i if hg else i - 1, (hg - 1) % SPB, 1)
            assert last or own.n == OWN_TURN

        for hg in range(SPB):
            dve.memset(qa[64:P, hg, :, :].rearrange("p a t -> p (a t)").bitcast(F32), 0.0).then_inc(filled_q, 1)
        own = Tally(dve, dve_step)
        for a in range(G):
            for c in range(16 * a, 16 * a + 16):
                maximum(-1, c)
            split(-1, a, own)
            copy_m(-1, a)
        assert own.n == OWN_TURN

        def batch(i):
            for hg in range(SPB):
                turn(i, hg, False)

        batch(0)
        with dve.Fori(1, B - 1) as i:
            batch(i)
        for hg in range(SPB):
            turn(B - 1, hg, hg == SPB - 1)
        keep_o(LAST, ("o", "last"), B - 1, SPB - 1, 1)


def output_and_experts(nc, ctx, io, x2, inter, out):

    def sb(name, shape, dt=F32):
        return ctx.enter_context(nc.sbuf_tensor(name, shape, dt))

    def sem(name):
        return ctx.enter_context(nc.semaphore(name))

    FC = F // P
    RMS_EPS = 1e-6
    ident = sb("ident_d", [P, P])
    wo = sb("wo", [P, D])
    bo = sb("bo", [P, D])
    rms = sb("rms", [P, D])
    gate = sb("gate", [P, E])
    w1 = sb("w1", [P, E, F])
    w2 = sb("w2", [P, E, FC, D])
    b1 = sb("b1", [P, E, FC])
    b2 = sb("b2", [E, D])
    rank = sb("rank", [P, E])
    xi = sb("xi", [P, GT, D])
    iT = sb("iT", [P, GC])
    xs = sb("xs", [P, GT, D])
    x3 = sb("x3", [P, GT, D])
    sq = sb("sq", [P, GT, D])
    xn = sb("xn", [P, GT, D])
    xnT = sb("xnT", [P, 2, GC])
    st = sb("std", [P, 2, GT, 6])
    mv = sb("mvd", [P, 2, GT, 2])
    sv = sb("svd", [P, 2, 5, GT])
    lg = sb("lgd", [P, 5, GT, E])
    tops = sb("tops", [P, 5, GT])
    wts = sb("wts", [P, 2, GT, E])
    wT = sb("wTd", [E, GC])
    hT = sb("hT", [P, 2, FC, GC])
    acc = sb("acc", [P, 2, GT, D])
    ys = sb("ys", [P, GT, D])
    ps_h = [ctx.enter_context(nc.psum_tensor(f"ps_h{k}", [P, 512], F32)) for k in range(2)]
    ps_y = [ctx.enter_context(nc.psum_tensor(f"ps_y{k}", [P, 512], F32)) for k in range(2)]
    ps_w = [ctx.enter_context(nc.psum_tensor(f"ps_w2{k}", [P, 512], F32)) for k in range(4)]

    consts = sem("consts_d")
    xi_done = sem("xi_done")
    i_turned = sem("i_turned")
    iT_done = sem("iT_done")
    proj_done = sem("proj_done")
    xn_done = sem("xn_done")
    xn_turned = sem("xn_turned")
    xnT_done = sem("xnT_done")
    logits_done = sem("logits_done")
    l_shifted = sem("l_shifted")
    l_exp = sem("l_exp")
    weights_done = sem("weights_done")
    w_turned = sem("w_turned")
    wT_done = sem("wT_done")
    bias_done = sem("bias_done")
    acc_begun = sem("acc_begun")
    h_ready = sem("h_ready")
    h_done = sem("h_done")
    y_ready = sem("y_ready")
    y_taken = sem("y_taken")
    out_done = sem("out_done")
    stored = sem("stored_d")
    front_step = sem("front_step")
    back_step = sem("back_step")
    FRONT_STEPS, BACK_STEPS = 37, 14

    loads = [(ident[:, :], io["ident"]), (wo[:, :], io["wo"]), (bo[:, :], io["bo"].to_broadcast([P, D])),
             (rms[:, :], io["rms"].to_broadcast([P, D])), (gate[:, :], io["gate"]), (w1[:, :, :], io["w1"]),
             (w2[:, :, :, :], io["w2"]), (b1[:, :, :], io["b1"]), (b2[:, :], io["b2"]), (rank[:, :], io["rank"])]
    ALL = 16 * len(loads)
    block = ctx.enter_context(nc.Block())

    @block.sync
    def _(sp):
        for dst, src in loads:
            sp.dma_start(dst, src).then_inc(consts, 16)
        def group(g):
            sp.wait_ge(out_done, g + 1)
            sp.dma_start(out.rearrange("(t p) d -> p t d", p=P)[:, bass.ds(g * GT, GT), :], ys[:, :, :]).then_inc(stored, 16)

        group(0)
        with sp.Fori(1, GROUPS) as g:
            group(g)
        sp.wait_ge(stored, 16 * GROUPS)

    @block.gpsimd
    def _(pool):
        def group(n):
            pool.wait_ge(i_turned, n)
            pool.tensor_copy(xi[:, :, :], inter[:, bass.ds(n * GT, GT), :]).then_inc(xi_done, 1)

        group(0)
        with pool.Fori(1, GROUPS) as n:
            group(n)

    @block.scalar
    def _(act):
        def copy_i(n):
            act.wait_ge(i_turned, n + 1)
            act.wait_ge(proj_done, n)
            act.activation(iT[:, :], ps_w[0][:, :], ACT.Copy).then_inc(iT_done, 1)

        def copy_xn(n, par):
            act.wait_ge(xn_turned, n + 1)
            act.activation(xnT[:, par, :], ps_w[2][:, :], ACT.Copy).then_inc(xnT_done, 1)

        def exps(n):
            act.wait_ge(l_shifted, n + 1)
            act.activation(lg[:, 1, :, :], lg[:, 0, :, :], ACT.Exp).then_inc(l_exp, 1)

        def copy_w(n):
            act.wait_ge(w_turned, n + 1)
            act.wait_ge(bias_done, n)
            act.activation(wT[:, :], ps_w[0][0:E, :], ACT.Copy).then_inc(wT_done, 1)

        def silu(g, e, c):
            n = e * FC + c
            act.wait_ge(h_ready, g * (E * FC) + n + 1)
            if e >= 2:
                act.wait_ge(y_ready, g * E + e - 1)
            else:
                act.wait_ge(y_ready, g * E)
            act.activation(hT[:, e % 2, c, :], ps_h[n % 2][:, :], ACT.Silu, bias=b1[:, e, c:c + 1],
                           scale=1.0).then_inc(h_done, 1)

        def turn(g, par, last):
            n = g + 1
            for e in range(E):
                for c in range(FC):
                    silu(g, e, c)
                if not last:
                    if e == 1:
                        copy_i(n)
                    elif e == 4:
                        copy_xn(n, 1 - par)
                    elif e == 5:
                        exps(n)
                    elif e == 7:
                        copy_w(n)

        act.wait_ge(consts, ALL)
        copy_i(0)
        copy_xn(0, 0)
        exps(0)
        copy_w(0)
        def two_groups(i):
            for par in range(2):
                turn(i * 2 + par, par, False)

        two_groups(0)
        with act.Fori(1, GROUPS // 2 - 1) as i:
            two_groups(i)
        turn(GROUPS - 2, 0, False)
        turn(GROUPS - 1, 1, True)

    @block.tensor
    def _(pe):
        def turn_i(n):
            pe.wait_ge(xi_done, n + 1)
            pe.wait_ge(wT_done, n)
            for k in range(GT):
                mm = pe.transpose(ps_w[0][:, k * P:(k + 1) * P], xi[:, k, :], ident[:, :])
            mm.then_inc(i_turned, 1)

        def project(n):
            pe.wait_ge(iT_done, n + 1)
            pe.wait_ge(acc_begun, n)
            for k in range(GT):
                mm = pe.matmul(ps_w[1][:, k * P:(k + 1) * P], iT[:, k * P:(k + 1) * P], wo[:, :], start=True, stop=True)
            mm.then_inc(proj_done, 1)

        def turn_xn(n):
            pe.wait_ge(xn_done, n + 1)
            for k in range(GT):
                mm = pe.transpose(ps_w[2][:, k * P:(k + 1) * P], xn[:, k, :], ident[:, :])
            mm.then_inc(xn_turned, 1)

        def logits(n, par):
            pe.wait_ge(xnT_done, n + 1)
            for k in range(GT):
                mm = pe.matmul(ps_w[3][:, k * E:(k + 1) * E], xnT[:, par, k * P:(k + 1) * P], gate[:, :],
                               start=True, stop=True)
            mm.then_inc(logits_done, 1)

        def turn_w(n, par):
            pe.wait_ge(weights_done, n + 1)
            for k in range(GT):
                mm = pe.transpose(ps_w[0][0:E, k * P:(k + 1) * P], wts[:, par, k, :], ident[:, :])
            mm.then_inc(w_turned, 1)

        def biases(n):
            pe.wait_ge(wT_done, n + 1)
            for k in range(GT):
                mm = pe.matmul(ps_w[1][:, k * P:(k + 1) * P], wT[:, k * P:(k + 1) * P], b2[:, :], start=True, stop=True)
            mm.then_inc(bias_done, 1)

        def inner(g, par, e):
            for c in range(FC):
                n = e * FC + c
                if n >= 2:
                    pe.wait_ge(h_done, g * (E * FC) + n - 1)
                else:
                    pe.wait_ge(h_done, g * (E * FC))
                pe.matmul(ps_h[n % 2][:, :], w1[:, e, c * P:(c + 1) * P], xnT[:, par, :],
                          start=True, stop=True).then_inc(h_ready, 1)

        def outer(g, e):
            pe.wait_ge(h_done, g * (E * FC) + (e + 1) * FC)
            pe.wait_ge(y_taken, g * E + max(e - 1, 0))
            for k in range(GT):
                for c in range(FC):
                    mm = pe.matmul(ps_y[e % 2][:, k * P:(k + 1) * P], hT[:, e % 2, c, k * P:(k + 1) * P], w2[:, e, c, :],
                                   start=(c == 0), stop=(c == FC - 1))
            mm.then_inc(y_ready, 1)

        def turn(g, par, last):
            n = g + 1
            for e in range(E):
                inner(g, par, e)
                if not last:
                    if e == 1:
                        turn_i(n)
                    elif e == 2:
                        project(n)
                    elif e == 4:
                        turn_xn(n)
                    elif e == 5:
                        logits(n, 1 - par)
                    elif e == 7:
                        turn_w(n, 1 - par)
                if e >= 1:
                    outer(g, e - 1)
            if not last:
                biases(n)
            outer(g, E - 1)

        pe.wait_ge(consts, ALL)
        turn_i(0)
        project(0)
        turn_xn(0)
        logits(0, 0)
        turn_w(0, 0)
        biases(0)
        def two_groups(i):
            for par in range(2):
                turn(i * 2 + par, par, False)

        two_groups(0)
        with pe.Fori(1, GROUPS // 2 - 1) as i:
            two_groups(i)
        turn(GROUPS - 2, 0, False)
        turn(GROUPS - 1, 1, True)

    @block.vector
    def _(dve):
        def third_norm(n, own):
            dve.wait_ge(proj_done, n + 1)
            dve.wait_ge(xn_turned, n)
            own.wait(own.done(dve.tensor_tensor(xs[:, :, :], ps_w[1][:, :].rearrange("p (k d) -> p k d", k=GT),
                                                bo[:, :].unsqueeze(1).to_broadcast([P, GT, D]), ALU.add)))
            own.wait(own.done(dve.tensor_tensor(xs[:, :, :], xs[:, :, :], x2[:, bass.ds(n * GT, GT), :], ALU.add)))
            own.wait(own.done(layernorm(own, xs, lambda k: x3[:, k, :], st[:, 0], mv[:, 0], sv[:, 0, 0, :], sv[:, 0, 1, :],
                                        sv[:, 0, 2, :])))
            own.wait(own.done(dve.tensor_tensor(sq[:, :, :], x3[:, :, :], x3[:, :, :], ALU.mult)))
            own.wait(own.done(dve.tensor_reduce(sv[:, 0, 3, :], sq[:, :, :], AX.X, ALU.add)))
            own.wait(own.done(dve.tensor_scalar(sv[:, 0, 0, :], sv[:, 0, 3, :], 1.0 / D, RMS_EPS, ALU.mult, ALU.add)))
            own.wait(own.done(rsqrt(own, sv[:, 0, 0, :], sv[:, 0, 1, :], sv[:, 0, 2, :])))
            for k in range(GT):
                last = dve.scalar_tensor_tensor(xn[:, k, :], x3[:, k, :], sv[:, 0, 1, k:k + 1], rms[:, :],
                                                ALU.mult, ALU.mult)
            last.then_inc(xn_done, 1)

        def shift(n, own):
            dve.wait_ge(logits_done, n + 1)
            r = ps_w[3][:, 0:GT * E].rearrange("p (k e) -> p k e", k=GT)
            own.wait(own.done(dve.tensor_reduce(tops[:, 0, :], r, AX.X, ALU.max)))
            dve.tensor_tensor(lg[:, 0, :, :], r, tops[:, 0, :].unsqueeze(2).to_broadcast([P, GT, E]),
                              ALU.subtract).then_inc(l_shifted, 1)

        def choose(n, par, own):
            def wide(row):
                return tops[:, row, :].unsqueeze(2).to_broadcast([P, GT, E])
            dve.wait_ge(l_exp, n + 1)
            dve.tensor_reduce(tops[:, 1, :], lg[:, 1, :, :], AX.X, ALU.add)
            own.wait(own.done(dve.tensor_reduce(tops[:, 2, :], lg[:, 1, :, :], AX.X, ALU.max)))
            dve.reciprocal(tops[:, 3, :], tops[:, 1, :])
            own.wait(own.done(dve.tensor_tensor(lg[:, 2, :, :], lg[:, 1, :, :], wide(2), ALU.is_ge)))
            dve.tensor_tensor(tops[:, 4, :], tops[:, 2, :], tops[:, 3, :], ALU.mult)
            own.wait(own.done(dve.tensor_tensor(lg[:, 3, :, :], lg[:, 2, :, :],
                                                rank[:, :].unsqueeze(1).to_broadcast([P, GT, E]), ALU.mult)))
            own.wait(own.done(dve.tensor_reduce(tops[:, 0, :], lg[:, 3, :, :], AX.X, ALU.max)))
            own.wait(own.done(dve.tensor_tensor(lg[:, 4, :, :], lg[:, 3, :, :], wide(0), ALU.is_ge)))
            dve.tensor_tensor(wts[:, par, :, :], lg[:, 4, :, :], wide(4), ALU.mult).then_inc(weights_done, 1)

        def begin(n, par):
            dve.wait_ge(bias_done, n + 1)
            dve.tensor_tensor(acc[:, par, :, :], ps_w[1][:, :].rearrange("p (k d) -> p k d", k=GT), x3[:, :, :],
                              ALU.add).then_inc(acc_begun, 1)

        def take(g, par, e, own):
            dve.wait_ge(y_ready, g * E + e + 1)
            if e == 0:
                dve.wait_ge(acc_begun, g + 1)
            else:
                dve.wait_ge(y_taken, g * E + e)
            for k in range(GT):
                last = dve.scalar_tensor_tensor(acc[:, par, k, :], ps_y[e % 2][:, k * P:(k + 1) * P],
                                                wts[:, par, k, e:e + 1], acc[:, par, k, :], ALU.mult, ALU.add)
            last.then_inc(y_taken, 1)

        def last_norm(g, par, own):
            dve.wait_ge(y_taken, g * E + E)
            dve.wait_ge(stored, 16 * g)
            layernorm(own, acc[:, par], lambda k: ys[:, k, :], st[:, 1], mv[:, 1], sv[:, 1, 0, :], sv[:, 1, 1, :],
                      sv[:, 1, 2, :]).then_inc(out_done, 1)

        def turn(g, par, last):
            n = g + 1
            own = Tally(dve, front_step, n * FRONT_STEPS)
            back = Tally(dve, back_step, g * BACK_STEPS)
            for e in range(E):
                if not last:
                    if e == 2:
                        third_norm(n, own)
                    elif e == 5:
                        shift(n, own)
                    elif e == 6:
                        choose(n, 1 - par, own)
                if e >= 1:
                    take(g, par, e - 1, back)
            if not last:
                begin(n, 1 - par)
                assert own.n == FRONT_STEPS, own.n
            take(g, par, E - 1, back)
            last_norm(g, par, back)
            assert back.n == BACK_STEPS, back.n

        dve.wait_ge(consts, ALL)
        own = Tally(dve, front_step)
        third_norm(0, own)
        shift(0, own)
        choose(0, 0, own)
        begin(0, 0)
        def two_groups(i):
            for par in range(2):
                turn(i * 2 + par, par, False)

        two_groups(0)
        with dve.Fori(1, GROUPS // 2 - 1) as i:
            two_groups(i)
        turn(GROUPS - 2, 0, False)
        turn(GROUPS - 1, 1, True)


def build(nc, io, out):
    with ExitStack() as ctx:
        inter = ctx.enter_context(nc.sbuf_tensor("inter", [P, TILES, D], F32))
        parts_dram = nc.dram_tensor("parts_dram", [2, PARTS, P, B * N], BF16, kind="Internal").ap()
        with ExitStack() as phase:
            layer0_attention(nc, phase, io, inter)
        x2 = ctx.enter_context(nc.sbuf_tensor("x2", [P, TILES, D], F32))
        v1 = ctx.enter_context(nc.sbuf_tensor("v1", [P, TILES, H1, D1 + 1], F32))
        with ExitStack() as phase:
            between_attentions(nc, phase, io, inter, x2, v1, parts_dram)
        with ExitStack() as phase:
            layer1_attention(nc, phase, io, v1, parts_dram, inter)
        with ExitStack() as phase:
            output_and_experts(nc, phase, io, x2, inter, out)


def _tables():
    f = np.float32

    def angles(width):
        inv = (f(1) / f(10000) ** (np.arange(0, width, 2, dtype=f) / f(width))).astype(f)
        return (np.arange(N, dtype=f)[:, None] * inv[None]).astype(f)

    t = {}
    a = np.concatenate([angles(DH)] * 2, 1)
    cos, sin = np.cos(a), np.sin(a) * np.repeat(f([-1, 1]), DH // 2)
    t["csT"] = np.concatenate([cos.T, sin.T], 0) * f(DH ** -0.5)
    t["cosn"] = cos.reshape(WIN, P, DH).transpose(1, 0, 2)
    t["sinn"] = sin.reshape(WIN, P, DH).transpose(1, 0, 2)
    masks = np.zeros((P, WIN, 2, KEYS), f)
    q = np.arange(P)[:, None]
    for w in range(WIN):
        own = np.where(np.arange(P)[None] > q, -1e30, 0)
        before = np.full((P, P), -1e30 if w == 0 else 0)
        slots = [before, own]
        segs = np.where(w * P + q > SEG * np.arange(NSEG)[None] + SEG - 1, 0, -1e30)
        masks[:, w, 0] = np.concatenate(slots + [segs], 1)
        masks[:, w, 1] = np.concatenate([segs] + slots, 1)
    t["masks"] = masks.astype(mybir.dt.np(BF16))
    t["ident"] = np.eye(P, dtype=f)
    t["identb"] = np.eye(P).astype(mybir.dt.np(BF16))
    t["segsel"] = (np.arange(P)[:, None] // SEG == np.arange(SPW)[None]).astype(f)
    t["headsel"] = ((np.arange(P)[:, None] // SPW) % 4 == np.arange(4)[None]).astype(f)
    a = np.repeat(angles(D1), 2, -1)
    cos = np.tile(np.cos(a).T, (H1, 1))
    sin = np.tile((np.sin(a) * np.tile(f([-1, 1]), D1 // 2)).T, (H1, 1))
    scale = f(1) / np.sqrt(f(D))
    t["cos1"] = np.stack([cos * scale, cos], 1)
    t["sin1"] = np.stack([sin * scale, sin], 1)
    t["rank"] = np.tile((E - np.arange(E)).astype(f), (P, 1))
    return t


def kernel(**inputs):
    import concourse.bacc as _bacc
    from concourse.bass_utils import run_bass_kernel_spmd as _run

    v = {k: np.asarray(a) for k, a in inputs.items()}

    def swapped(a):
        return a.reshape(*a.shape[:-1], D // 2, 2)[..., ::-1].reshape(a.shape)

    arrays = _tables()
    x = v["L0_attn_x"].reshape(TILES, P, D)
    wq0 = v["L0_attn_Wq"].reshape(D, H0, DH)
    h = DH // 2
    wq, bq, wk, bk = (v["L1_attn_" + n] for n in ("Wq", "bq", "Wk", "bk"))
    arrays.update(
        x=x.reshape(TILES * P, D), xT=x.transpose(0, 2, 1),
        wqs=np.concatenate([wq0, wq0[:, :, h:], wq0[:, :, :h]], 2),
        wkv=v["L0_attn_Wkv"], wout=v["L0_attn_Wout"], wproj=v["L0_attn_Wproj"],
        lg=v["L0_attn_ln_local_g"][None], lb=v["L0_attn_ln_local_b"][None],
        gg=v["L0_attn_ln_global_g"][None], gb=v["L0_attn_ln_global_b"][None],
        bout=v["L0_attn_bout"][None], w=v["L0_ffn_weight"],
        wqk=np.stack([wq, swapped(wq), wk, swapped(wk)], 1), bqk=np.stack([bq, swapped(bq), bk, swapped(bk)], 1),
        wv=v["L1_attn_Wv"], bv=v["L1_attn_bv"][None], wo=v["L1_attn_Wo"], bo=v["L1_attn_bo"][None],
        rms=v["L1_ffn_rms_w"][None], gate=v["L1_ffn_gate_w"].T,
        w1=v["L1_ffn_W1"].transpose(1, 0, 2), b1=v["L1_ffn_b1"].reshape(E, F // P, P).transpose(2, 0, 1),
        w2=v["L1_ffn_W2"].reshape(E, F // P, P, D).transpose(2, 0, 1, 3), b2=v["L1_ffn_b2"])
    arrays = {f"in_{k}": np.ascontiguousarray(a) for k, a in arrays.items()}

    nc = _bacc.Bacc("TRN2", target_bir_lowering=False, num_devices=1)
    io = {k[3:]: nc.dram_tensor(k, a.shape, mybir.dt.from_np(a.dtype), kind="ExternalInput").ap()
          for k, a in arrays.items()}
    out = nc.dram_tensor("out", (TILES * P, D), F32, kind="ExternalOutput").ap()
    build(nc, io, out)
    r = _run(nc, [arrays], core_ids=[0])
    return r.results[0]["out"].reshape(B, N, D)
```

```python
from contextlib import ExitStack

import numpy as np

import concourse.bass as bass
from concourse import mybir

F32 = mybir.dt.float32
BF16 = mybir.dt.bfloat16
I32 = mybir.dt.int32
ALU = mybir.AluOpType
ACT = mybir.ActivationFunctionType
AX = mybir.AxisListType

P = 128
B, N, D = 4, 1024, 128
TILES = B * N // P
WIN = N // P
EPS = 1e-5

H0, DH = 16, 64
PAIRS = H0 // 2
SEG = 16
SPW = P // SEG
NSEG = N // SEG
KEYS = 2 * P + NSEG
GLOB = (2 * P, 0)
LOCAL = (0, NSEG)
RING = 3


class Tally:

    def __init__(self, eng, sem, start=0):
        self.eng, self.sem, self.start, self.n = eng, sem, start, 0

    def done(self, ins):
        ins.then_inc(self.sem, 1)
        self.n += 1
        return self.n

    def wait(self, n=None):
        self.eng.wait_ge(self.sem, self.start + (self.n if n is None else n))


def is_first(n):
    return isinstance(n, int) and n == 0


def rsqrt(own, v, y, t):
    dve = own.eng
    own.wait(own.done(dve.tensor_scalar(t.bitcast(I32), v.bitcast(I32), 1, None, ALU.logical_shift_right)))
    own.wait(own.done(dve.tensor_scalar(y.bitcast(I32), t.bitcast(I32), -1.0, 1597463007.0, ALU.mult, ALU.add)))
    for k in range(3):
        own.wait(own.done(dve.tensor_tensor(t, y, y, ALU.mult)))
        own.wait(own.done(dve.scalar_tensor_tensor(t, t, -0.5, v, ALU.mult, ALU.mult)))
        last = dve.scalar_tensor_tensor(y, t, 1.5, y, ALU.add, ALU.mult)
        if k < 2:
            own.wait(own.done(last))
    return last


def layer0_attention(nc, ctx, io, res):

    def sb(name, shape, dt=F32):
        return ctx.enter_context(nc.sbuf_tensor(name, shape, dt))

    def sem(name):
        return ctx.enter_context(nc.semaphore(name))

    x_sb = sb("x_sb", [P, TILES, D])
    xT = sb("xT", [P, 2, P])
    wqs = sb("wqs", [P, H0, P])
    wkv = sb("wkv", [P, H0 * DH])
    wout = sb("wout", [P, PAIRS, D])
    wproj = sb("wproj", [P, DH])
    lg, lb = sb("lg", [P, DH]), sb("lb", [P, DH])
    gg, gb = sb("gg", [P, DH]), sb("gb", [P, DH])
    csT = sb("csT", [P, N])
    cosn = sb("cosn", [P, WIN, DH])
    sinn = sb("sinn", [P, WIN, DH])
    masks = sb("masks", [P, WIN, 2, KEYS], BF16)
    identb = sb("identb", [P, P], BF16)
    ident = sb("ident", [P, P])
    segsel = sb("segsel", [P, SPW])
    headsel = sb("headsel", [P, 4])
    qT = sb("qT", [P, 2, H0, P])
    KT = sb("KT", [P, H0, RING * P])
    KG = sb("KG", [P, H0, NSEG])
    V = sb("V", [P, 2, H0 * DH])
    gV = sb("gV", [P, 2, PAIRS, P])
    rc, rs = sb("rc", [P, H0, DH]), sb("rs_", [P, H0, DH])
    kvr = sb("kvr", [P, H0, DH])
    wl = sb("wl", [P, H0, DH])
    cen = sb("cen", [P, H0, DH])
    vn = sb("vn", [P, H0, DH])
    vst = sb("vst", [P, H0, DH])
    st = sb("st", [P, H0, 6])
    sm = sb("sm", [P, 16, H0])
    logit = sb("logit", [P, H0])
    e0, e1, pk = (sb(n, [H0, P]) for n in ("e0", "e1", "pk"))
    smax, ssum, srec = (sb(n, [H0, SPW]) for n in ("smax", "ssum", "srec"))
    wg = sb("wg", [P, H0, SPW])
    gm = sb("gm", [P, 4, DH])
    g0, g1, g2 = sb("g0", [P, DH]), sb("g1", [P, DH]), sb("g2", [P, DH])
    gk = sb("gk", [P, 2, DH])
    gst, gmv, gsm = sb("gst", [P, 6]), sb("gmv", [P, 2]), sb("gsm", [P, 8])
    spare = sb("spare", [P, 9])
    pr = sb("pr", [P, 2, 2 * KEYS])
    nmax = sb("nmax", [P, 2, 2])
    psums = sb("psums", [P, 2, 2])
    prec = sb("prec", [P, 2, 2])
    prT = sb("prT", [P, 2, 5 * P])
    oT = sb("oT", [P, 2, PAIRS, P])

    ps_s = [ctx.enter_context(nc.psum_tensor(f"ps_s{k}", [P, 2, 512], F32)) for k in range(2)]
    ps_xg = ctx.enter_context(nc.psum_tensor("ps_xg", [P, 1024], F32))
    ps_k = ps_xg[:, 5 * P:7 * P]
    ps_o = ctx.enter_context(nc.psum_tensor("ps_o", [P, 512], F32))
    ps_r = ctx.enter_context(nc.psum_tensor("ps_r", [P, 512], F32))
    gk_dram = nc.dram_tensor("gk_dram", [H0, NSEG, DH], F32, kind="Internal").ap()

    consts = sem("consts")
    late = sem("late")
    zeroed = sem("zeroed")
    x_landed = [sem(f"x_landed{k}") for k in range(2)]
    scores_ready = sem("scores_ready")
    max_done = sem("max_done")
    exp_done = sem("exp_done")
    recip_done = sem("recip_done")
    norm_done = sem("norm_done")
    turned = sem("turned")
    p_copied = sem("p_copied")
    pv_done = sem("pv_done")
    o_copied = sem("o_copied")
    proj_ready = sem("proj_ready")
    res_done = sem("res_done")
    kv_ready = sem("kv_ready")
    rot_products = sem("rot_products")
    kvr_done = sem("kvr_done")
    q_ready = sem("q_ready")
    q_done = sem("q_done")
    wl_done = sem("wl_done")
    cen_done = sem("cen_done")
    vn_done = sem("vn_done")
    vst_done = sem("vst_done")
    v_copied = sem("v_copied")
    keys_ready = sem("keys_ready")
    kt_copied = sem("kt_copied")
    logit_done = sem("logit_done")
    logit_turned = sem("logit_turned")
    e0_done = sem("e0_done")
    e1_done = sem("e1_done")
    pk_done = sem("pk_done")
    pk_turned = sem("pk_turned")
    wg_done = sem("wg_done")
    sums_ready = sem("sums_ready")
    gm_done = sem("gm_done")
    gk_done = sem("gk_done")
    gk_turned = sem("gk_turned")
    kg_copied = sem("kg_copied")
    gk_zeroed = sem("gk_zeroed")
    gk_stored = sem("gk_stored")
    gv_landed = [sem(f"gv_landed{k}") for k in range(2)]
    dve_step = sem("dve_step")
    DVE_STEPS = 35

    loads = [(wkv[:, :], io["wkv"]), (cosn[:, :, :], io["cosn"]), (sinn[:, :, :], io["sinn"]),
             (wproj[:, :], io["wproj"].rearrange("d a -> a d").to_broadcast([P, DH])),
             (lg[:, :], io["lg"].to_broadcast([P, DH])), (lb[:, :], io["lb"].to_broadcast([P, DH])),
             (gg[:, :], io["gg"].to_broadcast([P, DH])), (gb[:, :], io["gb"].to_broadcast([P, DH])),
             (ident[:, :], io["ident"]), (segsel[:, :], io["segsel"]), (headsel[:, :], io["headsel"]),
             (wqs[:, :, :], io["wqs"]), (csT[:, :], io["csT"])]
    late_loads = [(identb[:, :], io["identb"]), (masks[:, :, :, :], io["masks"]),
                  (wout[:, :, :], io["wout"].rearrange("(k p) d -> p k d", p=P)),
                  (x_sb[:, :, :], io["x"].rearrange("(t p) d -> p t d", p=P))]
    ALL_CONSTS, ALL_LATE = 16 * len(loads), 16 * len(late_loads)

    def row(small, k):
        return small[:, k, :]

    def before(t, p, k):
        return (t, p - k) if p >= k else (t - 1, p - k + PAIRS)

    block = ctx.enter_context(nc.Block())

    @block.sync
    def _(sp):
        def load_x(n, par):
            sp.dma_start(xT[:, par, :], io["xT"][bass.ds(n, 1), :, :].rearrange("a p t -> (a p) t")
                         ).then_inc(x_landed[par], 16)

        def store_segments(n, w):
            sp.wait_ge(gk_done, n + 1)
            sp.dma_start(gk_dram[:, bass.ds(w * SPW, SPW), :].rearrange("h s d -> h s d"),
                         gk[:, 0, :]).then_inc(gk_stored, 16)

        def load_segments(n, np_):
            sp.wait_ge(gk_stored, 16 * (n + 1))
            for a in range(2):
                sp.dma_start(gV[a * NSEG:(a + 1) * NSEG, np_, :, a * DH:(a + 1) * DH],
                             gk_dram.rearrange("(k a) s d -> a s k d", a=2)[a]).then_inc(gv_landed[np_], 16)

        load_x(0, 0)
        for dst, src in loads:
            sp.dma_start(dst, src).then_inc(consts, 16)
        load_x(1, 1)
        for dst, src in late_loads:
            sp.dma_start(dst, src).then_inc(late, 16)
        sp.wait_ge(zeroed, 5)
        sp.dma_start(gk_dram.rearrange("h s d -> (h s) d").rearrange("(a p) d -> p a d", p=P),
                     gV[:, 0, :, 0:DH]).then_inc(gk_zeroed, 16)
        sp.wait_ge(gk_zeroed, 16)
        store_segments(0, 0)
        load_segments(0, 0)

        def two_tiles(i):
            for par in range(2):
                t = i * 2 + par
                n = t + 1
                sp.wait_ge(q_done, 4 * (t + 1))
                sp.wait_ge(consts, ALL_CONSTS)
                load_x((t + 2) % TILES, par)
                store_segments(n, n % WIN)
                load_segments(n, 1 - par)

        two_tiles(0)
        with sp.Fori(1, TILES // 2) as i:
            two_tiles(i)
        for par in range(2):
            sp.wait_ge(x_landed[par], 16 * (TILES // 2 + 1))
        sp.wait_ge(gv_landed[0], 32 * (TILES // 2 + 1))
        sp.wait_ge(gv_landed[1], 32 * (TILES // 2))

    @block.tensor
    def _(pe):
        def kv(n, np_, half, turns=0):
            if half == 0:
                pe.wait_ge(x_landed[np_], 16 * (turns + 1))
                if not is_first(n):
                    pe.wait_ge(kg_copied, n)
            else:
                pe.wait_ge(rot_products, 2 * n + 1)
            pe.matmul(ps_r[:, :], xT[:, np_, :], wkv[:, half * 512:half * 512 + 512],
                      start=True, stop=True).then_inc(kv_ready, 1)

        def q(n, np_, quad):
            if quad == 0:
                pe.wait_ge(rot_products, 2 * n + 2)
            else:
                pe.wait_ge(q_done, 4 * n + quad)
            for k in range(4):
                mm = pe.matmul(ps_r[:, k * P:(k + 1) * P], wqs[:, 4 * quad + k, :], xT[:, np_, :],
                               start=True, stop=True)
            mm.then_inc(q_ready, 1)

        def logit_turn(n):
            pe.wait_ge(logit_done, n + 1)
            if not is_first(n) and not (isinstance(n, int) and n == 1):
                pe.wait_ge(res_done, n - 1)
            else:
                pe.wait_ge(q_done, 4 * n + 4)
            pe.transpose(ps_r[0:H0, 0:P], logit[:, :], ident[:, :]).then_inc(logit_turned, 1)

        def pk_turn(n):
            pe.wait_ge(pk_done, n + 1)
            pe.matmul(ps_r[:, 0:H0], pk[:, :], ident[0:H0, 0:H0], start=True, stop=True).then_inc(pk_turned, 1)

        def seg_sums(n):
            pe.wait_ge(wg_done, n + 1)
            for j in range(4):
                mm = pe.matmul(ps_r[32 * j:32 * j + 32, 0:4 * DH],
                               wg[:, 4 * j:4 * j + 4, :].rearrange("p h s -> p (h s)"),
                               kvr[:, 4 * j:4 * j + 4, :].rearrange("p h d -> p (h d)"), start=True, stop=True)
            mm.then_inc(sums_ready, 1)

        def keys_turn(n, j):
            if j % 2 == 0:
                pe.wait_ge(vst_done, 2 * n + j // 2 + 1)
            if j or not is_first(n):
                pe.wait_ge(kt_copied, 16 * n + 4 * j)
            for k in range(2):
                h = 4 * j + 2 * k
                mm = pe.transpose(ps_k[:, k * P:(k + 1) * P], vst[:, h:h + 2, :].rearrange("p h d -> p (h d)"),
                                  ident[:, :])
            mm.then_inc(keys_ready, 1)

        def seg_turn(n):
            pe.wait_ge(gk_done, n + 1)
            pe.transpose(ps_r[:, 0:P], gk[:, :, :].rearrange("p a d -> p (a d)"), ident[:, :]).then_inc(gk_turned, 1)

        def out_proj(t, par):
            if not (isinstance(t, int) and t == TILES - 1):
                pe.wait_ge(q_done, 4 * t + 12)
            pe.wait_ge(o_copied, 4 * t + 4)
            for k in range(PAIRS):
                mm = pe.matmul(ps_r[:, 0:D], oT[:, par, k, :], wout[:, k, :], start=(k == 0), stop=(k == PAIRS - 1))
            mm.then_inc(proj_ready, 1)

        def scores(t, par, p, slots, w):
            if p % 2 == 0:
                pe.wait_ge(kt_copied, 16 * t + 4 + 2 * p)
            pe.wait_ge(q_done, 4 * (t + 1))
            if p >= 2 or not is_first(t):
                pe.wait_ge(exp_done, PAIRS * t + p - 1)
            bank = ps_s[p % 2]
            for a in range(2):
                h = 2 * p + a
                pe.matmul(bank[:, a, 0:KEYS], identb[:, :], masks[:, bass.ds(w, 1), a, :].rearrange("p a k -> p (a k)"),
                          start=True, stop=False)
                for k, slot in enumerate(slots):
                    at = LOCAL[a] + k * P
                    pe.matmul(bank[:, a, at:at + P], qT[:, par, h, :], KT[:, h, bass.ds(slot * P, P)],
                              start=False, stop=False)

        def seg_scores(t, par, p):
            bank = ps_s[p % 2]
            if p == 0:
                pe.wait_ge(kg_copied, t + 1)
            for a in range(2):
                h = 2 * p + a
                mm = pe.matmul(bank[:, a, GLOB[a]:GLOB[a] + NSEG], qT[:, par, h, :], KG[:, h, :], start=False, stop=True)
            mm.then_inc(scores_ready, 1)

        def turn(t, p, keys=None):
            if p or not is_first(t):
                pe.wait_ge(p_copied, PAIRS * t + p)
            if p in (0, 1, 6, 7):
                pe.wait_ge(kt_copied, 16 * t + {0: 12, 1: 16, 6: 20, 7: 24}[p])
            if keys is not None:
                keys_turn(*keys)
            pe.wait_ge(norm_done, PAIRS * t + p + 1)
            r = pr[:, p % 2, :]
            for k, at in enumerate((0, P, 3 * P, 4 * P, 2 * P)):
                mm = pe.transpose(ps_xg[:, k * P:(k + 1) * P], r[:, at:at + P], ident[:, :])
            mm.then_inc(turned, 1)

        def values(t, par, p, turns):
            pe.wait_ge(p_copied, PAIRS * t + p + 1)
            if p == 0:
                pe.wait_ge(gv_landed[par], 32 * (turns + 1))
            if p % 4 == 0:
                pe.wait_ge(v_copied, 2 * t + p // 4 + 1)
            if p % 2 == 0 and (p or not is_first(t)):
                pe.wait_ge(o_copied, 4 * t + p // 2)
            at = (p % 4) * P
            pT = prT[:, p % 2, :]
            pe.matmul(ps_o[:, at:at + P], gV[:, par, p, :], pT[:, 4 * P:5 * P], start=True, stop=False,
                      skip_group_check=True)
            for s in range(2):
                for a in range(2):
                    h = 2 * p + a
                    mm = pe.matmul(ps_o[DH * a:DH * a + DH, at:at + P], V[:, (par + 1 + s) % 2, h * DH:(h + 1) * DH],
                                   pT[:, (2 * a + s) * P:(2 * a + s + 1) * P], start=False, stop=(s == 1),
                                   skip_group_check=True)
            mm.then_inc(pv_done, 1)

        pe.wait_ge(consts, ALL_CONSTS)
        kv(0, 0, 0)
        kv(0, 0, 1)
        for quad in range(4):
            q(0, 0, quad)
        logit_turn(0)
        pk_turn(0)
        seg_sums(0)
        keys_turn(0, 0)
        keys_turn(0, 1)
        seg_turn(0)
        pe.wait_ge(zeroed, 6)
        pe.wait_ge(late, ALL_LATE)

        def two_tiles(i):
            for par in range(2):
                t = i * 2 + par
                n, np_ = t + 1, 1 - par
                slots = (t + RING - 1) % RING, t % RING
                for p in range(PAIRS):
                    if p == 5:
                        logit_turn(n)
                    scores(t, par, p, slots, t % WIN)
                    if p:
                        seg_scores(t, par, p)
                    if p == 1:
                        kv(n, np_, 1)
                    elif p == 2:
                        q(n, np_, 1)
                    elif p == 3:
                        q(n, np_, 3)
                    elif p == 6:
                        pk_turn(n)
                    if p >= 2:
                        values(t, par, p - 2, i)
                    elif not is_first(t):
                        values(t - 1, np_, p - 2 + PAIRS, None)
                    if p == 0 and not is_first(t):
                        seg_turn(t)
                    if p == 0 and is_first(t):
                        keys_turn(t, 2)
                    elif p == 0:
                        turn(t - 1, PAIRS - 1, (t, 2))
                    else:
                        turn(t, p - 1, {1: (t, 3), 6: (n, 0), 7: (n, 1)}.get(p))
                    if p == 0:
                        seg_scores(t, par, p)
                    if p == 0:
                        kv(n, np_, 0, i + par)
                    elif p == 1:
                        q(n, np_, 0)
                    elif p == 2:
                        q(n, np_, 2)
                    elif p == 3 and not is_first(t):
                        out_proj(t - 1, np_)
                    elif p == 6:
                        seg_sums(n)

        two_tiles(0)
        with pe.Fori(1, TILES // 2) as i:
            two_tiles(i)
        seg_turn(TILES)
        last = TILES - 1
        values(last, 1, PAIRS - 2, None)
        turn(last, PAIRS - 1)
        values(last, 1, PAIRS - 1, None)
        pe.wait_ge(kg_copied, TILES + 1)
        out_proj(last, 1)

    @block.scalar
    def _(act):
        def exps(t, p):
            act.wait_ge(max_done, PAIRS * t + p + 1)
            if p >= 2 or not is_first(t):
                act.wait_ge(turned, PAIRS * t + p - 1)
            for a in range(2):
                e = act.activation(pr[:, p % 2, a * KEYS:(a + 1) * KEYS], ps_s[p % 2][:, a, 0:KEYS], ACT.Exp,
                                   bias=nmax[:, p % 2, a:a + 1], scale=1.0, accum_out=psums[:, p % 2, a:a + 1])
            e.then_inc(exp_done, 1)

        def copy_p(t, p):
            act.wait_ge(turned, PAIRS * t + p + 1)
            if p >= 2 or not is_first(t):
                act.wait_ge(pv_done, PAIRS * t + p - 1)
            act.activation(prT[:, p % 2, :], ps_xg[:, 0:5 * P], ACT.Copy).then_inc(p_copied, 1)

        def copy_o(t, par, j):
            act.wait_ge(pv_done, PAIRS * t + 2 * j + 2)
            if j == 0 and not (isinstance(t, int) and t < 2):
                act.wait_ge(proj_ready, t - 1)
            at = (2 * j % 4) * P
            act.activation(oT[:, par, 2 * j:2 * j + 2, :].rearrange("p k t -> p (k t)"), ps_o[:, at:at + 2 * P],
                           ACT.Copy).then_inc(o_copied, 1)

        def seg_exp(n):
            act.wait_ge(e0_done, n + 1)
            act.activation(e1[:, :], e0[:, :], ACT.Exp).then_inc(e1_done, 1)

        def copy_keys(n, slot, j):
            act.wait_ge(keys_ready, 4 * n + j + 1)
            for a in range(2):
                for to in range(2):
                    act.activation(KT[DH * to:DH * to + DH, 4 * j + a:4 * j + 4:2, bass.ds(slot * P, P)],
                                   ps_k[DH * a:DH * a + DH, :].rearrange("p (k t) -> p k t", k=2), ACT.Copy
                                   ).then_inc(kt_copied, 1)

        act.wait_ge(zeroed, 6)
        seg_exp(0)
        copy_keys(0, 0, 0)
        copy_keys(0, 0, 1)

        def two_tiles(i):
            for par in range(2):
                t = i * 2 + par
                n = t + 1
                for p in range(PAIRS):
                    if p == 5:
                        seg_exp(n)
                    exps(t, p)
                    if p >= 1:
                        copy_p(t, p - 1)
                    elif not is_first(t):
                        copy_p(t - 1, PAIRS - 1)
                    if p == 1 and not is_first(t):
                        copy_o(t - 1, 1 - par, 3)
                    elif p in (3, 5, 7):
                        copy_o(t, par, p // 2 - 1)
                    if p < 2:
                        copy_keys(t, t % RING, 2 + p)
                    elif p >= 6:
                        copy_keys(n, n % RING, p - 6)

        two_tiles(0)
        with act.Fori(1, TILES // 2) as i:
            two_tiles(i)
        copy_p(TILES - 1, PAIRS - 1)
        copy_o(TILES - 1, 1, 3)

    @block.gpsimd
    def _(pool):
        for n, fill in enumerate((KT[:, :, :], KG[:, :, :], V[:, :, :], gV[:, :, :, :], st[:, :, :])):
            pool.memset(fill, 0.0).then_inc(zeroed, 1)
        pool.wait_ge(zeroed, 5)
        pool.memset(spare[:, :], 0.0).then_inc(zeroed, 1)

        def carry_wait(k):
            pool.tensor_tensor(spare[:, k:k + 1], spare[:, 8:9], spare[:, 8:9], ALU.mult)

        def heads(half):
            return slice(8 * half, 8 * half + 8)

        def add_halves(n, half):
            pool.wait_ge(rot_products, 2 * n + half + 1)
            if half == 0 and not is_first(n):
                pool.wait_ge(gm_done, n)
            hs = heads(half)
            pool.tensor_tensor(kvr[:, hs, :], rc[:, hs, :], rs[:, hs, :], ALU.add).then_inc(kvr_done, 1)

        def weigh(n):
            pool.wait_ge(kvr_done, 2 * n + 2)
            if not is_first(n):
                pool.wait_ge(logit_done, n)
            pool.tensor_tensor(wl[:, :, :], kvr[:, :, :], wproj[:, :].unsqueeze(1).to_broadcast([P, H0, DH]),
                               ALU.mult).then_inc(wl_done, 1)

        def gain(n, half):
            pool.wait_ge(cen_done, 2 * n + half + 1)
            if not is_first(n):
                pool.wait_ge(vst_done, 2 * n)
            hs = heads(half)
            pool.tensor_tensor(vn[:, hs, :], cen[:, hs, :], lg[:, :].unsqueeze(1).to_broadcast([P, 8, DH]),
                               ALU.mult).then_inc(vn_done, 1)

        def norm(t, p):
            pool.wait_ge(recip_done, PAIRS * t + p + 1)
            carry_wait(p % 2)
            for a in range(2):
                r = pr[:, p % 2, a * KEYS:(a + 1) * KEYS]
                s = pool.tensor_scalar(r, r, prec[:, p % 2, a:a + 1], 1.0, ALU.mult, ALU.mult)
            s.then_inc(norm_done, 1)

        def keep_values(n, slot, half):
            pool.wait_ge(vst_done, 2 * n + half + 1)
            if not is_first(n):
                pool.wait_ge(pv_done, PAIRS * (n - 1) + 4 * half + 4)
            carry_wait(2)
            pool.tensor_scalar(V[:, slot, half * 512:half * 512 + 512],
                               vst[:, heads(half), :].rearrange("p h d -> p (h d)"), 1.0, 1.0,
                               ALU.mult, ALU.mult).then_inc(v_copied, 1)

        pool.wait_ge(consts, ALL_CONSTS)
        add_halves(0, 0)
        add_halves(0, 1)
        weigh(0)
        gain(0, 0)
        gain(0, 1)
        pool.wait_ge(zeroed, 6)
        keep_values(0, 0, 0)

        def two_tiles(i):
            for par in range(2):
                t = i * 2 + par
                n = t + 1
                for p in range(PAIRS):
                    if p == 1:
                        add_halves(n, 0)
                    elif p == 3:
                        keep_values(t, par, 1)
                    elif p == 5:
                        gain(n, 0)
                    norm(t, p)
                    if p == 1:
                        add_halves(n, 1)
                    elif p == 2:
                        weigh(n)
                    elif p == 5:
                        gain(n, 1)
                    elif p == 6:
                        keep_values(n, 1 - par, 0)

        two_tiles(0)
        with pool.Fori(1, TILES // 2) as i:
            two_tiles(i)

    @block.vector
    def _(dve):
        def heads(half):
            return slice(8 * half, 8 * half + 8)

        def rotate(n, w, half):
            dve.wait_ge(kv_ready, 2 * n + half + 1)
            if not is_first(n):
                dve.wait_ge(kvr_done, 2 * n)
            hs = heads(half)
            r = ps_r[:, :].rearrange("p (h d) -> p h d", h=8)
            c = cosn[:, bass.ds(w, 1), :].to_broadcast([P, 8, DH])
            h = DH // 2
            s0 = sinn[:, bass.ds(w, 1), 0:h].to_broadcast([P, 8, h])
            s1 = sinn[:, bass.ds(w, 1), h:DH].to_broadcast([P, 8, h])
            dve.tensor_tensor(rc[:, hs, :], r, c, ALU.mult)
            dve.tensor_tensor(rs[:, hs, 0:h], r[:, :, h:DH], s0, ALU.mult)
            dve.tensor_tensor(rs[:, hs, h:DH], r[:, :, 0:h], s1, ALU.mult).then_inc(rot_products, 1)

        def q_mult(n, np_, w, quad):
            dve.wait_ge(q_ready, 4 * n + quad + 1)
            dve.tensor_tensor(qT[:, np_, 4 * quad:4 * quad + 4, :], ps_r[:, :].rearrange("p (h t) -> p h t", h=4),
                              csT[:, bass.ds(w * P, P)].unsqueeze(1).to_broadcast([P, 4, P]),
                              ALU.mult).then_inc(q_done, 1)

        def stats(n, half):
            dve.wait_ge(kvr_done, 2 * n + half + 1)
            for h in range(8 * half, 8 * half + 8):
                last = dve.bn_stats(st[:, h, :], kvr[:, h, :])
            return last

        def variance(n, own, mark):
            own.wait(mark)
            dve.tensor_tensor(row(sm, 0), st[:, :, 1], st[:, :, 4], ALU.add)
            dve.tensor_tensor(row(sm, 1), st[:, :, 1], st[:, :, 4], ALU.subtract)
            m = own.done(dve.tensor_tensor(row(sm, 3), st[:, :, 2], st[:, :, 5], ALU.add))
            own.wait(m)
            dve.tensor_scalar(row(sm, 2), row(sm, 0), 0.5, None, ALU.mult)
            dve.tensor_scalar(row(sm, 8), row(sm, 3), 1.0 / DH, EPS, ALU.mult, ALU.add)
            m = own.done(dve.scalar_tensor_tensor(row(sm, 4), row(sm, 1), 0.25, row(sm, 1), ALU.mult, ALU.mult))
            own.wait(m)
            own.wait(own.done(dve.tensor_tensor(row(sm, 5), row(sm, 4), row(sm, 8), ALU.add)))
            return own.done(rsqrt(own, row(sm, 5), row(sm, 7), row(sm, 6)))

        def normalise(n, half, own, mark):
            own.wait(mark)
            if not is_first(n):
                dve.wait_ge(vn_done, 2 * n)
            for h in range(8 * half, 8 * half + 8):
                c = dve.tensor_scalar(cen[:, h, :], kvr[:, h, :], sm[:, 2, h:h + 1], sm[:, 7, h:h + 1],
                                      ALU.subtract, ALU.mult)
            c.then_inc(cen_done, 1)

        def add_bias(n, half):
            dve.wait_ge(vn_done, 2 * n + half + 1)
            if not is_first(n):
                dve.wait_ge(v_copied, 2 * n)
                dve.wait_ge(keys_ready, 4 * n)
            hs = heads(half)
            dve.tensor_tensor(vst[:, hs, :], vn[:, hs, :], lb[:, :].unsqueeze(1).to_broadcast([P, 8, DH]),
                              ALU.add).then_inc(vst_done, 1)

        def logits(n):
            dve.wait_ge(wl_done, n + 1)
            dve.tensor_reduce(logit[:, :], wl[:, :, :], AX.X, ALU.add).then_inc(logit_done, 1)

        def seg_shift(n, own):
            dve.wait_ge(logit_turned, n + 1)
            r = ps_r[0:H0, 0:P].rearrange("h (g s) -> h g s", s=SEG)
            own.wait(own.done(dve.tensor_reduce(smax[:, :], r, AX.X, ALU.max)))
            dve.tensor_tensor(e0[:, :].rearrange("h (g s) -> h g s", s=SEG), r,
                              smax[:, :].unsqueeze(2).to_broadcast([H0, SPW, SEG]), ALU.subtract).then_inc(e0_done, 1)

        def seg_probs(n, own):
            dve.wait_ge(e1_done, n + 1)
            e = e1[:, :].rearrange("h (g s) -> h g s", s=SEG)
            own.wait(own.done(dve.tensor_reduce(ssum[:, :], e, AX.X, ALU.add)))
            own.wait(own.done(dve.reciprocal(srec[:, :], ssum[:, :])))
            dve.tensor_tensor(pk[:, :].rearrange("h (g s) -> h g s", s=SEG), e,
                              srec[:, :].unsqueeze(2).to_broadcast([H0, SPW, SEG]), ALU.mult).then_inc(pk_done, 1)

        def seg_weights(n):
            dve.wait_ge(pk_turned, n + 1)
            dve.tensor_tensor(wg[:, :, :], ps_r[:, 0:H0].unsqueeze(2).to_broadcast([P, H0, SPW]),
                              segsel[:, :].unsqueeze(1).to_broadcast([P, H0, SPW]), ALU.mult).then_inc(wg_done, 1)

        def seg_variance(n, own):
            dve.wait_ge(sums_ready, n + 1)
            dve.tensor_tensor(gm[:, :, :], ps_r[:, 0:4 * DH].rearrange("p (h d) -> p h d", h=4),
                              headsel[:, :].unsqueeze(2).to_broadcast([P, 4, DH]), ALU.mult).then_inc(gm_done, 1)
            dve.wait_ge(gm_done, n + 1)
            own.wait(own.done(dve.tensor_reduce(g0[:, :], gm[:, :, :].rearrange("p h d -> p d h"), AX.X, ALU.add)))
            own.wait(own.done(dve.bn_stats(gst[:, :], g0[:, :])))
            dve.memset(gsm[:, 7:8], 0.0)
            own.wait(own.done(dve.bn_aggr(gmv[:, :], gst[:, :])))
            own.done(dve.tensor_scalar(gsm[:, 0:1], gmv[:, 1:2], EPS, None, ALU.add))

        def seg_scale(n, own):
            own.wait()
            return own.done(rsqrt(own, gsm[:, 0:1], gsm[:, 1:2], gsm[:, 2:3]))

        def seg_keys(n, own, mark):
            own.wait(mark)
            own.wait(own.done(dve.tensor_scalar(g1[:, :], g0[:, :], gmv[:, 0:1], gsm[:, 1:2], ALU.subtract, ALU.mult)))
            own.wait(own.done(dve.tensor_tensor(g2[:, :], g1[:, :], gg[:, :], ALU.mult)))
            if not is_first(n):
                dve.wait_ge(gk_stored, 16 * n)
                if not (isinstance(n, int) and n == 1):
                    dve.wait_ge(pv_done, PAIRS * (n - 1))
            dve.tensor_tensor(gk[:, :, :], g2[:, :].unsqueeze(1).to_broadcast([P, 2, DH]),
                              gb[:, :].unsqueeze(1).to_broadcast([P, 2, DH]), ALU.add).then_inc(gk_done, 1)

        def copy_segments(n, w):
            dve.wait_ge(gk_turned, n + 1)
            if not is_first(n):
                dve.wait_ge(scores_ready, PAIRS * n)
            r = ps_r[:, 0:P].rearrange("p (k a s) -> p k a s", a=2, s=SPW)
            for a in range(2):
                c = dve.tensor_copy(KG[:, a:H0:2, bass.ds(w * SPW, SPW)], r[:, :, a, :])
            c.then_inc(kg_copied, 1)

        def maxima(t, p):
            dve.wait_ge(scores_ready, PAIRS * t + p + 1)
            dve.tensor_reduce(nmax[:, p % 2, :], ps_s[p % 2][:, :, 0:KEYS], AX.X, ALU.max,
                              negate=True).then_inc(max_done, 1)

        def recips(t, p):
            dve.wait_ge(exp_done, PAIRS * t + p + 1)
            dve.reciprocal(prec[:, p % 2, :], psums[:, p % 2, :]).then_inc(recip_done, 1)

        def residual(t):
            dve.wait_ge(proj_ready, t + 1)
            dve.tensor_tensor(res[:, bass.ds(t, 1), :].rearrange("p a d -> p (a d)"), ps_r[:, 0:D],
                              x_sb[:, bass.ds(t, 1), :].rearrange("p a d -> p (a d)"), ALU.add).then_inc(res_done, 1)

        dve.wait_ge(consts, ALL_CONSTS)
        dve.wait_ge(zeroed, 6)
        own = Tally(dve, dve_step, 0)
        rotate(0, 0, 0)
        rotate(0, 0, 1)
        for quad in range(4):
            q_mult(0, 0, 0, quad)
        stats(0, 0)
        mark = variance(0, own, own.done(stats(0, 1)))
        logits(0)
        seg_shift(0, own)
        normalise(0, 0, own, mark)
        normalise(0, 1, own, mark)
        seg_probs(0, own)
        seg_weights(0)
        seg_variance(0, own)
        mark = seg_scale(0, own)
        seg_keys(0, own, mark)
        add_bias(0, 0)
        add_bias(0, 1)
        assert own.n == DVE_STEPS, own.n
        copy_segments(0, 0)
        dve.wait_ge(late, ALL_LATE)

        def two_tiles(i):
            for par in range(2):
                t = i * 2 + par
                n, np_ = t + 1, 1 - par
                w = n % WIN
                own = Tally(dve, dve_step, n * DVE_STEPS)
                for p in range(PAIRS):
                    if p == 0 and not is_first(t):
                        copy_segments(t, t % WIN)
                    elif p == 4 and not is_first(t):
                        residual(t - 1)
                    elif p == 5:
                        seg_shift(n, own)
                    elif p == 7:
                        seg_variance(n, own)
                    maxima(t, p)
                    if p < 2:
                        rotate(n, w, p)
                    elif p == 2:
                        q_mult(n, np_, w, 1)
                    elif p == 3:
                        q_mult(n, np_, w, 3)
                    elif p == 4:
                        logits(n)
                    elif p == 5:
                        seg_probs(n, own)
                    elif p == 6:
                        seg_weights(n)
                    elif p == 7:
                        scale_mark = seg_scale(n, own)
                    recips(t, p)
                    if p == 1:
                        q_mult(n, np_, w, 0)
                        stats(n, 0)
                    elif p == 2:
                        q_mult(n, np_, w, 2)
                        mark = own.done(stats(n, 1))
                    elif p == 3:
                        mark = variance(n, own, mark)
                    elif p in (4, 5):
                        normalise(n, p - 4, own, mark)
                        if p == 5:
                            add_bias(n, 0)
                    elif p == 6:
                        add_bias(n, 1)
                    elif p == 7:
                        seg_keys(n, own, scale_mark)
                assert own.n == DVE_STEPS, own.n

        two_tiles(0)
        with dve.Fori(1, TILES // 2) as i:
            two_tiles(i)
        copy_segments(TILES, 0)
        residual(TILES - 1)

GROUPS = TILES // 4
GT = 4
GC = GT * P
H1, D1 = 16, 8
PARTS = 3
E, F = 8, 512


def layernorm(own, src, dst, st, mv, ve, y, t, n=GT):
    dve = own.eng
    for k in range(n):
        last = dve.bn_stats(st[:, k, :], src[:, k, :])
    own.wait(own.done(last))
    dve.memset(t[:, 0:1], 0.0)
    for k in range(n):
        last = dve.bn_aggr(mv[:, k, :], st[:, k, :])
    own.wait(own.done(last))
    own.wait(own.done(dve.tensor_scalar(ve, mv[:, :, 1], EPS, None, ALU.add)))
    own.wait(own.done(rsqrt(own, ve, y, t)))
    for k in range(n):
        last = dve.tensor_scalar(dst(k), src[:, k, :], mv[:, k, 0:1], y[:, k:k + 1], ALU.subtract, ALU.mult)
    return last


def between_attentions(nc, ctx, io, res, x2, v1, parts_dram):

    def sb(name, shape, dt=F32):
        return ctx.enter_context(nc.sbuf_tensor(name, shape, dt))

    def sem(name):
        return ctx.enter_context(nc.semaphore(name))

    bout = sb("bout", [P, D])
    bv = sb("bv", [P, D])
    bqk = sb("bqk", [P, 4])
    wqk = sb("wqk", [P, 4, D])
    wv = sb("wv", [P, D])
    cos1, sin1 = sb("cos1", [P, N]), sb("sin1", [P, N])
    ident = sb("ident_b", [P, P])
    ones = sb("ones_b", [P, P])
    w = sb("w", [P, D])
    tern = sb("tern", [P, D])
    ternT = sb("ternT", [P, D])
    ws = sb("ws", [P, 8])
    xa = sb("xa", [P, GT, D])
    xb = sb("xb", [P, GT, D])
    x1 = sb("x1", [P, GT, D])
    x1T = sb("x1T", [P, GC])
    xf = sb("xf", [P, GT, D])
    x2T = sb("x2T", [P, GC])
    st = sb("stb", [P, GT, 6])
    mv = sb("mvb", [P, GT, 2])
    sv = sb("svb", [P, 3, GT])
    rot = sb("rot", [P, 2, 2, GC])
    full = sb("full", [P, 2, GC])
    rest = sb("rest", [P, 2, 2, GC])
    part = sb("part", [P, 2, PARTS, GC], BF16)
    ps = [ctx.enter_context(nc.psum_tensor(f"psb{k}", [P, 512], F32)) for k in range(8)]

    consts = sem("consts_b")
    tables_in = sem("tables_in")
    w_step = sem("w_step")
    row_sums = sem("row_sums")
    w_sum = sem("w_sum")
    tern_done = sem("tern_done")
    tern_turned = sem("tern_turned")
    ternT_done = sem("ternT_done")
    ones_done = sem("ones_done")
    x1_done = sem("x1_done")
    x1_turned = sem("x1_turned")
    x1T_done = sem("x1T_done")
    ffn_done = sem("ffn_done")
    x2_done = sem("x2_done")
    x2_turned = sem("x2_turned")
    x2T_done = sem("x2T_done")
    qk_done = sem("qk_done")
    v_done = sem("v_done")
    v_kept = sem("v_kept")
    rot_done = sem("rot_done")
    full_done = sem("full_done")
    hi_done = sem("hi_done")
    r1_done = sem("r1_done")
    mid_done = sem("mid_done")
    r2_done = sem("r2_done")
    lo_done = sem("lo_done")
    stored = [sem(f"stored{k}") for k in range(2)]
    dve_step = sem("dve_step_b")
    STEPS = 30

    loads = [(bout[:, :], io["bout"].to_broadcast([P, D])), (bv[:, :], io["bv"].to_broadcast([P, D])),
             (bqk[:, :], io["bqk"]), (wqk[:, :, :], io["wqk"]), (wv[:, :], io["wv"]),
             (ident[:, :], io["ident"]), (w[:, :], io["w"])]
    tables = [(cos1[:, :], io["cos1"]), (sin1[:, :], io["sin1"])]
    ALL = 16 * len(loads)
    block = ctx.enter_context(nc.Block())

    @block.sync
    def _(sp):
        for dst, src in loads:
            sp.dma_start(dst, src).then_inc(consts, 16)
        for dst, src in tables:
            sp.dma_start(dst, src).then_inc(tables_in, 16)

        def group(g):
            for k in range(2):
                sp.wait_ge(lo_done, 2 * g + k + 1)
                sp.dma_start(parts_dram[k].rearrange("j c t -> c j t")[:, :, bass.ds(g * GC, GC)],
                             part[:, k, :, :]).then_inc(stored[k], 16)

        group(0)
        with sp.Fori(1, GROUPS) as g:
            group(g)
        for k in range(2):
            sp.wait_ge(stored[k], 16 * GROUPS)

    @block.gpsimd
    def _(pool):
        pool.memset(ones[:, :], 1.0).then_inc(ones_done, 1)
        pool.memset(v1[:, :, :, :], 0.0).then_inc(ones_done, 1)
        def group(g):
            for k in range(2):
                pool.wait_ge(rot_done, 4 * g + 2 * k + 2)
                pool.wait_ge(r1_done, 2 * g + k)
                pool.tensor_tensor(full[:, k, :], rot[:, k, 0, :], rot[:, k, 1, :], ALU.add).then_inc(full_done, 1)

        group(0)
        with pool.Fori(1, GROUPS) as g:
            group(g)

    @block.scalar
    def _(act):
        def front(n):
            act.wait_ge(x1_turned, n + 1)
            act.activation(x1T[:, :], ps[0][:, :], ACT.Copy).then_inc(x1T_done, 1)

        def group(g, last=False):
            act.wait_ge(x2_turned, g + 1)
            act.activation(x2T[:, :], ps[2][:, :], ACT.Copy).then_inc(x2T_done, 1)
            if not last:
                front(g + 1)
            for src, ready, done, j in ((full, full_done, hi_done, 0), (rest, r1_done, mid_done, 1),
                                        (rest, r2_done, lo_done, 2)):
                for k in range(2):
                    act.wait_ge(ready, 2 * g + k + 1)
                    if j == 0:
                        act.wait_ge(stored[k], 16 * g)
                    s = full[:, k, :] if j == 0 else rest[:, k, j - 1, :]
                    act.activation(part[:, k, j, :], s, ACT.Copy).then_inc(done, 1)

        front(0)
        group(0)
        with act.Fori(1, GROUPS - 1) as g:
            group(g)
        group(GROUPS - 1, True)

    @block.tensor
    def _(pe):
        pe.wait_ge(ones_done, 2)
        pe.wait_ge(consts, ALL)
        pe.wait_ge(row_sums, 1)
        pe.matmul(ps[0][:, 0:1], ones[:, :], ws[:, 0:1], start=True, stop=True).then_inc(w_sum, 1)
        pe.wait_ge(tern_done, 1)
        pe.transpose(ps[1][:, 0:D], tern[:, :], ident[:, :]).then_inc(tern_turned, 1)
        pe.wait_ge(ternT_done, 1)

        def front(n):
            pe.wait_ge(x1_done, n + 1)
            for k in range(GT):
                mm = pe.transpose(ps[0][:, k * P:(k + 1) * P], x1[:, k, :], ident[:, :])
            mm.then_inc(x1_turned, 1)
            pe.wait_ge(x1T_done, n + 1)
            for k in range(GT):
                mm = pe.matmul(ps[1][:, k * P:(k + 1) * P], x1T[:, k * P:(k + 1) * P], ternT[:, :], start=True, stop=True)
            mm.then_inc(ffn_done, 1)

        def group(g, last=False):
            pe.wait_ge(x2_done, g + 1)
            for k in range(GT):
                mm = pe.transpose(ps[2][:, k * P:(k + 1) * P], xb[:, k, :], ident[:, :])
            mm.then_inc(x2_turned, 1)
            pe.wait_ge(x2T_done, g + 1)
            pe.wait_ge(rot_done, 4 * g)
            for k in range(4):
                pe.matmul(ps[4 + k][:, :], wqk[:, k, :], x2T[:, :], start=True, stop=True).then_inc(qk_done, 1)
            pe.wait_ge(v_kept, g)
            for k in range(GT):
                mm = pe.matmul(ps[3][:, k * P:(k + 1) * P], x2T[:, k * P:(k + 1) * P], wv[:, :], start=True, stop=True)
            mm.then_inc(v_done, 1)
            if not last:
                front(g + 1)

        front(0)
        group(0)
        with pe.Fori(1, GROUPS - 1) as g:
            group(g)
        group(GROUPS - 1, True)

    @block.vector
    def _(dve):
        dve.wait_ge(consts, ALL)
        dve.wait_ge(ones_done, 2)
        own = Tally(dve, w_step)
        dve.tensor_reduce(ws[:, 0:1], w[:, :], AX.X, ALU.add, apply_absolute_value=True).then_inc(row_sums, 1)
        dve.wait_ge(w_sum, 1)
        own.wait(own.done(dve.tensor_scalar(ws[:, 1:2], ps[0][:, 0:1], 1.0 / (D * D), EPS, ALU.mult, ALU.max)))
        own.wait(own.done(dve.reciprocal(ws[:, 2:3], ws[:, 1:2])))
        own.wait(own.done(dve.tensor_scalar(tern[:, :], w[:, :], ws[:, 2:3], None, ALU.mult)))
        own.wait(own.done(dve.tensor_scalar(tern[:, :], tern[:, :], 12582912.0, None, ALU.add)))
        own.wait(own.done(dve.tensor_scalar(tern[:, :], tern[:, :], -12582912.0, 1.0, ALU.add, ALU.min)))
        dve.tensor_scalar(tern[:, :], tern[:, :], -1.0, ws[:, 1:2], ALU.max, ALU.mult).then_inc(tern_done, 1)
        dve.wait_ge(tern_turned, 1)
        dve.tensor_copy(ternT[:, :], ps[1][:, 0:D]).then_inc(ternT_done, 1)

        def first_norm(n, own):
            own.wait(own.done(dve.tensor_tensor(xa[:, :, :], res[:, bass.ds(n * GT, GT), :],
                                                bout[:, :].unsqueeze(1).to_broadcast([P, GT, D]), ALU.add)))
            layernorm(own, xa, lambda k: x1[:, k, :], st, mv, sv[:, 0, :], sv[:, 1, :], sv[:, 2, :]).then_inc(x1_done, 1)

        def second_norm(n, own):
            dve.wait_ge(ffn_done, n + 1)
            dve.wait_ge(x1_done, n + 1)
            own.wait(own.done(dve.tensor_tensor(xf[:, :, :], ps[1][:, :].rearrange("p (k d) -> p k d", k=GT),
                                                x1[:, :, :], ALU.add)))
            dve.wait_ge(x2_turned, n)
            layernorm(own, xf, lambda k: xb[:, k, :], st, mv, sv[:, 0, :], sv[:, 1, :], sv[:, 2, :]).then_inc(x2_done, 1)
            assert own.n == STEPS, own.n

        def keep(n):
            dve.wait_ge(x2_done, n + 1)
            dve.tensor_copy(x2[:, bass.ds(n * GT, GT), :], xb[:, :, :])

        def group(g, last=False):
            own = Tally(dve, dve_step, (g + 1) * STEPS)
            if not last:
                first_norm(g + 1, own)
            half = bass.ds(g % 2 * GC, GC)
            for k in range(2):
                for c, table in enumerate((cos1, sin1)):
                    dve.wait_ge(qk_done, 4 * g + 2 * k + c + 1)
                    dve.wait_ge(full_done, 2 * g)
                    dve.scalar_tensor_tensor(rot[:, k, c, :], ps[4 + 2 * k + c][:, :], bqk[:, 2 * k + c:2 * k + c + 1],
                                             table[:, half], ALU.add, ALU.mult).then_inc(rot_done, 1)
            dve.wait_ge(v_done, g + 1)
            dve.tensor_tensor(v1[:, bass.ds(g * GT, GT), :, 0:D1],
                              ps[3][:, :].rearrange("p (k h d) -> p k h d", k=GT, h=H1),
                              bv[:, :].rearrange("p (h d) -> p h d", h=H1).unsqueeze(1).to_broadcast([P, GT, H1, D1]),
                              ALU.add).then_inc(v_kept, 1)
            if not last:
                second_norm(g + 1, own)
            for k in range(2):
                dve.wait_ge(hi_done, 2 * g + k + 1)
                dve.wait_ge(lo_done, 2 * g)
                dve.tensor_tensor(rest[:, k, 0, :], full[:, k, :], part[:, k, 0, :], ALU.subtract).then_inc(r1_done, 1)
            if not last:
                keep(g + 1)
            for k in range(2):
                dve.wait_ge(mid_done, 2 * g + k + 1)
                dve.wait_ge(r1_done, 2 * g + k + 1)
                dve.tensor_tensor(rest[:, k, 1, :], rest[:, k, 0, :], part[:, k, 1, :], ALU.subtract).then_inc(r2_done, 1)

        own = Tally(dve, dve_step)
        first_norm(0, own)
        second_norm(0, own)
        keep(0)
        dve.wait_ge(tables_in, 16 * len(tables))
        group(0)
        with dve.Fori(1, GROUPS - 1) as g:
            group(g)
        group(GROUPS - 1, True)
        dve.memset(v1[:, :, :, D1:D1 + 1], 1.0).then_inc(ones_done, 1)


def layer1_attention(nc, ctx, io, v1, parts_dram, inter):

    def sb(name, shape, dt=F32):
        return ctx.enter_context(nc.sbuf_tensor(name, shape, dt))

    def sem(name):
        return ctx.enter_context(nc.semaphore(name))

    G = 4
    SPB = H1 // G
    KB = N // P
    HALF = N // 2
    STEPS = 2 * KB
    FULL = 96
    CHUNKS = [5] * 8 + [4] * 6 + [0, 0]
    TURN_M = {8: 0, 14: 1}
    TURN_O0, TURN_O1 = 11, 2
    LOADS = 2 * PARTS * PARTS
    assert sum(CHUNKS) == G * KB * 2
    LAST = B * SPB - 1
    SCALE1 = float(D) ** -0.5

    units, n = [], 0
    for step in range(STEPS):
        units += [("c", n + k) for k in range(CHUNKS[step])]
        n += CHUNKS[step]
        if step in TURN_M:
            units.append(("m", TURN_M[step]))
        if step in (TURN_O0, TURN_O1):
            units.append(("o", 0 if step == TURN_O0 else 1))
    before_all = [u for m in range(2) for u in [("c", 32 * m + k) for k in range(32)] + [("m", m)]]

    def units_of(s):
        if isinstance(s, int) and s < 0:
            return before_all, 0
        if is_first(s):
            return [u for u in units if u != ("o", 1)], len(before_all)
        went = len(before_all) - 1 + len(units) * s
        return ([("o", 1), ("o", 0), ("o", "last")] if isinstance(s, int) and s == LAST else units), went

    def count(s, unit):
        seq, went = units_of(s)
        return went + (seq.index(unit) + 1)

    def bank(s, unit):
        return units_of(s)[0].index(unit) % 3

    def freed(s, unit):
        seq, went = units_of(s)
        u = seq.index(unit)
        if u >= 3:
            return went + (u - 2)
        if isinstance(s, int) and s < 0:
            return None
        past = len(units_of(s - 1)[0] if isinstance(s, int) else units)
        return went - (past - 1 - max(v for v in range(past) if v % 3 == u))

    ident = sb("ident_c", [P, P])
    identb = sb("identb_c", [P, P], BF16)
    qa = sb("qa", [P, SPB, G, N], BF16)
    ka = sb("ka", [P, SPB, G, N], BF16)
    vg = sb("vg", [P, 2, KB, G, 32])
    pT = sb("pT", [P, 2, G, HALF])
    cmax = sb("cmax", [P, G, KB, 2])
    nm = sb("nm", [P, 2, 2, KB])
    nr = sb("nr", [P, 2, 2, KB])
    mp = sb("mp", [P, 2, 2, PARTS, KB], BF16)
    mT = sb("mT", [2 * PARTS * KB, 2, P], BF16)
    oT = sb("oT1", [P, HALF])
    orec = sb("orec", [P, G, G])

    ps_t = [ctx.enter_context(nc.psum_tensor(f"ps_t{k}", [P, 2, HALF], F32)) for k in range(2)]
    ps_q = [ctx.enter_context(nc.psum_tensor(f"ps_q{k}", [P, 512], F32)) for k in range(3)]
    ps_o = ctx.enter_context(nc.psum_tensor("ps_o1", [P, 512], F32))

    consts = sem("consts_c")
    filled_q = sem("filled_q")
    filled_k = sem("filled_k")
    loaded = [sem(f"loaded{k}") for k in range(SPB)]
    vg_done = sem("vg_done")
    unit_ready = sem("unit_ready")
    unit_read = sem("unit_read")
    m_split = sem("m_split")
    m_placed = [sem(f"m_placed{k}") for k in range(SPB)]
    t_ready = sem("t_ready")
    t_exp = sem("t_exp")
    pv_done = sem("pv_done1")
    o_copied = sem("o_copied1")
    o_inverted = sem("o_inverted")
    dve_step = sem("dve_step_c")
    OWN_TURN = 5 * 2

    def turned_m(s, m):
        return ps_q[bank(s, ("m", m))][0:2 * PARTS * KB, 0:P]

    def after(i, hg, k):
        return (i + (hg + k) // SPB), (hg + k) % SPB

    block = ctx.enter_context(nc.Block())

    @block.sync
    def _(sp):
        sp.dma_start(ident[:, :], io["ident"]).then_inc(consts, 16)
        sp.dma_start(identb[:, :], io["identb"]).then_inc(consts, 16)

        def load(b, hg):
            chans = slice(hg * G * D1, (hg + 1) * G * D1)
            for i in range(PARTS):
                for j in range(PARTS):
                    r = slice((i * PARTS + j) * D1, (i * PARTS + j + 1) * D1)
                    for dst, src in ((qa, parts_dram[0, i]), (ka, parts_dram[1, j])):
                        sp.dma_start(dst[r, hg, :, :], src[chans, bass.ds(b * N, N)].rearrange("(a d) t -> d a t", a=G)
                                     ).then_inc(loaded[hg], 16)

        def place(s, hg):
            for m in range(2):
                sp.wait_ge(unit_read, count(s, ("m", m)))
                for a in range(2):
                    rows = slice(a * PARTS * KB, (a + 1) * PARTS * KB)
                    sp.dma_start(qa[FULL:FULL + PARTS, hg, 2 * m + a, :], mT[rows, m, :]).then_inc(m_placed[hg], 16)

        def turn(i, hg, last_batch):
            s = i * SPB + hg
            b, at = after(i, hg, 3)
            if not (last_batch and hg >= 1):
                sp.wait_ge(t_exp, 32 * s)
                load(b, at)
            if not (last_batch and hg == SPB - 1):
                place(s, (hg + 1) % SPB)

        for hg in range(SPB - 1):
            sp.wait_ge(filled_q, hg + 1)
            sp.wait_ge(filled_k, hg + 1)
            load(0, hg)
        sp.wait_ge(filled_q, SPB)
        sp.wait_ge(filled_k, SPB + 1)
        place(-1, 0)
        def batch(i):
            for hg in range(SPB):
                turn(i, hg, False)

        batch(0)
        with sp.Fori(1, B - 1) as i:
            batch(i)
        for hg in range(SPB):
            turn(B - 1, hg, True)

    @block.gpsimd
    def _(pool):
        for hg in range(SPB):
            pool.memset(ka[64:P, hg, :, :].rearrange("p a t -> p (a t)").bitcast(F32), 0.0).then_inc(filled_k, 1)
        pool.wait_ge(filled_k, SPB)
        pool.memset(ka[FULL:FULL + PARTS, :, :, :], 1.0).then_inc(filled_k, 1)
        pool.wait_ge(filled_k, SPB + 1)
        pool.memset(vg[:, :, :, :, :], 0.0).then_inc(vg_done, 1)
        pool.wait_ge(vg_done, 1)

        def values(b, hg):
            for k in range(KB):
                c = pool.tensor_copy(vg[:, hg % 2, k, :, 0:D1 + 1],
                                     v1[:, bass.ds(b * KB + k, 1), hg * G:(hg + 1) * G, :]
                                     .rearrange("p a h d -> p (a h) d"))
            c.then_inc(vg_done, 1)

        def turn(i, hg):
            pool.wait_ge(pv_done, STEPS * (i * SPB + hg))
            values(*after(i, hg, 1))

        values(0, 0)
        def batch(i):
            for hg in range(SPB):
                turn(i, hg)

        batch(0)
        with pool.Fori(1, B - 1) as i:
            batch(i)
        for hg in range(SPB - 1):
            turn(B - 1, hg)

    @block.scalar
    def _(act):
        def exps(s, step, k):
            act.wait_ge(t_ready, 32 * s + 2 * step + k + 1)
            if step >= 2 or not is_first(s):
                act.wait_ge(pv_done, STEPS * s + step - 1)
            act.activation(pT[:, step % 2, 2 * k:2 * k + 2, :], ps_t[k][:, :, :], ACT.Exp,
                           scale=SCALE1).then_inc(t_exp, 1)

        def copy_o(s, h):
            act.wait_ge(pv_done, STEPS * s + KB * h + KB)
            if h:
                act.wait_ge(unit_ready, count(s, ("o", 0)))
            elif not is_first(s):
                act.wait_ge(unit_ready, count(s, ("o", 1)))
            act.activation(oT[:, :], ps_o[:, :], ACT.Copy).then_inc(o_copied, 1)

        def one_set(s):
            for step in range(STEPS):
                for k in range(2):
                    exps(s, step, k)
                if step == 0 and not is_first(s):
                    copy_o(s - 1, 1)
                if step == KB:
                    copy_o(s, 0)

        one_set(0)
        with act.Fori(1, LAST) as s:
            one_set(s)
        one_set(LAST)
        copy_o(LAST, 1)

    @block.tensor
    def _(pe):
        def chunk(s, hg, c):
            a, k, h = c // 16, c // 2 % KB, c % 2
            free = freed(s, ("c", c))
            if free is not None:
                pe.wait_ge(unit_read, free)
            pe.matmul(ps_q[bank(s, ("c", c))][:, :], qa[0:FULL, hg, a, k * P:(k + 1) * P],
                      ka[0:FULL, hg, a, h * 512:(h + 1) * 512], start=True, stop=True).then_inc(unit_ready, 1)

        def turn_m(s, m):
            pe.wait_ge(unit_read, freed(s, ("m", m)))
            pe.wait_ge(m_split, 2 * s + m + 3)
            pe.matmul(turned_m(s, m), mp[:, m, :, :, :].rearrange("p a j k -> p (a j k)"), identb[:, :],
                      start=True, stop=True).then_inc(unit_ready, 1)

        def scores(s, hg, step, k):
            kb, h = step % KB, step // KB
            if step or not is_first(s):
                pe.wait_ge(t_exp, 32 * s + 2 * step + k - 1)
            for a in range(2):
                mm = pe.matmul(ps_t[k][:, a, :], ka[:, hg, 2 * k + a, kb * P:(kb + 1) * P],
                               qa[:, hg, 2 * k + a, h * HALF:(h + 1) * HALF], start=True, stop=True)
            mm.then_inc(t_ready, 1)

        def values(s, hg, step, heads):
            kb = step % KB
            if heads[0] == 0:
                pe.wait_ge(t_exp, 32 * s + 2 * step + 2)
                if kb == 0:
                    pe.wait_ge(o_copied, 2 * s + step // KB)
            for a in heads:
                mm = pe.matmul(ps_o[32 * a:32 * a + 32, :], vg[:, hg % 2, kb, a, :], pT[:, step % 2, a, :],
                               start=(kb == 0), stop=(kb == KB - 1), skip_group_check=True)
            if heads[-1] == G - 1:
                mm.then_inc(pv_done, 1)

        def turn_o(s, h, copied):
            pe.wait_ge(unit_read, freed(s, ("o", h)))
            pe.wait_ge(o_copied, copied)
            for k in range(4):
                mm = pe.transpose(ps_q[bank(s, ("o", h))][:, k * P:(k + 1) * P], oT[:, k * P:(k + 1) * P], ident[:, :])
            mm.then_inc(unit_ready, 1)

        def turn(i, hg, last):
            s = i * SPB + hg
            b, at = after(i, hg, 1)
            first = is_first(s)
            if not last:
                pe.wait_ge(loaded[at], 16 * LOADS * (b + 1))
            done = 0

            def some(n, step):
                nonlocal done
                if not last and done < sum(CHUNKS[:step + 1]):
                    for c in range(done, min(done + n, sum(CHUNKS[:step + 1]))):
                        chunk(s, at, c)
                        done = c + 1

            for step in range(STEPS):
                some(1, step)
                if step == 0:
                    pe.wait_ge(m_placed[hg], 16 * G * (i + 1))
                    pe.wait_ge(vg_done, s + 2)
                    if first:
                        pe.wait_ge(filled_k, SPB + 1)
                scores(s, hg, step, 0)
                some(1, step)
                scores(s, hg, step, 1)
                some(1, step)
                for heads in ((0, 1), (2, 3)):
                    if step:
                        values(s, hg, step - 1, heads)
                    elif not first:
                        values(s - 1, hg - 1, STEPS - 1, heads)
                    some(1, step)
                if not last and step in TURN_M:
                    turn_m(s, TURN_M[step])
                if step == TURN_O0:
                    turn_o(s, 0, 2 * s + 1)
                if step == TURN_O1 and not first:
                    turn_o(s, 1, 2 * s)

        pe.wait_ge(consts, 32)
        pe.wait_ge(loaded[0], 16 * LOADS)
        for m in range(2):
            for c in range(32 * m, 32 * m + 32):
                chunk(-1, 0, c)
            turn_m(-1, m)
        def batch(i):
            for hg in range(SPB):
                turn(i, hg, False)

        batch(0)
        with pe.Fori(1, B - 1) as i:
            batch(i)
        for hg in range(SPB):
            turn(B - 1, hg, hg == SPB - 1)
        values(B * SPB - 1, SPB - 1, STEPS - 1, range(G))
        turn_o(LAST, "last", 2 * B * SPB)

    @block.vector
    def _(dve):
        def maximum(s, c):
            a, k, h = c // 16, c // 2 % KB, c % 2
            dve.wait_ge(unit_ready, count(s, ("c", c)))
            dve.tensor_reduce(cmax[:, a, k, h:h + 1], ps_q[bank(s, ("c", c))][:, :], AX.X, ALU.max,
                              negate=True).then_inc(unit_read, 1)

        def split(s, m, own):
            dve.wait_ge(unit_read, count(s, ("c", 32 * m + 31)))
            two = slice(2 * m, 2 * m + 2)
            own.wait(own.done(dve.tensor_tensor(nm[:, m, :, :], cmax[:, two, :, 0], cmax[:, two, :, 1], ALU.min)))
            own.wait(own.done(dve.tensor_copy(mp[:, m, :, 0, :], nm[:, m, :, :])))
            own.wait(own.done(dve.tensor_tensor(nr[:, m, :, :], nm[:, m, :, :], mp[:, m, :, 0, :], ALU.subtract)))
            own.wait(own.done(dve.tensor_copy(mp[:, m, :, 1, :], nr[:, m, :, :])))
            own.wait(own.done(dve.tensor_tensor(nm[:, m, :, :], nr[:, m, :, :], mp[:, m, :, 1, :], ALU.subtract)))
            dve.tensor_copy(mp[:, m, :, 2, :], nm[:, m, :, :]).then_inc(m_split, 1)

        def copy_m(s, m, placed=None, times=None):
            dve.wait_ge(unit_ready, count(s, ("m", m)))
            if m == 0 and placed is not None:
                dve.wait_ge(placed, times)
            dve.tensor_copy(mT[:, m, :], turned_m(s, m)).then_inc(unit_read, 1)

        def keep_o(s, unit, b, hg, h):
            n = 2 * (b * SPB + hg) + h
            dve.wait_ge(unit_ready, count(s, unit))
            r = ps_q[bank(s, unit)][:, :].rearrange("p (k a c) -> p k a c", k=4, a=G)
            dve.wait_ge(unit_read, count(s, unit) - 1)
            dve.reciprocal(orec[:, :, :], r[:, :, :, D1]).then_inc(o_inverted, 1)
            dve.wait_ge(o_inverted, n + 1)
            dst = inter[:, bass.ds(b * KB + h * 4, 4), hg * (G * D1):(hg + 1) * (G * D1)].rearrange("p k (a d) -> p k a d", a=G)
            dve.tensor_tensor(dst, r[:, :, :, 0:D1], orec[:, :, :].unsqueeze(3).to_broadcast([P, 4, G, D1]),
                              ALU.mult).then_inc(unit_read, 1)

        def turn(i, hg, last):
            s = i * SPB + hg
            own = Tally(dve, dve_step, OWN_TURN * (s + 1))
            c = 0
            for step in range(STEPS):
                if not last:
                    for _ in range(CHUNKS[step]):
                        maximum(s, c)
                        if c % 32 == 31:
                            split(s, c // 32, own)
                        c += 1
                    if step in TURN_M:
                        copy_m(s, TURN_M[step], m_placed[hg], 16 * G * (i + 1))
                if step == TURN_O0:
                    keep_o(s, ("o", 0), i, hg, 0)
                if step == TURN_O1 and not is_first(s):
                    keep_o(s, ("o", 1), i if hg else i - 1, (hg - 1) % SPB, 1)
            assert last or own.n == OWN_TURN

        for hg in range(SPB):
            dve.memset(qa[64:P, hg, :, :].rearrange("p a t -> p (a t)").bitcast(F32), 0.0).then_inc(filled_q, 1)
        own = Tally(dve, dve_step)
        for m in range(2):
            for c in range(32 * m, 32 * m + 32):
                maximum(-1, c)
            split(-1, m, own)
            copy_m(-1, m)
        assert own.n == OWN_TURN

        def batch(i):
            for hg in range(SPB):
                turn(i, hg, False)

        batch(0)
        with dve.Fori(1, B - 1) as i:
            batch(i)
        for hg in range(SPB):
            turn(B - 1, hg, hg == SPB - 1)
        keep_o(LAST, ("o", "last"), B - 1, SPB - 1, 1)


def output_and_experts(nc, ctx, io, x2, inter, out):

    def sb(name, shape, dt=F32):
        return ctx.enter_context(nc.sbuf_tensor(name, shape, dt))

    def sem(name):
        return ctx.enter_context(nc.semaphore(name))

    FC = F // P
    RMS_EPS = 1e-6
    SLOTS = TILES + E - 1
    RT, RGROUPS = 8, TILES // 8
    RC = RT * P
    ident = sb("ident_d", [P, P])
    wo = sb("wo", [P, D])
    bo = sb("bo", [P, D])
    rms = sb("rms", [P, D])
    gate = sb("gate", [P, E])
    rank = sb("rank", [P, E])
    before = sb("before", [P, P])
    starts = sb("starts", [P, SLOTS])
    ones = sb("ones_d", [P, P])
    w1 = sb("w1", [P, E, F])
    w2 = sb("w2", [P, E, FC, D])
    b1 = sb("b1", [P, E, F])
    b2 = sb("b2", [P, E, D])
    zeros = sb("zeros", [P, D])
    onehot = sb("onehot", [P, TILES, E])
    score = sb("score", [P, TILES])
    place = sb("place", [P, TILES], I32)
    expert_of = sb("expert_of", [P, SLOTS], I32)
    xs_dram = nc.dram_tensor("xs_dram", [SLOTS * P, D], F32, kind="Internal").ap()
    ys_dram = nc.dram_tensor("ys_dram", [SLOTS * P, D], F32, kind="Internal").ap()

    consts = sem("consts_d")
    weights = sem("weights_d")
    cleared = sem("cleared")
    loads = [(ident[:, :], io["ident"]), (wo[:, :], io["wo"]), (bo[:, :], io["bo"].to_broadcast([P, D])),
             (rms[:, :], io["rms"].to_broadcast([P, D])), (gate[:, :], io["gate"]), (rank[:, :], io["rank"]),
             (before[:, :], io["before"]), (starts[:, :], io["starts"])]
    expert_loads = [(w1[:, :, :], io["w1"]), (w2[:, :, :, :], io["w2"]),
                    (b1[:, :, :].rearrange("p e f -> p (e f)"), io["b1"].to_broadcast([P, E * F])),
                    (b2[:, :, :].rearrange("p e d -> p (e d)"), io["b2"].to_broadcast([P, E * D]))]
    ALL, ALL_WEIGHTS = 16 * len(loads), 16 * len(expert_loads)


    def route(ctx):

        def sb(name, shape, dt=F32):
            return ctx.enter_context(nc.sbuf_tensor(name, shape, dt))

        def sem(name):
            return ctx.enter_context(nc.semaphore(name))

        xi = sb("xi", [P, RT, D])
        iT = sb("iT", [P, RC])
        xs = sb("xs", [P, RT, D])
        sq = sb("sq", [P, RT, D])
        xn = sb("xn", [P, RT, D])
        x3 = sb("x3", [P, RT, D])
        xnT = sb("xnT", [P, RC])
        st, mv, sv = sb("std", [P, RT, 6]), sb("mvd", [P, RT, 2]), sb("svd", [P, 4, RT])
        lg = sb("lgd", [P, 4, RT, E])
        tops = sb("tops", [P, 5, RT])
        ps_w = [ctx.enter_context(nc.psum_tensor(f"ps_w2{k}", [P, RC if k < 3 else 512], F32)) for k in range(4)]
        xi_done = sem("xi_done")
        i_turned = sem("i_turned")
        iT_done = sem("iT_done")
        proj_done = sem("proj_done")
        xn_done = sem("xn_done")
        xn_turned = sem("xn_turned")
        xnT_done = sem("xnT_done")
        logits_done = sem("logits_done")
        l_shifted = sem("l_shifted")
        l_exp = sem("l_exp")
        filled = sem("filled_d")
        chosen = sem("chosen")
        own_step = sem("own_step_d")
        FRONT_STEPS, BACK_STEPS = 32, 6
        block = ctx.enter_context(nc.Block())

        @block.sync
        def _(sp):
            for dst, src in loads:
                sp.dma_start(dst, src).then_inc(consts, 16)
            for dst, src in expert_loads:
                sp.dma_start(dst, src).then_inc(weights, 16)
            sp.wait_ge(filled, 2)
            for j in range(SLOTS):
                sp.dma_start(xs_dram[j * P:(j + 1) * P, :], zeros[:, :]).then_inc(cleared, 16)
            sp.wait_ge(weights, ALL_WEIGHTS)
            sp.wait_ge(cleared, 16 * SLOTS)

        @block.gpsimd
        def _(pool):
            pool.memset(zeros[:, :], 0.0).then_inc(filled, 1)
            pool.memset(ones[:, :], 1.0).then_inc(filled, 1)

            def group(n):
                pool.wait_ge(i_turned, n)
                pool.tensor_copy(xi[:, :, :], inter[:, bass.ds(n * RT, RT), :]).then_inc(xi_done, 1)

            group(0)
            with pool.Fori(1, RGROUPS) as n:
                group(n)

        @block.scalar
        def _(act):
            def front(n):
                act.wait_ge(i_turned, n + 1)
                act.activation(iT[:, :], ps_w[0][:, :], ACT.Copy).then_inc(iT_done, 1)

            def group(g, last=False):
                if not last:
                    front(g + 1)
                act.wait_ge(xn_turned, g + 1)
                act.activation(xnT[:, :], ps_w[2][:, :], ACT.Copy).then_inc(xnT_done, 1)
                act.wait_ge(l_shifted, g + 1)
                act.activation(lg[:, 1, :, :], lg[:, 0, :, :], ACT.Exp).then_inc(l_exp, 1)

            front(0)
            group(0)
            with act.Fori(1, RGROUPS - 1) as g:
                group(g)
            group(RGROUPS - 1, True)

        @block.tensor
        def _(pe):
            def front(n):
                pe.wait_ge(xi_done, n + 1)
                for k in range(RT):
                    mm = pe.transpose(ps_w[0][:, k * P:(k + 1) * P], xi[:, k, :], ident[:, :])
                mm.then_inc(i_turned, 1)
                pe.wait_ge(iT_done, n + 1)
                pe.wait_ge(xn_done, n)
                for k in range(RT):
                    mm = pe.matmul(ps_w[1][:, k * P:(k + 1) * P], iT[:, k * P:(k + 1) * P], wo[:, :], start=True, stop=True)
                mm.then_inc(proj_done, 1)

            def group(g, last=False):
                if not last:
                    front(g + 1)
                pe.wait_ge(xn_done, g + 1)
                for k in range(RT):
                    mm = pe.transpose(ps_w[2][:, k * P:(k + 1) * P], xn[:, k, :], ident[:, :])
                mm.then_inc(xn_turned, 1)
                pe.wait_ge(xnT_done, g + 1)
                pe.wait_ge(l_shifted, g)
                for k in range(RT):
                    mm = pe.matmul(ps_w[3][:, k * E:(k + 1) * E], xnT[:, k * P:(k + 1) * P], gate[:, :],
                                   start=True, stop=True)
                mm.then_inc(logits_done, 1)

            pe.wait_ge(consts, ALL)
            front(0)
            group(0)
            with pe.Fori(1, RGROUPS - 1) as g:
                group(g)
            group(RGROUPS - 1, True)

        @block.vector
        def _(dve):
            def third_norm(n, own):
                dve.wait_ge(proj_done, n + 1)
                own.wait(own.done(dve.tensor_tensor(xs[:, :, :], ps_w[1][:, :].rearrange("p (k d) -> p k d", k=RT),
                                                    bo[:, :].unsqueeze(1).to_broadcast([P, RT, D]), ALU.add)))
                own.wait(own.done(dve.tensor_tensor(xs[:, :, :], xs[:, :, :], x2[:, bass.ds(n * RT, RT), :], ALU.add)))
                own.wait(own.done(layernorm(own, xs, lambda k: x3[:, k, :], st, mv, sv[:, 0, :], sv[:, 1, :], sv[:, 2, :], RT)))
                own.wait(own.done(dve.tensor_tensor(sq[:, :, :], x3[:, :, :], x3[:, :, :], ALU.mult)))
                own.wait(own.done(dve.tensor_reduce(sv[:, 3, :], sq[:, :, :], AX.X, ALU.add)))
                own.wait(own.done(dve.tensor_scalar(sv[:, 0, :], sv[:, 3, :], 1.0 / D, RMS_EPS, ALU.mult, ALU.add)))
                own.wait(own.done(rsqrt(own, sv[:, 0, :], sv[:, 1, :], sv[:, 2, :])))
                dve.wait_ge(xn_turned, n)
                for k in range(RT):
                    last = dve.scalar_tensor_tensor(xn[:, k, :], x3[:, k, :], sv[:, 1, k:k + 1], rms[:, :],
                                                    ALU.mult, ALU.mult)
                last.then_inc(xn_done, 1)
                dve.tensor_copy(x2[:, bass.ds(n * RT, RT), :], x3[:, :, :])
                dve.wait_ge(xn_done, n + 1)
                own.wait(own.done(dve.tensor_copy(inter[:, bass.ds(n * RT, RT), :], xn[:, :, :])))

            def shift(g, own):
                dve.wait_ge(logits_done, g + 1)
                r = ps_w[3][:, 0:RT * E].rearrange("p (k e) -> p k e", k=RT)
                own.wait(own.done(dve.tensor_reduce(tops[:, 0, :], r, AX.X, ALU.max)))
                dve.tensor_tensor(lg[:, 0, :, :], r, tops[:, 0, :].unsqueeze(2).to_broadcast([P, RT, E]),
                                  ALU.subtract).then_inc(l_shifted, 1)

            def choose(g, own):
                def wide(row):
                    return tops[:, row, :].unsqueeze(2).to_broadcast([P, RT, E])
                dve.wait_ge(l_exp, g + 1)
                dve.tensor_reduce(tops[:, 1, :], lg[:, 1, :, :], AX.X, ALU.add)
                own.wait(own.done(dve.tensor_reduce(tops[:, 2, :], lg[:, 1, :, :], AX.X, ALU.max)))
                dve.reciprocal(tops[:, 3, :], tops[:, 1, :])
                own.wait(own.done(dve.tensor_tensor(lg[:, 2, :, :], lg[:, 1, :, :], wide(2), ALU.is_ge)))
                dve.tensor_tensor(score[:, bass.ds(g * RT, RT)], tops[:, 2, :], tops[:, 3, :], ALU.mult)
                own.wait(own.done(dve.tensor_tensor(lg[:, 3, :, :], lg[:, 2, :, :],
                                                    rank[:, :].unsqueeze(1).to_broadcast([P, RT, E]), ALU.mult)))
                own.wait(own.done(dve.tensor_reduce(tops[:, 4, :], lg[:, 3, :, :], AX.X, ALU.max)))
                own.wait(own.done(dve.tensor_tensor(onehot[:, bass.ds(g * RT, RT), :], lg[:, 3, :, :], wide(4), ALU.is_ge)))

            def group(g, last=False):
                front = Tally(dve, own_step, (g + 1) * FRONT_STEPS + g * BACK_STEPS)
                back = Tally(dve, own_step, (g + 2) * FRONT_STEPS + g * BACK_STEPS - (FRONT_STEPS if last else 0))
                if not last:
                    third_norm(g + 1, front)
                    assert front.n == FRONT_STEPS, front.n
                shift(g, back)
                choose(g, back)
                assert back.n == BACK_STEPS, back.n

            dve.wait_ge(consts, ALL)
            own = Tally(dve, own_step)
            third_norm(0, own)
            group(0)
            with dve.Fori(1, RGROUPS - 1) as g:
                group(g)
            group(RGROUPS - 1, True)

    def sort_tokens(ctx):
        def sb(name, shape, dt=F32):
            return ctx.enter_context(nc.sbuf_tensor(name, shape, dt))

        def sem(name):
            return ctx.enter_context(nc.semaphore(name))

        run = sb("run", [P, 2, TILES, E])
        count = sb("count", [P, TILES, E])
        at = sb("at", [P, TILES, E])
        total = sb("total", [P, E])
        whole = sb("whole", [P, E], I32)
        size = sb("size", [P, E])
        ends = sb("ends", [P, 2, E])
        first = sb("first", [P, E])
        placef = sb("placef", [P, TILES])
        passed = sb("passed", [P, SLOTS, E])
        expertf = sb("expertf", [P, SLOTS])
        ps_c = ctx.enter_context(nc.psum_tensor("ps_c", [P, 512], F32))
        ps_b = ctx.enter_context(nc.psum_tensor("ps_b", [P, 512], F32))
        counted = sem("counted")
        placed = sem("placed")
        scattered = sem("scattered")
        own_step = sem("own_step_s")
        block = ctx.enter_context(nc.Block())

        @block.tensor
        def _(pe):
            o = onehot[:, :, :].rearrange("p t e -> p (t e)")
            pe.matmul(ps_c[:, 0:TILES * E], ones[:, :], o, start=True, stop=True)
            pe.matmul(ps_b[:, 0:TILES * E], before[:, :], o, start=True, stop=True).then_inc(counted, 1)

        @block.vector
        def _(dve):
            own = Tally(dve, own_step)

            def do(ins):
                own.wait(own.done(ins))

            dve.wait_ge(counted, 1)
            do(dve.tensor_copy(count[:, :, :].rearrange("p t e -> p (t e)"), ps_c[:, 0:TILES * E]))
            do(dve.tensor_copy(run[:, 0, :, :], count[:, :, :]))
            k, a = 1, 0
            while k < TILES:
                do(dve.tensor_copy(run[:, 1 - a, 0:k, :], run[:, a, 0:k, :]))
                do(dve.tensor_tensor(run[:, 1 - a, k:TILES, :], run[:, a, k:TILES, :], run[:, a, 0:TILES - k, :], ALU.add))
                k, a = 2 * k, 1 - a
            do(dve.tensor_scalar(total[:, :], run[:, a, TILES - 1, :], P - 1.0, None, ALU.add))
            do(dve.tensor_copy(whole[:, :], total[:, :]))
            shift = P.bit_length() - 1
            do(dve.tensor_scalar(whole[:, :], whole[:, :], shift, None, ALU.logical_shift_right))
            do(dve.tensor_scalar(size[:, :], whole[:, :], float(P), None, ALU.mult))
            do(dve.tensor_copy(ends[:, 0, :], size[:, :]))
            k, b = 1, 0
            while k < E:
                do(dve.tensor_copy(ends[:, 1 - b, 0:k], ends[:, b, 0:k]))
                do(dve.tensor_tensor(ends[:, 1 - b, k:E], ends[:, b, k:E], ends[:, b, 0:E - k], ALU.add))
                k, b = 2 * k, 1 - b
            do(dve.tensor_tensor(first[:, :], ends[:, b, :], size[:, :], ALU.subtract))
            do(dve.tensor_tensor(at[:, :, :], run[:, a, :, :], count[:, :, :], ALU.subtract))
            do(dve.tensor_tensor(at[:, :, :], at[:, :, :], first[:, :].unsqueeze(1).to_broadcast([P, TILES, E]), ALU.add))
            do(dve.tensor_tensor(at[:, :, :], at[:, :, :],
                                 ps_b[:, 0:TILES * E].rearrange("p (t e) -> p t e", t=TILES), ALU.add))
            do(dve.tensor_tensor(at[:, :, :], at[:, :, :], onehot[:, :, :], ALU.mult))
            do(dve.tensor_reduce(placef[:, :], at[:, :, :], AX.X, ALU.add))
            dve.tensor_copy(place[:, :], placef[:, :]).then_inc(placed, 1)
            do(dve.tensor_tensor(passed[:, :, :], starts[:, :].unsqueeze(2).to_broadcast([P, SLOTS, E]),
                                 ends[:, b, :].unsqueeze(1).to_broadcast([P, SLOTS, E]), ALU.is_ge))
            do(dve.tensor_reduce(expertf[:, :], passed[:, :, :], AX.X, ALU.add))
            do(dve.tensor_scalar(expertf[:, :], expertf[:, :], E - 1.0, None, ALU.min))
            do(dve.tensor_copy(expert_of[:, :], expertf[:, :]))

        @block.gpsimd
        def _(pool):
            pool.wait_ge(placed, 1)
            for t in range(TILES):
                pool.indirect_dma_start(xs_dram[:, :], bass.IndirectOffsetOnAxis(place[:, t:t + 1], 0),
                                        inter[:, t, :], None).then_inc(scattered, 16)
            pool.wait_ge(scattered, 16 * TILES)

    def run_experts(ctx):
        def sb(name, shape, dt=F32):
            return ctx.enter_context(nc.sbuf_tensor(name, shape, dt))

        def sem(name):
            return ctx.enter_context(nc.semaphore(name))

        xg = sb("xg", [P, 2, D])
        xT = sb("xT_d", [P, 2, P])
        hb = sb("hb", [P, 2, F])
        hs = sb("hs", [P, 2, F])
        hT = sb("hT", [P, 2, F])
        yo = sb("yo", [P, 2, D])
        ps_x, ps_h, ps_t, ps_y = ([ctx.enter_context(nc.psum_tensor(f"ps_e{n}{k}", [P, 512], F32)) for k in range(2)]
                                  for n in "xhty")
        x_in = [sem(f"x_in{k}") for k in range(2)]
        y_out = [sem(f"y_out{k}") for k in range(2)]
        x_turned = sem("x_turned")
        xT_done = sem("xT_done_d")
        h_ready = sem("h_ready")
        hb_done = sem("hb_done")
        hs_done = sem("hs_done")
        h_turned = sem("h_turned")
        hT_done = sem("hT_done")
        y_ready = sem("y_ready")
        yo_done = sem("yo_done")
        block = ctx.enter_context(nc.Block())
        PAIRS_OF = SLOTS // 2
        assert SLOTS % 2 == 1

        def pairs(eng, tile):
            def two(i):
                tile(i * 2, 0, i)
                tile(i * 2 + 1, 1, i)
            two(0)
            two(1)
            with eng.Fori(2, PAIRS_OF) as i:
                two(i)
            tile(SLOTS - 1, 0, PAIRS_OF)

        @block.sync
        def _(sp):
            def load(j, par):
                sp.dma_start(xg[:, par, :], xs_dram[bass.ds(j * P, P), :]).then_inc(x_in[par], 16)

            def tile(j, par, i):
                if not (isinstance(j, int) and j == SLOTS - 1):
                    sp.wait_ge(x_turned, j + 1)
                    load(j + 2 if par == 0 else (j + 2) % SLOTS, par)

            load(0, 0)
            load(1, 1)
            pairs(sp, tile)
            for par in range(2):
                sp.wait_ge(x_in[par], 16 * (PAIRS_OF + 1))

        @block.tensor
        def _(pe):
            def turn_x(j, par, i):
                pe.wait_ge(x_in[par], 16 * (i + 1))
                pe.wait_ge(xT_done, j - 1) if not isinstance(j, int) or j > 1 else None
                pe.transpose(ps_x[par][:, 0:P], xg[:, par, :], ident[:, :]).then_inc(x_turned, 1)

            def inner(j, par):
                e = pe.value_load(expert_of[0:1, bass.ds(j, 1)], min_val=0, max_val=E - 1)
                pe.wait_ge(xT_done, j + 1)
                if not isinstance(j, int) or j > 1:
                    pe.wait_ge(hb_done, j - 1)
                pe.matmul(ps_h[par][:, :], xT[:, par, :], w1[:, bass.ds(e, 1), :].rearrange("p a f -> p (a f)"),
                          start=True, stop=True).then_inc(h_ready, 1)

            def turn_h(j, par):
                pe.wait_ge(hs_done, j + 1)
                if not isinstance(j, int) or j > 1:
                    pe.wait_ge(hT_done, j - 1)
                for c in range(FC):
                    mm = pe.transpose(ps_t[par][:, c * P:(c + 1) * P], hs[:, par, c * P:(c + 1) * P], ident[:, :])
                mm.then_inc(h_turned, 1)

            def outer(j, par):
                e = pe.value_load(expert_of[0:1, bass.ds(j, 1)], min_val=0, max_val=E - 1)
                pe.wait_ge(hT_done, j + 1)
                if not isinstance(j, int) or j > 1:
                    pe.wait_ge(yo_done, j - 1)
                for c in range(FC):
                    mm = pe.matmul(ps_y[par][:, 0:D], hT[:, par, c * P:(c + 1) * P],
                                   w2[:, bass.ds(e, 1), c, :].rearrange("p a d -> p (a d)"),
                                   start=(c == 0), stop=(c == FC - 1))
                mm.then_inc(y_ready, 1)

            def tile(j, par, i):
                first = isinstance(j, int) and j == 0
                last = isinstance(j, int) and j == SLOTS - 1
                inner(j, par)
                if not last:
                    turn_x(j + 1, 1 - par, i + par)
                if not isinstance(j, int) or j > 1:
                    outer(j - 2, par)
                if not first:
                    turn_h(j - 1, 1 - par)

            turn_x(0, 0, 0)
            pairs(pe, tile)
            outer(SLOTS - 2, 1)
            turn_h(SLOTS - 1, 0)
            outer(SLOTS - 1, 0)

        @block.scalar
        def _(act):
            def copy_x(j, par):
                act.wait_ge(x_turned, j + 1)
                if not isinstance(j, int) or j > 1:
                    act.wait_ge(h_ready, j - 1)
                act.activation(xT[:, par, :], ps_x[par][:, 0:P], ACT.Copy).then_inc(xT_done, 1)

            def copy_h(j, par):
                act.wait_ge(h_turned, j + 1)
                if not isinstance(j, int) or j > 1:
                    act.wait_ge(y_ready, j - 1)
                act.activation(hT[:, par, :], ps_t[par][:, :], ACT.Copy).then_inc(hT_done, 1)

            def store(j, par):
                act.wait_ge(yo_done, j + 1)
                act.dma_start(ys_dram[bass.ds(j * P, P), :], yo[:, par, :]).then_inc(y_out[par], 16)

            def tile(j, par, i):
                first = isinstance(j, int) and j == 0
                last = isinstance(j, int) and j == SLOTS - 1
                if not isinstance(j, int) or j > 2:
                    store(j - 3, 1 - par)
                if not last:
                    copy_x(j + 1, 1 - par)
                act.wait_ge(hb_done, j + 1)
                if not isinstance(j, int) or j > 1:
                    act.wait_ge(h_turned, j - 1)
                act.activation(hs[:, par, :], hb[:, par, :], ACT.Silu).then_inc(hs_done, 1)
                if not first:
                    copy_h(j - 1, 1 - par)

            copy_x(0, 0)
            pairs(act, tile)
            copy_h(SLOTS - 1, 0)
            for back in (3, 2, 1):
                store(SLOTS - back, (SLOTS - back) % 2)
            act.wait_ge(y_out[0], 16 * (PAIRS_OF + 1))
            act.wait_ge(y_out[1], 16 * PAIRS_OF)

        @block.vector
        def _(dve):
            def add_b2(j, par, turns):
                e = dve.value_load(expert_of[0:1, bass.ds(j, 1)], min_val=0, max_val=E - 1)
                dve.wait_ge(y_ready, j + 1)
                if not isinstance(j, int) or j > 1:
                    dve.wait_ge(y_out[par], 16 * turns)
                dve.tensor_tensor(yo[:, par, :], ps_y[par][:, 0:D], b2[:, bass.ds(e, 1), :].rearrange("p a d -> p (a d)"),
                                  ALU.add).then_inc(yo_done, 1)

            def tile(j, par, i):
                e = dve.value_load(expert_of[0:1, bass.ds(j, 1)], min_val=0, max_val=E - 1)
                dve.wait_ge(h_ready, j + 1)
                if not isinstance(j, int) or j > 1:
                    dve.wait_ge(hs_done, j - 1)
                dve.tensor_tensor(hb[:, par, :], ps_h[par][:, :], b1[:, bass.ds(e, 1), :].rearrange("p a f -> p (a f)"),
                                  ALU.add).then_inc(hb_done, 1)
                if not isinstance(j, int) or j > 1:
                    add_b2(j - 2, par, i - 1)

            pairs(dve, tile)
            add_b2(SLOTS - 2, 1, PAIRS_OF - 1)
            add_b2(SLOTS - 1, 0, PAIRS_OF)

    def last_norm(ctx):
        def sb(name, shape, dt=F32):
            return ctx.enter_context(nc.sbuf_tensor(name, shape, dt))

        def sem(name):
            return ctx.enter_context(nc.semaphore(name))

        acc = sb("acc", [P, RT, D])
        ys = sb("ys", [P, RT, D])
        st, mv, sv = sb("stl", [P, RT, 6]), sb("mvl", [P, RT, 2]), sb("svl", [P, 3, RT])
        gathered = [sem(f"gathered{k}") for k in range(RGROUPS)]
        out_done = sem("out_done")
        stored = sem("stored_d")
        own_step = sem("own_step_l")
        STEPS = 16
        block = ctx.enter_context(nc.Block())

        @block.gpsimd
        def _(pool):
            for t in range(TILES):
                pool.indirect_dma_start(inter[:, t, :], None, ys_dram[:, :],
                                        bass.IndirectOffsetOnAxis(place[:, t:t + 1], 0)
                                        ).then_inc(gathered[t // RT], 16)

        @block.sync
        def _(sp):
            with sp.Fori(0, RGROUPS) as g:
                sp.wait_ge(out_done, g + 1)
                sp.dma_start(out.rearrange("(t p) d -> p t d", p=P)[:, bass.ds(g * RT, RT), :], ys[:, :, :]
                             ).then_inc(stored, 16)
            sp.wait_ge(stored, 16 * RGROUPS)

        @block.vector
        def _(dve):
            def group(g):
                own = Tally(dve, own_step, g * STEPS)
                if not is_first(g):
                    dve.wait_ge(out_done, g)
                own.wait(own.done(dve.tensor_tensor(acc[:, :, :], inter[:, bass.ds(g * RT, RT), :],
                                                    score[:, bass.ds(g * RT, RT)].unsqueeze(2).to_broadcast([P, RT, D]),
                                                    ALU.mult)))
                own.wait(own.done(dve.tensor_tensor(acc[:, :, :], acc[:, :, :], x2[:, bass.ds(g * RT, RT), :], ALU.add)))
                if not is_first(g):
                    dve.wait_ge(stored, 16 * g)
                layernorm(own, acc, lambda k: ys[:, k, :], st, mv, sv[:, 0, :], sv[:, 1, :], sv[:, 2, :],
                          RT).then_inc(out_done, 1)
                assert own.n == STEPS, own.n

            for g in range(RGROUPS):
                dve.wait_ge(gathered[g], 16 * RT)
                group(g)

    for part in (route, sort_tokens, run_experts, last_norm):
        with ExitStack() as step:
            part(step)


def build(nc, io, out):
    with ExitStack() as ctx:
        inter = ctx.enter_context(nc.sbuf_tensor("inter", [P, TILES, D], F32))
        parts_dram = nc.dram_tensor("parts_dram", [2, PARTS, P, B * N], BF16, kind="Internal").ap()
        with ExitStack() as phase:
            layer0_attention(nc, phase, io, inter)
        x2 = ctx.enter_context(nc.sbuf_tensor("x2", [P, TILES, D], F32))
        v1 = ctx.enter_context(nc.sbuf_tensor("v1", [P, TILES, H1, D1 + 1], F32))
        with ExitStack() as phase:
            between_attentions(nc, phase, io, inter, x2, v1, parts_dram)
        with ExitStack() as phase:
            layer1_attention(nc, phase, io, v1, parts_dram, inter)
        with ExitStack() as phase:
            output_and_experts(nc, phase, io, x2, inter, out)


def _tables():
    f = np.float32

    def angles(width):
        inv = (f(1) / f(10000) ** (np.arange(0, width, 2, dtype=f) / f(width))).astype(f)
        return (np.arange(N, dtype=f)[:, None] * inv[None]).astype(f)

    t = {}
    a = np.concatenate([angles(DH)] * 2, 1)
    cos, sin = np.cos(a), np.sin(a) * np.repeat(f([-1, 1]), DH // 2)
    t["csT"] = np.concatenate([cos.T, sin.T], 0) * f(DH ** -0.5)
    t["cosn"] = cos.reshape(WIN, P, DH).transpose(1, 0, 2)
    t["sinn"] = sin.reshape(WIN, P, DH).transpose(1, 0, 2)
    masks = np.zeros((P, WIN, 2, KEYS), f)
    q = np.arange(P)[:, None]
    for w in range(WIN):
        own = np.where(np.arange(P)[None] > q, -1e30, 0)
        before = np.full((P, P), -1e30 if w == 0 else 0)
        slots = [before, own]
        segs = np.where(w * P + q > SEG * np.arange(NSEG)[None] + SEG - 1, 0, -1e30)
        masks[:, w, 0] = np.concatenate(slots + [segs], 1)
        masks[:, w, 1] = np.concatenate([segs] + slots, 1)
    t["masks"] = masks.astype(mybir.dt.np(BF16))
    t["ident"] = np.eye(P, dtype=f)
    t["identb"] = np.eye(P).astype(mybir.dt.np(BF16))
    t["segsel"] = (np.arange(P)[:, None] // SEG == np.arange(SPW)[None]).astype(f)
    t["headsel"] = ((np.arange(P)[:, None] // SPW) % 4 == np.arange(4)[None]).astype(f)
    a = np.repeat(angles(D1), 2, -1)
    cos = np.tile(np.cos(a).T, (H1, 1))
    sin = np.tile((np.sin(a) * np.tile(f([-1, 1]), D1 // 2)).T, (H1, 1))
    t["cos1"] = cos
    t["sin1"] = sin
    t["before"] = np.triu(np.ones((P, P), f), 1)
    t["starts"] = np.tile(np.arange(TILES + E - 1, dtype=f) * P, (P, 1))
    t["rank"] = np.tile((E - np.arange(E)).astype(f), (P, 1))
    return t


def kernel(**inputs):
    import concourse.bacc as _bacc
    from concourse.bass_utils import run_bass_kernel_spmd as _run

    v = {k: np.asarray(a) for k, a in inputs.items()}

    def swapped(a):
        return a.reshape(*a.shape[:-1], D // 2, 2)[..., ::-1].reshape(a.shape)

    arrays = _tables()
    x = v["L0_attn_x"].reshape(TILES, P, D)
    wq0 = v["L0_attn_Wq"].reshape(D, H0, DH)
    h = DH // 2
    wq, bq, wk, bk = (v["L1_attn_" + n] for n in ("Wq", "bq", "Wk", "bk"))
    arrays.update(
        x=x.reshape(TILES * P, D), xT=x.transpose(0, 2, 1),
        wqs=np.concatenate([wq0, wq0[:, :, h:], wq0[:, :, :h]], 2),
        wkv=v["L0_attn_Wkv"], wout=v["L0_attn_Wout"], wproj=v["L0_attn_Wproj"],
        lg=v["L0_attn_ln_local_g"][None], lb=v["L0_attn_ln_local_b"][None],
        gg=v["L0_attn_ln_global_g"][None], gb=v["L0_attn_ln_global_b"][None],
        bout=v["L0_attn_bout"][None], w=v["L0_ffn_weight"],
        wqk=np.stack([wq, swapped(wq), wk, swapped(wk)], 1), bqk=np.stack([bq, swapped(bq), bk, swapped(bk)], 1),
        wv=v["L1_attn_Wv"], bv=v["L1_attn_bv"][None], wo=v["L1_attn_Wo"], bo=v["L1_attn_bo"][None],
        rms=v["L1_ffn_rms_w"][None], gate=v["L1_ffn_gate_w"].T,
        w1=v["L1_ffn_W1"].transpose(1, 0, 2), b1=v["L1_ffn_b1"].reshape(1, E * F),
        w2=v["L1_ffn_W2"].reshape(E, F // P, P, D).transpose(2, 0, 1, 3), b2=v["L1_ffn_b2"].reshape(1, E * D))
    arrays = {f"in_{k}": np.ascontiguousarray(a) for k, a in arrays.items()}

    nc = _bacc.Bacc("TRN2", target_bir_lowering=False, num_devices=1)
    io = {k[3:]: nc.dram_tensor(k, a.shape, mybir.dt.from_np(a.dtype), kind="ExternalInput").ap()
          for k, a in arrays.items()}
    out = nc.dram_tensor("out", (TILES * P, D), F32, kind="ExternalOutput").ap()
    build(nc, io, out)
    r = _run(nc, [arrays], core_ids=[0])
    return r.results[0]["out"].reshape(B, N, D)
```
